# Optimizing a Trainium2 kernel written in Bass

```python
import numpy as np
import jax
import jax.numpy as jnp

def _softmax(x, axis=-1):
    return jax.nn.softmax(x, axis=axis)

def _gelu(x):
    return jax.nn.gelu(x, approximate=True)

def _silu(x):
    return jax.nn.silu(x)

def _sigmoid(x):
    return jax.nn.sigmoid(x)

def _layernorm(x, axis=-1, eps=1e-05):
    m = jnp.mean(x, axis=axis, keepdims=True)
    v = jnp.var(x, axis=axis, keepdims=True)
    return (x - m) / jnp.sqrt(v + eps)

def _scatter_add(tgt, idx, src, axis=0):
    return tgt.at[idx].add(src)

def _segment_sum(src, seg, n):
    return jax.ops.segment_sum(src, seg, n)
kernel_name = 'mk_cond_seq_d4_seqx_r8_ccd29a'

def setup_inputs(seed: int=0):
    np.random.seed(seed)
    _w = jnp.asarray

    def _rec_inputs():
        import jax
        import jax.numpy as jnp
        _rk = jax.random.key(seed)
        x = -0.0003482 + 1 * jax.random.normal(jax.random.fold_in(_rk, 1), (8, 128, 144), jnp.float32)
        _lenS = 128 - jax.random.randint(jax.random.fold_in(_rk, 7), (8,), 0, max(1, 128 // 4) + 1, jnp.int32)
        _lenS2 = 128 - jax.random.randint(jax.random.fold_in(_rk, 8), (8,), 0, max(1, 128 // 4) + 1, jnp.int32)
        cond_1152 = 0.00257642 + 1.0011 * jax.random.normal(jax.random.fold_in(_rk, 11), (8, 144), jnp.float32)
        return (x, cond_1152)
    x, cond_1152 = _rec_inputs()

    def _L0_cond_setup():
        import jax, jax.numpy as jnp
        import numpy as np
        from jax.scipy.linalg import expm
        N, D, COND_DIM = (144, 64, 144)
        B, T = (16, 128)

        def _rotation(cond, W, b):
            v = jax.nn.silu(cond) @ W.T + b
            iu, ju = jnp.triu_indices(D, k=1)
            A = jnp.zeros((cond.shape[0], D, D), dtype=v.dtype)
            A = A.at[:, iu, ju].set(v).at[:, ju, iu].set(-v)
            return expm(A)
        key = jax.random.key(seed)
        k1, k2, k3, k4, k5 = jax.random.split(key, 5)
        x = jax.random.normal(k1, (B, T, N), dtype=jnp.float32)
        cond = jax.random.normal(k2, (B, COND_DIM), dtype=jnp.float32)
        P = jax.random.normal(k3, (N, D), dtype=jnp.float32)
        n_skew = D * (D - 1) // 2
        bound = 1.0 / np.sqrt(COND_DIM)
        W = jax.random.uniform(k4, (n_skew, COND_DIM), minval=-bound, maxval=bound, dtype=jnp.float32)
        b = jax.random.uniform(k5, (n_skew,), minval=-bound, maxval=bound, dtype=jnp.float32)
        return {'x': x, 'cond': cond, 'P': P, 'W': W, 'b': b}
    _L0_cond_all = _L0_cond_setup()
    _L0_cond_in = {k: v for k, v in _L0_cond_all.items() if k in ('P', 'W', 'b')}
    del _L0_cond_all

    def _L1_cond_setup():
        import jax, jax.numpy as jnp
        import numpy as np
        B, L, C = (8, 128, 144)
        H = 16
        D = C // H
        FF = int(C * 4.0)
        EPS = 1e-06

        def _layernorm(x):
            mu = jnp.mean(x, axis=-1, keepdims=True)
            var = jnp.mean(jnp.square(x - mu), axis=-1, keepdims=True)
            return (x - mu) * jax.lax.rsqrt(var + EPS)

        def _modulate(x, shift, scale):
            return x * (1.0 + scale) + shift

        def _attention(h, W_qkv, b_qkv, W_proj, b_proj):
            b, l, c = h.shape
            qkv = h @ W_qkv + b_qkv
            qkv = qkv.reshape(b, l, 3, H, D)
            q, k, v = (qkv[:, :, 0], qkv[:, :, 1], qkv[:, :, 2])
            scale = D ** (-0.5)
            scores = jnp.einsum('blhd,bmhd->bhlm', q * scale, k)
            attn = jax.nn.softmax(scores, axis=-1)
            o = jnp.einsum('bhlm,bmhd->blhd', attn, v).reshape(b, l, c)
            return o @ W_proj + b_proj
        key = jax.random.key(seed)
        ks = jax.random.split(key, 12)
        s = 0.02
        return {'x': jax.random.normal(ks[0], (B, L, C), jnp.float32), 'c': jax.random.normal(ks[1], (B, 1, C), jnp.float32), 'W_qkv': jax.random.normal(ks[2], (C, 3 * C), jnp.float32) * s, 'b_qkv': jnp.zeros((3 * C,), jnp.float32), 'W_proj': jax.random.normal(ks[3], (C, C), jnp.float32) * s, 'b_proj': jnp.zeros((C,), jnp.float32), 'W_fc1': jax.random.normal(ks[4], (C, FF), jnp.float32) * s, 'b_fc1': jnp.zeros((FF,), jnp.float32), 'W_fc2': jax.random.normal(ks[5], (FF, C), jnp.float32) * s, 'b_fc2': jnp.zeros((C,), jnp.float32), 'W_ada': jax.random.normal(ks[6], (C, 6 * C), jnp.float32) * s, 'b_ada': jnp.zeros((6 * C,), jnp.float32)}
    _L1_cond_all = _L1_cond_setup()
    _L1_cond_in = {k: v for k, v in _L1_cond_all.items() if k in ('W_qkv', 'b_qkv', 'W_proj', 'b_proj', 'W_fc1', 'b_fc1', 'W_fc2', 'b_fc2', 'W_ada', 'b_ada')}
    del _L1_cond_all

    def _L2_cond_setup():
        import jax, jax.numpy as jnp
        import numpy as np
        B, S, D = (8, 128, 144)
        H = 16
        HD = D // H
        HID = int(D * 4.0)
        LN_EPS = 1e-05

        def layer_norm(x, w, b):
            m = jnp.mean(x, axis=-1, keepdims=True)
            v = jnp.mean(jnp.square(x - m), axis=-1, keepdims=True)
            return (x - m) * jax.lax.rsqrt(v + LN_EPS) * w + b

        def modulate(x, shift, scale):
            return x * (1.0 + scale[:, None, :]) + shift[:, None, :]

        def attention(x, wq, wk, wv, wo, wo_b):
            b, s, d = x.shape
            q = (x @ wq).reshape(b, s, H, HD).transpose(0, 2, 1, 3)
            k = (x @ wk).reshape(b, s, H, HD).transpose(0, 2, 1, 3)
            v = (x @ wv).reshape(b, s, H, HD).transpose(0, 2, 1, 3)
            scale = 1.0 / np.sqrt(HD).astype(np.float32)
            att = jnp.einsum('bhqd,bhkd->bhqk', q, k) * scale
            att = jax.nn.softmax(att, axis=-1)
            out = jnp.einsum('bhqk,bhkd->bhqd', att, v)
            out = out.transpose(0, 2, 1, 3).reshape(b, s, d)
            return out @ wo + wo_b
        key = jax.random.key(seed)
        ks = jax.random.split(key, 16)
        s = 0.02
        return {'x': jax.random.normal(ks[0], (B, S, D), jnp.float32), 'c': jax.random.normal(ks[1], (B, D), jnp.float32), 'ln1_w': jnp.ones((D,), jnp.float32), 'ln1_b': jnp.zeros((D,), jnp.float32), 'wq': jax.random.normal(ks[2], (D, D), jnp.float32) * s, 'wk': jax.random.normal(ks[3], (D, D), jnp.float32) * s, 'wv': jax.random.normal(ks[4], (D, D), jnp.float32) * s, 'wo': jax.random.normal(ks[5], (D, D), jnp.float32) * s, 'wo_b': jnp.zeros((D,), jnp.float32), 'ln2_w': jnp.ones((D,), jnp.float32), 'ln2_b': jnp.zeros((D,), jnp.float32), 'fc1_w': jax.random.normal(ks[6], (D, HID), jnp.float32) * s, 'fc1_b': jnp.zeros((HID,), jnp.float32), 'fc2_w': jax.random.normal(ks[7], (HID, D), jnp.float32) * s, 'fc2_b': jnp.zeros((D,), jnp.float32), 'ada_w': jax.random.normal(ks[8], (D, 6 * D), jnp.float32) * s, 'ada_b': jnp.zeros((6 * D,), jnp.float32)}
    _L2_cond_all = _L2_cond_setup()
    _L2_cond_in = {k: v for k, v in _L2_cond_all.items() if k in ('ln1_w', 'ln1_b', 'wq', 'wk', 'wv', 'wo', 'wo_b', 'ln2_w', 'ln2_b', 'fc1_w', 'fc1_b', 'fc2_w', 'fc2_b', 'ada_w', 'ada_b')}
    del _L2_cond_all

    def _L3_cond_setup():
        import jax, jax.numpy as jnp
        import numpy as np
        DIM = 144
        HEADS = 16
        HEAD_DIM = DIM // HEADS
        HIDDEN = int(DIM * 4.0)
        EPS = 1e-12

        def rmsnorm(x, g, d):
            n = jnp.linalg.norm(x, axis=-1, keepdims=True)
            return x / jnp.maximum(n, EPS) * d ** 0.5 * g

        def modulate(x, scale, shift):
            return x * (1.0 + scale[:, None, :]) + shift[:, None, :]
        key = jax.random.key(seed)
        ks = jax.random.split(key, 12)
        B, N = (8, 128)
        s = 0.02
        return {'x': jax.random.normal(ks[0], (B, N, DIM), jnp.float32), 'c': jax.random.normal(ks[1], (B, DIM), jnp.float32), 'g1': jnp.ones((1,), jnp.float32), 'g2': jnp.ones((1,), jnp.float32), 'qkv_w': jax.random.normal(ks[2], (3 * DIM, DIM), jnp.float32) * s, 'qkv_b': jnp.zeros((3 * DIM,), jnp.float32), 'qg': jnp.ones((1,), jnp.float32), 'kg': jnp.ones((1,), jnp.float32), 'proj_w': jax.random.normal(ks[3], (DIM, DIM), jnp.float32) * s, 'proj_b': jnp.zeros((DIM,), jnp.float32), 'fc1_w': jax.random.normal(ks[4], (HIDDEN, DIM), jnp.float32) * s, 'fc1_b': jnp.zeros((HIDDEN,), jnp.float32), 'fc2_w': jax.random.normal(ks[5], (DIM, HIDDEN), jnp.float32) * s, 'fc2_b': jnp.zeros((DIM,), jnp.float32), 'ada_w': jax.random.normal(ks[6], (6 * DIM, DIM), jnp.float32) * s, 'ada_b': jnp.zeros((6 * DIM,), jnp.float32)}
    _L3_cond_all = _L3_cond_setup()
    _L3_cond_in = {k: v for k, v in _L3_cond_all.items() if k in ('g1', 'g2', 'qkv_w', 'qkv_b', 'qg', 'kg', 'proj_w', 'proj_b', 'fc1_w', 'fc1_b', 'fc2_w', 'fc2_b', 'ada_w', 'ada_b')}
    del _L3_cond_all
    return {'x': x, 'cond_1152': cond_1152, 'L0_cond_P': _L0_cond_in['P'], 'L0_cond_W': _L0_cond_in['W'], 'L0_cond_b': _L0_cond_in['b'], 'L1_cond_W_qkv': _L1_cond_in['W_qkv'], 'L1_cond_b_qkv': _L1_cond_in['b_qkv'], 'L1_cond_W_proj': _L1_cond_in['W_proj'], 'L1_cond_b_proj': _L1_cond_in['b_proj'], 'L1_cond_W_fc1': _L1_cond_in['W_fc1'], 'L1_cond_b_fc1': _L1_cond_in['b_fc1'], 'L1_cond_W_fc2': _L1_cond_in['W_fc2'], 'L1_cond_b_fc2': _L1_cond_in['b_fc2'], 'L1_cond_W_ada': _L1_cond_in['W_ada'], 'L1_cond_b_ada': _L1_cond_in['b_ada'], 'L2_cond_ln1_w': _L2_cond_in['ln1_w'], 'L2_cond_ln1_b': _L2_cond_in['ln1_b'], 'L2_cond_wq': _L2_cond_in['wq'], 'L2_cond_wk': _L2_cond_in['wk'], 'L2_cond_wv': _L2_cond_in['wv'], 'L2_cond_wo': _L2_cond_in['wo'], 'L2_cond_wo_b': _L2_cond_in['wo_b'], 'L2_cond_ln2_w': _L2_cond_in['ln2_w'], 'L2_cond_ln2_b': _L2_cond_in['ln2_b'], 'L2_cond_fc1_w': _L2_cond_in['fc1_w'], 'L2_cond_fc1_b': _L2_cond_in['fc1_b'], 'L2_cond_fc2_w': _L2_cond_in['fc2_w'], 'L2_cond_fc2_b': _L2_cond_in['fc2_b'], 'L2_cond_ada_w': _L2_cond_in['ada_w'], 'L2_cond_ada_b': _L2_cond_in['ada_b'], 'L3_cond_g1': _L3_cond_in['g1'], 'L3_cond_g2': _L3_cond_in['g2'], 'L3_cond_qkv_w': _L3_cond_in['qkv_w'], 'L3_cond_qkv_b': _L3_cond_in['qkv_b'], 'L3_cond_qg': _L3_cond_in['qg'], 'L3_cond_kg': _L3_cond_in['kg'], 'L3_cond_proj_w': _L3_cond_in['proj_w'], 'L3_cond_proj_b': _L3_cond_in['proj_b'], 'L3_cond_fc1_w': _L3_cond_in['fc1_w'], 'L3_cond_fc1_b': _L3_cond_in['fc1_b'], 'L3_cond_fc2_w': _L3_cond_in['fc2_w'], 'L3_cond_fc2_b': _L3_cond_in['fc2_b'], 'L3_cond_ada_w': _L3_cond_in['ada_w'], 'L3_cond_ada_b': _L3_cond_in['ada_b']}

def reference(x, cond_1152, L0_cond_P, L0_cond_W, L0_cond_b, L1_cond_W_qkv, L1_cond_b_qkv, L1_cond_W_proj, L1_cond_b_proj, L1_cond_W_fc1, L1_cond_b_fc1, L1_cond_W_fc2, L1_cond_b_fc2, L1_cond_W_ada, L1_cond_b_ada, L2_cond_ln1_w, L2_cond_ln1_b, L2_cond_wq, L2_cond_wk, L2_cond_wv, L2_cond_wo, L2_cond_wo_b, L2_cond_ln2_w, L2_cond_ln2_b, L2_cond_fc1_w, L2_cond_fc1_b, L2_cond_fc2_w, L2_cond_fc2_b, L2_cond_ada_w, L2_cond_ada_b, L3_cond_g1, L3_cond_g2, L3_cond_qkv_w, L3_cond_qkv_b, L3_cond_qg, L3_cond_kg, L3_cond_proj_w, L3_cond_proj_b, L3_cond_fc1_w, L3_cond_fc1_b, L3_cond_fc2_w, L3_cond_fc2_b, L3_cond_ada_w, L3_cond_ada_b):
    import jax
    import jax.numpy as jnp

    def _L0_cond_ref(x, cond, P, W, b):
        import jax, jax.numpy as jnp
        import numpy as np
        from jax.scipy.linalg import expm
        N, D, COND_DIM = (144, 64, 144)
        B, T = (16, 128)

        def _rotation(cond, W, b):
            v = jax.nn.silu(cond) @ W.T + b
            iu, ju = jnp.triu_indices(D, k=1)
            A = jnp.zeros((cond.shape[0], D, D), dtype=v.dtype)
            A = A.at[:, iu, ju].set(v).at[:, ju, iu].set(-v)
            return expm(A)
        U, _ = jnp.linalg.qr(P)
        R = _rotation(cond, W, b)
        z = jnp.einsum('btn,nd->btd', x, U)
        z_rot = jnp.einsum('btd,bde->bte', z, R)
        x_rot = x + jnp.einsum('btd,nd->btn', z_rot - z, U)
        return x_rot

    def _L1_cond_ref(x, c, W_qkv, b_qkv, W_proj, b_proj, W_fc1, b_fc1, W_fc2, b_fc2, W_ada, b_ada):
        import jax, jax.numpy as jnp
        import numpy as np
        B, L, C = (8, 128, 144)
        H = 16
        D = C // H
        FF = int(C * 4.0)
        EPS = 1e-06

        def _layernorm(x):
            mu = jnp.mean(x, axis=-1, keepdims=True)
            var = jnp.mean(jnp.square(x - mu), axis=-1, keepdims=True)
            return (x - mu) * jax.lax.rsqrt(var + EPS)

        def _modulate(x, shift, scale):
            return x * (1.0 + scale) + shift

        def _attention(h, W_qkv, b_qkv, W_proj, b_proj):
            b, l, c = h.shape
            qkv = h @ W_qkv + b_qkv
            qkv = qkv.reshape(b, l, 3, H, D)
            q, k, v = (qkv[:, :, 0], qkv[:, :, 1], qkv[:, :, 2])
            scale = D ** (-0.5)
            scores = jnp.einsum('blhd,bmhd->bhlm', q * scale, k)
            attn = jax.nn.softmax(scores, axis=-1)
            o = jnp.einsum('bhlm,bmhd->blhd', attn, v).reshape(b, l, c)
            return o @ W_proj + b_proj
        ada = jax.nn.silu(c) @ W_ada + b_ada
        shift_msa, scale_msa, gate_msa, shift_mlp, scale_mlp, gate_mlp = jnp.split(ada, 6, axis=-1)
        h = _modulate(_layernorm(x), shift_msa, scale_msa)
        x = x + gate_msa * _attention(h, W_qkv, b_qkv, W_proj, b_proj)
        h = _modulate(_layernorm(x), shift_mlp, scale_mlp)
        mlp = jax.nn.gelu(h @ W_fc1 + b_fc1, approximate=True) @ W_fc2 + b_fc2
        x = x + gate_mlp * mlp
        return x

    def _L2_cond_ref(x, c, ln1_w, ln1_b, wq, wk, wv, wo, wo_b, ln2_w, ln2_b, fc1_w, fc1_b, fc2_w, fc2_b, ada_w, ada_b):
        import jax, jax.numpy as jnp
        import numpy as np
        B, S, D = (8, 128, 144)
        H = 16
        HD = D // H
        HID = int(D * 4.0)
        LN_EPS = 1e-05

        def layer_norm(x, w, b):
            m = jnp.mean(x, axis=-1, keepdims=True)
            v = jnp.mean(jnp.square(x - m), axis=-1, keepdims=True)
            return (x - m) * jax.lax.rsqrt(v + LN_EPS) * w + b

        def modulate(x, shift, scale):
            return x * (1.0 + scale[:, None, :]) + shift[:, None, :]

        def attention(x, wq, wk, wv, wo, wo_b):
            b, s, d = x.shape
            q = (x @ wq).reshape(b, s, H, HD).transpose(0, 2, 1, 3)
            k = (x @ wk).reshape(b, s, H, HD).transpose(0, 2, 1, 3)
            v = (x @ wv).reshape(b, s, H, HD).transpose(0, 2, 1, 3)
            scale = 1.0 / np.sqrt(HD).astype(np.float32)
            att = jnp.einsum('bhqd,bhkd->bhqk', q, k) * scale
            att = jax.nn.softmax(att, axis=-1)
            out = jnp.einsum('bhqk,bhkd->bhqd', att, v)
            out = out.transpose(0, 2, 1, 3).reshape(b, s, d)
            return out @ wo + wo_b
        mod = jax.nn.silu(c) @ ada_w + ada_b
        sh_msa, sc_msa, g_msa, sh_mlp, sc_mlp, g_mlp = jnp.split(mod, 6, axis=1)
        h = modulate(layer_norm(x, ln1_w, ln1_b), sh_msa, sc_msa)
        x = x + g_msa[:, None, :] * attention(h, wq, wk, wv, wo, wo_b)
        h = modulate(layer_norm(x, ln2_w, ln2_b), sh_mlp, sc_mlp)
        h = jax.nn.gelu(h @ fc1_w + fc1_b, approximate=False) @ fc2_w + fc2_b
        x = x + g_mlp[:, None, :] * h
        return x

    def _L3_cond_ref(x, c, g1, g2, qkv_w, qkv_b, qg, kg, proj_w, proj_b, fc1_w, fc1_b, fc2_w, fc2_b, ada_w, ada_b):
        import jax, jax.numpy as jnp
        import numpy as np
        DIM = 144
        HEADS = 16
        HEAD_DIM = DIM // HEADS
        HIDDEN = int(DIM * 4.0)
        EPS = 1e-12

        def rmsnorm(x, g, d):
            n = jnp.linalg.norm(x, axis=-1, keepdims=True)
            return x / jnp.maximum(n, EPS) * d ** 0.5 * g

        def modulate(x, scale, shift):
            return x * (1.0 + scale[:, None, :]) + shift[:, None, :]
        B, N, D = x.shape
        mod = jax.nn.silu(c) @ ada_w.T + ada_b
        shift_msa, scale_msa, gate_msa, shift_mlp, scale_mlp, gate_mlp = jnp.split(mod, 6, axis=-1)
        gate_msa = jnp.tanh(gate_msa)
        gate_mlp = jnp.tanh(gate_mlp)
        h = modulate(rmsnorm(x, g1, D), scale_msa, shift_msa)
        qkv = h @ qkv_w.T + qkv_b
        qkv = qkv.reshape(B, N, 3, HEADS, HEAD_DIM).transpose(2, 0, 3, 1, 4)
        q, k, v = (qkv[0], qkv[1], qkv[2])
        q = rmsnorm(q, qg, HEAD_DIM)
        k = rmsnorm(k, kg, HEAD_DIM)
        q = q * HEAD_DIM ** (-0.5)
        attn = jax.nn.softmax(jnp.einsum('bhqd,bhkd->bhqk', q, k), axis=-1)
        o = jnp.einsum('bhqk,bhkd->bhqd', attn, v)
        o = o.transpose(0, 2, 1, 3).reshape(B, N, D)
        o = o @ proj_w.T + proj_b
        x = x + gate_msa[:, None, :] * o
        h2 = modulate(rmsnorm(x, g2, D), scale_mlp, shift_mlp)
        m = jax.nn.gelu(h2 @ fc1_w.T + fc1_b, approximate=True) @ fc2_w.T + fc2_b
        x = x + gate_mlp[:, None, :] * m
        return x
    x = _L0_cond_ref(x, cond_1152, L0_cond_P, L0_cond_W, L0_cond_b)
    x = _L1_cond_ref(x, cond_1152[:, None, :], L1_cond_W_qkv, L1_cond_b_qkv, L1_cond_W_proj, L1_cond_b_proj, L1_cond_W_fc1, L1_cond_b_fc1, L1_cond_W_fc2, L1_cond_b_fc2, L1_cond_W_ada, L1_cond_b_ada)
    x = _L2_cond_ref(x, cond_1152, L2_cond_ln1_w, L2_cond_ln1_b, L2_cond_wq, L2_cond_wk, L2_cond_wv, L2_cond_wo, L2_cond_wo_b, L2_cond_ln2_w, L2_cond_ln2_b, L2_cond_fc1_w, L2_cond_fc1_b, L2_cond_fc2_w, L2_cond_fc2_b, L2_cond_ada_w, L2_cond_ada_b)
    x = _L3_cond_ref(x, cond_1152, L3_cond_g1, L3_cond_g2, L3_cond_qkv_w, L3_cond_qkv_b, L3_cond_qg, L3_cond_kg, L3_cond_proj_w, L3_cond_proj_b, L3_cond_fc1_w, L3_cond_fc1_b, L3_cond_fc2_w, L3_cond_fc2_b, L3_cond_ada_w, L3_cond_ada_b)
    return x

_drawn_inputs = setup_inputs


def setup_inputs(seed=0):
    import zlib

    import numpy as np

    out = dict(_drawn_inputs(seed))
    spreads = {'L1_cond_b_qkv': (0.0, 0.8),
     'L1_cond_b_proj': (0.0, 0.502),
     'L1_cond_b_fc1': (0.0, 0.8),
     'L1_cond_b_fc2': (0.0, 0.453),
     'L1_cond_b_ada': (0.0, 0.534),
     'L2_cond_ln1_w': (1.0, 0.6),
     'L2_cond_ln1_b': (0.0, 0.8),
     'L2_cond_wo_b': (0.0, 0.412),
     'L2_cond_ln2_w': (1.0, 0.6),
     'L2_cond_ln2_b': (0.0, 0.8),
     'L2_cond_fc1_b': (0.0, 0.8),
     'L2_cond_fc2_b': (0.0, 0.517),
     'L2_cond_ada_b': (0.0, 0.511),
     'L3_cond_qkv_b': (0.0, 0.8),
     'L3_cond_proj_b': (0.0, 0.443),
     'L3_cond_fc1_b': (0.0, 0.8),
     'L3_cond_fc2_b': (0.0, 0.516),
     'L3_cond_ada_b': (0.0, 0.563)}
    factors = {'L1_cond_W_qkv': 8.0,
     'L1_cond_W_proj': 8.0,
     'L1_cond_W_fc1': 5.336,
     'L1_cond_W_fc2': 4.958,
     'L1_cond_W_ada': 2.758,
     'L2_cond_wq': 8.0,
     'L2_cond_wk': 8.0,
     'L2_cond_wv': 8.0,
     'L2_cond_wo': 8.0,
     'L2_cond_fc1_w': 5.044,
     'L2_cond_fc2_w': 4.533,
     'L3_cond_qkv_w': 8.0,
     'L3_cond_proj_w': 8.0,
     'L3_cond_fc1_w': 5.451,
     'L3_cond_fc2_w': 5.104}
    for name, (base, spread) in spreads.items():
        noise = np.random.default_rng([zlib.crc32(name.encode()), seed]).standard_normal(out[name].shape)
        drawn = base * np.exp(spread * noise) if base else spread * noise
        out[name] = jnp.asarray(drawn.astype(out[name].dtype))
    for name, factor in factors.items():
        out[name] = (out[name] * factor).astype(out[name].dtype)
    return out
```

```python
from contextlib import ExitStack

import numpy as np

import concourse.bass as bass
from concourse import mybir

F32 = mybir.dt.float32
BF16 = mybir.dt.bfloat16
U32 = mybir.dt.uint32
I32 = mybir.dt.int32
ALU = mybir.AluOpType
ACT = mybir.ActivationFunctionType
AX_X = mybir.AxisListType.X

B, T, C = 8, 128, 144
D = 64
CT = C - 128
KT = CT + 1
H, HD = 16, 9
FF = 4 * C
FFC = 5
LAYERS = 3
SLOTS = 6
HROWS = SLOTS * HD
Q1, Q2, Q3 = slice(1, 6, 2), slice(0, 3, 2), slice(4, 5)
K1, K2, K3 = slice(2, 5), slice(0, 2), slice(5, 6)
SCALE = float(HD) ** -0.5
SQUARINGS = 6
STEPS = LAYERS * B // 2
LN_EPS = [1e-6, 1e-5, 0.0]
RSQRT_SEED = 1597463007.0
FACT = [1.0]
for _n in range(1, 16):
    FACT.append(FACT[-1] * _n)
COS = [(-1.0) ** k / FACT[2 * k] for k in range(7)]
SIN = [(-1.0) ** k / FACT[2 * k + 1] for k in range(7)]
EYES = sorted(set(COS) | set(SIN) | {-1.0})


def eye_of(c):
    return EYES.index(c)


def plan_rotation():
    chain = [("upper", 0), ("skew", 0), ("n2", 0), ("n4", 0)]
    chain += [("poly", (k, f)) for k in (2, 1, 0) for f in (0, 1)]
    chain += [("expm", 0), ("expm", 1)]
    chain += [("square", (k, f)) for k in range(1, SQUARINGS + 1) for f in (0, 1) if k < SQUARINGS or f == 0]
    other = [("gate", (l, b)) for l in range(LAYERS) for b in range(B)]
    other.insert(B, ("mods", 0))
    other.insert(B + 1, ("mods", 1))
    fills = chain[:2]
    for k in range(max(len(chain) - 2, len(other))):
        fills += chain[2 + k:3 + k] + other[k:k + 1]
    return fills


def head_of(g, i):
    return 8 * (g // 2) + 2 * i + g % 2


def program(nc, t, out):
    ctx = ExitStack()
    with ctx:
        def sb(name, shape, dt=F32):
            return ctx.enter_context(nc.sbuf_tensor(name, shape, dt))

        def sem(name):
            return ctx.enter_context(nc.semaphore(name))

        x = sb("x", [T, B, C])
        x_t, x_u = sb("x_t", [128, B * T]), sb("x_u", [CT, B * T])
        c_t, c_u = sb("c_t", [128, B]), sb("c_u", [KT, B])
        e_t, e_u = sb("e_t", [128, B]), sb("e_u", [KT, B])
        s_t, s_u = sb("s_t", [128, B]), sb("s_u", [KT, B])
        p_t, p_u, pT = sb("p_t", [128, D]), sb("p_u", [CT, D]), sb("pT", [D, C])
        skw_t, skw_r = sb("skw_t", [128, D * D]), sb("skw_r", [128, D * D])
        skw_u = skw_r[0:KT, :]
        qkvw_t = [sb(f"qkvw_t{l}", [128, 3 * C]) for l in range(LAYERS)]
        qkvw_u = [sb(f"qkvw_u{l}", [KT, 3 * C]) for l in range(LAYERS)]
        projw_t = [sb(f"projw_t{l}", [128, C]) for l in range(LAYERS)]
        projw_u = [sb(f"projw_u{l}", [KT, C]) for l in range(LAYERS)]
        fc1w_t = [sb(f"fc1w_t{l}", [128, FF]) for l in range(LAYERS)]
        fc1w_u = [sb(f"fc1w_u{l}", [KT, FF]) for l in range(LAYERS)]
        fc2w = [sb(f"fc2w{l}", [128, FFC, C]) for l in range(LAYERS)]
        adaw_t = [sb(f"adaw_t{l}", [128, 6 * C]) for l in range(LAYERS)]
        adaw_u = [sb(f"adaw_u{l}", [KT, 6 * C]) for l in range(LAYERS)]
        aff_t, aff_u = sb("aff_t", [128, 6]), sb("aff_u", [KT, 6])
        qkg = sb("qkg", [T, 2])

        ident = sb("ident", [128, 128])
        identb = sb("identb", [128, 128], BF16)
        eyes = sb("eyes", [D, len(EYES), D])
        irep = sb("irep", [D, B, D])
        below = sb("below", [32, 2, D])
        diag = sb("diag", [32, 2, D])
        half, nhalf = sb("half", [32, 1]), sb("nhalf", [T, 2])
        one_h = sb("one_h", [96, H])
        sel = sb("sel", [128, H, 128], BF16)

        elim = sb("elim", [32, 2, 2 * D])
        top = sb("top", [32, 2, D])
        grow = sb("grow", [32, 4, 2 * D])
        trow = sb("trow", [32, 2, D])
        grec, gfac = sb("grec", [32, D]), sb("gfac", [32, 2, 2])
        root = sb("root", [32, D])
        beta = sb("beta", [32, D])
        den, drec = sb("den", [32, D]), sb("drec", [32, D])
        tnum, tfac = sb("tnum", [32, 2, 2]), sb("tfac", [32, 2, 2])
        sgn = sb("sgn", [32, D])
        sgnd = sb("sgnd", [32, 2, D])
        rscale = sb("rscale", [32, 2])
        linv = sb("linv", [32, 2, D])
        linvT = sb("linvT", [D, D])
        u_t, u_u, uT = sb("u_t", [128, D]), sb("u_u", [CT, D]), sb("uT", [D, C])
        zT, yT = sb("zT", [D, B * T]), sb("yT", [D, B * T])
        upper = sb("upper", [D, B, D])
        bmat = sb("bmat", [D, B, D])
        n2, n4 = sb("n2", [D, B, D]), sb("n4", [D, B, D])
        poly = [[sb(f"poly{k}{f}", [D, B, D]) for f in range(2)] for k in range(3)]
        nodd = sb("nodd", [D, B, D])
        ex, fx = [poly[2][0], poly[1][0]], [poly[2][1], poly[1][1]]

        mod_t, mod_u = sb("mod_t", [128, LAYERS, 4, B]), sb("mod_u", [KT, LAYERS, 4, B])
        mod_w = sb("mod_w", [128, B])
        gate = sb("gate", [T, LAYERS, B, 2, C])

        st6 = sb("st6", [T, 2, 2, 6])
        st2 = sb("st2", [T, 2, 2, 2])
        vare, rstd = sb("vare", [T, 2, 2]), sb("rstd", [T, 2, 2])
        msq = sb("msq", [T, 2, 2])
        ln = [[sb(f"ln{k}{h}", [T, C + 1]) for h in range(2)] for k in range(2)]
        hT_t = [sb(f"hT_t{h}", [128, T]) for h in range(2)]
        hT_u = [sb(f"hT_u{h}", [KT, T]) for h in range(2)]
        mT_t, mT_u = sb("mT_t", [128, 2, T]), sb("mT_u", [KT, 2, T])
        qk = [sb(f"qk{h}", [T, 2, H, HD]) for h in range(2)]
        sq = sb("sq", [T, 2 * H, HD])
        ssq, hy, ny, my = sb("ssq", [T, 2, H]), sb("hy", [T, 2, H]), sb("ny", [T, 2, H]), sb("my", [T, 2, H])
        res = [sb(f"res{h}", [T, 2, H, HD]) for h in range(2)]
        parts = [[sb(f"parts{k}{h}", [T, H, 64], BF16) for h in range(2)] for k in range(2)]
        n_qkT, n_hid = H // 4 * T, FFC * 2 * T
        qkT = [[skw_r[:, (2 * k + h) * n_qkT:(2 * k + h + 1) * n_qkT].bitcast(BF16)
                .rearrange("p (n t) -> p n t", t=T) for h in range(2)] for k in range(2)]
        hid = skw_r[:, 4 * n_qkT:4 * n_qkT + n_hid].rearrange("p (c h t) -> p c h t", c=FFC, h=2)
        prob = [skw_t[:, g * 4 * T:(g + 1) * 4 * T].rearrange("p (i t) -> p i t", t=T) for g in range(4)]
        o_raw = [skw_t[:, (4 + h) * 4 * T:(5 + h) * 4 * T].rearrange("p (g t) -> p g t", t=T) for h in range(2)]
        v_aug = [sb(f"v_aug{h}", [T, H, 32]) for h in range(2)]
        nmax = sb("nmax", [T, 2, H])
        nmp = [sb(f"nmp{h}", [T, 96], BF16) for h in range(2)]
        nmT = [sb(f"nmT{h}", [96, T], BF16) for h in range(2)]
        orec = [sb(f"orec{h}", [T, H]) for h in range(2)]
        o_n = [sb(f"o_n{h}", [T, C + 1]) for h in range(2)]
        oT_t = [sb(f"oT_t{h}", [128, T]) for h in range(2)]
        oT_u = [sb(f"oT_u{h}", [KT, T]) for h in range(2)]
        n_far = 4 * n_qkT + n_hid
        attd = [skw_r[:, n_far + h * C:n_far + (h + 1) * C] for h in range(2)]
        mlpd = skw_r[:, n_far + 2 * C:n_far + 4 * C].rearrange("p (h c) -> p h c", h=2)

        ps = ctx.enter_context(nc.psum_tensor("ps", [128, 8, 512], F32))

        ld = {n: sem("ld_" + n) for n in ("cond", "p", "skw", "x", "misc", "ada0", "ada1", "ada2",
                                          "blk0", "blk1", "blk2")}
        loads = {"cond": 2, "p": 4, "skw": 2, "x": 3, "misc": 3, "ada0": 2, "ada1": 2, "ada2": 2,
                 "blk0": 8, "blk1": 8, "blk2": 8}
        pool_step = sem("pool_step")
        dve_step = sem("dve_step")
        early_consts = sem("early_consts")
        late_consts = sem("late_consts")
        sel_ready = sem("sel_ready")
        silu_e, silu_ready = sem("silu_e"), sem("silu_ready")
        gram_full, gram_read = sem("gram_full"), sem("gram_read")
        grow_ready = sem("grow_ready")
        root_ready = sem("root_ready")
        pre_full, pre_read = sem("pre_full"), sem("pre_read")
        rot_full, rot_read = sem("rot_full"), sem("rot_read")
        linv_ready = sem("linv_ready")
        gates_tanh, mods_ready = sem("gates_tanh"), sem("mods_ready")
        var1, rstd1 = sem("var1"), sem("rstd1")
        var2, rstd2 = sem("var2"), sem("rstd2")
        ln_ready, ln2_ready = sem("ln_ready"), sem("ln2_ready")
        hT_full, hT_ready = sem("hT_full"), sem("hT_ready")
        h2T_full, h2T_ready = sem("h2T_full"), sem("h2T_ready")
        qkv_full, qkv_read = sem("qkv_full"), sem("qkv_read")
        v_ready, qk_normed = sem("v_ready"), sem("qk_normed")
        first_parts, parts_ready = sem("first_parts"), sem("parts_ready")
        qT_full, qT_ready = sem("qT_full"), sem("qT_ready")
        kT_full, kT_ready = sem("kT_full"), sem("kT_ready")
        s_full, max_ready = sem("s_full"), sem("max_ready")
        nmp_ready, mT_full, nmT_ready = sem("nmp_ready"), sem("mT_full"), sem("nmT_ready")
        sT_full, prob_ready, prob_used = sem("sT_full"), sem("prob_ready"), sem("prob_used")
        o_raw_ready, back_full, o_n_ready = sem("o_raw_ready"), sem("back_full"), sem("o_n_ready")
        oT_full, oT_ready = sem("oT_full"), sem("oT_ready")
        proj_full, att_ready, att_added = sem("proj_full"), sem("att_ready"), sem("att_added")
        fc1_full, hid_ready = sem("fc1_full"), sem("hid_ready")
        fc2_full, mlp_ready, mlp_added = sem("fc2_full"), sem("mlp_ready"), sem("mlp_added")
        stored = sem("stored")

        pre = plan_rotation()
        pre_at = {fill: k for k, fill in enumerate(pre)}
        reads, pre_reads = 0, []
        for fill in pre:
            reads += 2 if fill == ("poly", (0, 1)) else 1
            pre_reads.append(reads)

        def was_read(name, arg):
            return pre_reads[pre_at[name, arg]]

        block = ctx.enter_context(nc.Block())

        @block.sync
        def _(sp):
            def load(dst, src, s):
                sp.dma_start(dst, src).then_inc(ld[s], 16)

            load(p_t[:], t["p"][0:128, :], "p")
            load(p_u[:], t["p"][128:C, :], "p")
            load(c_t[:], t["cond"][0:128, :], "cond")
            load(c_u[0:CT, :], t["cond"][128:C, :], "cond")
            load(top[:], t["ptop"], "p")
            load(pT[:], t["pT"], "p")
            load(skw_t[:], t["skw"][0:128, :], "skw")
            load(skw_u, t["skw"][128:C + 1, :], "skw")
            for l in range(LAYERS):
                load(adaw_t[l][:], t[f"ada{l}"][0:128, :], f"ada{l}")
                load(adaw_u[l][:], t[f"ada{l}"][128:C + 1, :], f"ada{l}")
            load(x[:], t["x"], "x")
            load(x_t[:], t["xT"][0:128, :], "x")
            load(x_u[:], t["xT"][128:C, :], "x")
            load(aff_t[:], t["aff"][0:128, :], "misc")
            load(aff_u[0:CT, :], t["aff"][128:C, :], "misc")
            load(qkg[:], t["qkg"], "misc")
            for l in range(LAYERS):
                load(qkvw_t[l][:], t[f"qkv{l}"][0:128, :], f"blk{l}")
                load(qkvw_u[l][:], t[f"qkv{l}"][128:C + 1, :], f"blk{l}")
                load(projw_t[l][:], t[f"proj{l}"][0:128, :], f"blk{l}")
                load(projw_u[l][:], t[f"proj{l}"][128:C + 1, :], f"blk{l}")
                load(fc1w_t[l][:], t[f"fc1{l}"][0:128, :], f"blk{l}")
                load(fc1w_u[l][:], t[f"fc1{l}"][128:C + 1, :], f"blk{l}")
                load(fc2w[l][:, 0:4, :], t[f"fc2{l}"][0:512, :].rearrange("(c p) n -> p c n", p=128), f"blk{l}")
                load(fc2w[l][0:65, 4, :], t[f"fc2{l}"][512:FF + 1, :], f"blk{l}")
            for pair in range(B // 2):
                sp.wait_ge(mlp_added, 2 * (STEPS - B // 2 + pair) + 2)
                sp.dma_start(out[:, 2 * pair:2 * pair + 2, :], x[:, 2 * pair:2 * pair + 2, :]).then_inc(stored, 16)
            sp.wait_ge(stored, 16 * (B // 2))

        def loaded(eng, s):
            eng.wait_ge(ld[s], 16 * loads[s])

        @block.gpsimd
        def _(pool):
            g = nc.gpsimd
            n = [0]

            def step(ins):
                n[0] += 1
                ins.then_inc(pool_step, 1)
                pool.wait_ge(pool_step, n[0])

            def filled(tile, fill, base=0, compare=ALU.not_equal):
                step(g.memset(tile, 0.0))
                return g.affine_select(out=tile, in_=tile, compare_op=compare, fill=fill, base=-base,
                                       pattern=[[1, tile.shape[1]]], channel_multiplier=-1)

            g.memset(s_u[:], 1.0).then_inc(early_consts, 1)
            g.memset(half[:], 0.5)
            g.memset(nhalf[:], -0.5)
            for q in range(2):
                step(filled(elim[:, q, D:2 * D], 1.0, 32 * q))
                step(filled(diag[:, q, :], -1.0, 32 * q))
                step(filled(below[:, q, :], -1.0, 32 * q, ALU.is_ge))
            filled(ident[:], 1.0).then_inc(early_consts, 1)
            pool.wait_ge(early_consts, 2)
            for k, c in enumerate(EYES):
                g.tensor_scalar(eyes[:, k, :], ident[0:D, 0:D], c, None, ALU.mult)
            for b in range(B):
                step(g.tensor_copy(irep[:, b, :], ident[0:D, 0:D]))
            g.tensor_copy(identb[:], ident[:]).then_inc(early_consts, 1)

            for j in range(D):
                pool.wait_ge(grow_ready, j + 1)
                g.tensor_tensor(root[:, j:j + 1], grow[:, j % 4, j:j + 1], half[:], ALU.pow).then_inc(root_ready, 1)

            pool.wait_ge(pre_read, was_read("mods", 1))
            loaded(pool, "misc")
            for m, a, rows in ((mod_t, aff_t, 128), (mod_u, aff_u, CT)):
                for l in range(LAYERS):
                    for k in range(2):
                        mul, add = m[0:rows, l, 2 * k + 1, :], m[0:rows, l, 2 * k, :]
                        step(g.tensor_scalar(mul, mul, 1.0, None, ALU.add))
                        if l == 1:
                            w, b = a[0:rows, 2 * k:2 * k + 1], a[0:rows, 2 * k + 1:2 * k + 2]
                            step(g.tensor_scalar(mod_w[0:rows, :], mul, b, None, ALU.mult))
                            step(g.tensor_tensor(add, add, mod_w[0:rows, :], ALU.add))
                            step(g.tensor_scalar(mul, mul, w, None, ALU.mult))
                        if l == 2:
                            step(g.tensor_scalar(mul, mul, a[0:rows, 4 + k:5 + k], None, ALU.mult))
            g.memset(mod_w[:], 0.0).then_inc(mods_ready, 1)

            for s in range(STEPS + 1):
                if s < STEPS:
                    pool.wait_ge(var1, s + 1)
                    g.tensor_tensor(rstd[:, 0, :], vare[:, 0, :], nhalf[:], ALU.pow).then_inc(rstd1, 1)
                if s > 0:
                    pool.wait_ge(var2, s)
                    g.tensor_tensor(rstd[:, 1, :], vare[:, 1, :], nhalf[:], ALU.pow).then_inc(rstd2, 1)
                if s < STEPS:
                    for v in (2 * s, 2 * s + 1):
                        pool.wait_ge(att_ready, v + 1)
                        g.tensor_tensor(x[:, v % B, :], x[:, v % B, :], attd[v % 2], ALU.add).then_inc(att_added, 1)

        @block.scalar
        def _(act):
            a = nc.scalar

            loaded(act, "cond")
            a.activation(e_t[:], c_t[:], ACT.Exp, scale=-1.0)
            a.activation(e_u[0:CT, :], c_u[0:CT, :], ACT.Exp, scale=-1.0).then_inc(silu_e, 1)

            def flat(tile):
                return tile[:].rearrange("p b d -> p (b d)")

            for k, (name, arg) in enumerate(pre):
                act.wait_ge(pre_full, k + 1)
                src = ps[:, k % 6, :]
                if name == "upper":
                    i = a.activation(upper[:], src[0:D, :].rearrange("p (j b) -> p b j", b=B), ACT.Copy,
                                     scale=2.0 ** -SQUARINGS)
                elif name == "skew":
                    i = a.activation(flat(bmat), src[0:D, :], ACT.Copy)
                elif name == "n2":
                    i = a.activation(flat(n2), src[0:D, :], ACT.Copy)
                elif name == "n4":
                    i = a.activation(flat(n4), src[0:D, :], ACT.Copy)
                elif name == "poly":
                    i = a.activation(flat(poly[arg[0]][arg[1]]), src[0:D, :], ACT.Copy)
                    if arg == (0, 1):
                        i.then_inc(pre_read, 1)
                        i = a.activation(flat(nodd), src[0:D, :], ACT.Copy, scale=-1.0)
                elif name == "expm":
                    i = a.activation(flat((ex, fx)[arg][0]), src[0:D, :], ACT.Copy)
                elif name == "square":
                    i = a.activation(flat((ex, fx)[arg[1]][arg[0] % 2]), src[0:D, :], ACT.Copy)
                elif name == "mods":
                    m, rows = ((mod_t, 128), (mod_u, CT))[arg]
                    act.wait_ge(late_consts, 1)
                    i = a.activation(m[0:rows, :, :, :].rearrange("p l k b -> p (l k b)"),
                                     src[0:rows, 0:LAYERS * 4 * B], ACT.Copy)
                else:
                    i = a.activation(gate[:, arg[0], arg[1], :, :].rearrange("p k c -> p (k c)"), src[:, 0:2 * C], ACT.Copy)
                i.then_inc(pre_read, 1)

            act.wait_ge(gram_read, 3)
            for base in (0, 64):
                i = a.activation(sel[base:base + 32, :, :], one_h[base:base + 32, :].rearrange("p (h o) -> p h o", o=1)
                                 .broadcast_to([32, H, 128]), ACT.Copy)
            i.then_inc(sel_ready, 1)
            act.wait_ge(pre_read, pre_reads[-1])
            third = gate[:, 2, :, :, :].rearrange("p b k c -> p (b k c)")
            a.activation(third, third, ACT.Tanh).then_inc(gates_tanh, 1)

            def q_parts(v):
                h, l = v % 2, v // B
                act.wait_ge(qkv_full, v + 1)
                if v >= 2:
                    act.wait_ge(prob_used, 4 * (v - 2) + 4)
                a.activation(v_aug[h][:, :, 0:HD], ps[:, 1, 2 * C:3 * C].rearrange("p (h d) -> p h d", d=HD),
                             ACT.Copy).then_inc(v_ready, 1)
                if v >= 2:
                    act.wait_ge(kT_full, v - 1)
                if l == 2:
                    act.wait_ge(qk_normed, v - 2 * B + 1)
                for k, slots in ((0, Q1), (1, K1)):
                    src = qk[h][:, k, :, :] if l == 2 else \
                        ps[:, 1, k * C:(k + 1) * C].rearrange("p (h d) -> p h d", d=HD)
                    src = src.rearrange("p h (o d) -> p h o d", o=1).broadcast_to([T, H, 3, HD])
                    dst = parts[k][h][:, :, 0:HROWS].rearrange("p h (s d) -> p h s d", d=HD)[:, :, slots, :]
                    a.activation(dst, src, ACT.Copy).then_inc(first_parts, 1)

            def k_out(v):
                act.wait_ge(kT_full, v + 1)
                if v >= 2:
                    act.wait_ge(sT_full, 4 * (v - 2) + 4)
                a.activation(qkT[1][v % 2].rearrange("p k t -> p (k t)"), ps[:, 7, :].bitcast(BF16),
                             ACT.Copy).then_inc(kT_ready, 1)

            def exps(v):
                for g in range(4):
                    act.wait_ge(sT_full, 4 * v + g + 1)
                    if v >= 1:
                        act.wait_ge(prob_used, 4 * (v - 1) + g + 1)
                    a.activation(prob[g].rearrange("p i t -> p (i t)"), ps[:, 2 + g % 2, :], ACT.Exp,
                                 scale=SCALE).then_inc(prob_ready, 1)

            def o_out(v):
                act.wait_ge(prob_used, 4 * v + 4)
                if v >= 2:
                    act.wait_ge(back_full, v - 1)
                a.activation(o_raw[v % 2].rearrange("p g t -> p (g t)"), ps[:, 4, :],
                             ACT.Copy).then_inc(o_raw_ready, 1)

            def gelu(m):
                f = ACT.Gelu if m // (B // 2) == 1 else ACT.Gelu_apprx_tanh
                if m >= 1:
                    act.wait_ge(fc2_full, m)
                for r in range(3):
                    act.wait_ge(fc1_full, 3 * m + r + 1)
                    rows, n = (128, 2) if r < 2 else (64, 1)
                    a.activation(hid[0:rows, 2 * r:2 * r + n, :, :].rearrange("p c h t -> p (c h t)"),
                                 ps[0:rows, 4 + r % 2, 0:n * 2 * T], f).then_inc(hid_ready, 1)

            act.wait_ge(late_consts, 1)
            for s in range(STEPS + 1):
                va, vb = 2 * s, 2 * s + 1
                if s < STEPS:
                    q_parts(va)
                    q_parts(vb)
                if s > 0:
                    gelu(s - 1)
                if s < STEPS:
                    k_out(va)
                    k_out(vb)
                    for v in (va, vb):
                        exps(v)
                        o_out(v)

        @block.tensor
        def _(pe):
            def mm(o, lhsT, rhs, start=True, stop=True):
                return pe.matmul(o, lhsT, rhs, start=start, stop=stop, skip_group_check=True)

            loaded(pe, "p")
            for q in range(2):
                o = ps[0:32, 7, q * D:(q + 1) * D]
                mm(o, p_t[:, 32 * q:32 * q + 32], p_t[:], True, False)
                i = mm(o, p_u[:, 32 * q:32 * q + 32], p_u[:], False, True)
            i.then_inc(gram_full, 1)

            def sized(k, n):
                if k >= 6:
                    pe.wait_ge(pre_read, pre_reads[k - 6])
                return ps[0:D, k % 6, :].rearrange("p (b d) -> p b d", b=B) if n is None else ps[0:n, k % 6, :]

            pe.wait_ge(early_consts, 3)
            for k, (name, arg) in enumerate(pre):
                if name == "upper":
                    pe.wait_ge(silu_ready, 1)
                    loaded(pe, "skw")
                    o = sized(k, D)
                    for j in range(D):
                        mm(o[:, j * B:(j + 1) * B], skw_t[:, j * D:(j + 1) * D], s_t[:], True, False)
                        i = mm(o[:, j * B:(j + 1) * B], skw_u[:, j * D:(j + 1) * D], s_u[:], False, True)
                elif name == "skew":
                    pe.wait_ge(pre_read, was_read("upper", 0))
                    o = sized(k, None)
                    mm(o, ident[0:D, 0:D], upper[:], True, False)
                    for b in range(B):
                        i = mm(o[:, b, :], upper[:, b, :], eyes[:, eye_of(-1.0), :], False, b == B - 1)
                elif name == "n2":
                    pe.wait_ge(pre_read, was_read("skew", 0))
                    o = sized(k, None)
                    for b in range(B):
                        i = mm(o[:, b, :], bmat[:, b, :], bmat[:, b, :])
                elif name == "n4":
                    pe.wait_ge(pre_read, was_read("n2", 0))
                    o = sized(k, None)
                    for b in range(B):
                        i = mm(o[:, b, :], n2[:, b, :], n2[:, b, :])
                elif name == "poly":
                    d, f = arg
                    c = (COS, SIN)[f]
                    pe.wait_ge(pre_read, was_read("n4", 0) if d == 2 else was_read("poly", (d + 1, f)))
                    o = sized(k, None)
                    mm(o, eyes[:, eye_of(c[2 * d]), :], irep[:], True, False)
                    i = mm(o, eyes[:, eye_of(c[2 * d + 1]), :], n2[:], False, False)
                    if d == 2:
                        i = mm(o, eyes[:, eye_of(c[6]), :], n4[:], False, True)
                    else:
                        for b in range(B):
                            i = mm(o[:, b, :], n4[:, b, :], poly[d + 1][f][:, b, :], False, b == B - 1)
                elif name == "expm":
                    pe.wait_ge(pre_read, was_read("poly", (0, 1)))
                    o = sized(k, None)
                    mm(o, ident[0:D, 0:D], poly[0][0][:], True, False)
                    odd = (nodd, poly[0][1])[arg]
                    for b in range(B):
                        i = mm(o[:, b, :], bmat[:, b, :], odd[:, b, :], False, b == B - 1)
                elif name == "square":
                    d, f = arg
                    last = d == SQUARINGS
                    pe.wait_ge(pre_read, was_read("expm", 1) if d == 1 else was_read("square", (d - 1, 1)))
                    o = sized(k, None)
                    if last:
                        mm(o, eyes[:, eye_of(-1.0), :], irep[:], True, False)
                    e, t_ = ((ex, fx), (fx, ex))[f]
                    for b in range(B):
                        i = mm(o[:, b, :], t_[(d - 1) % 2][:, b, :], e[(d - 1) % 2][:, b, :], not last, b == B - 1 or not last)
                elif name == "mods":
                    m0, rows = ((0, 128), (128, CT))[arg]
                    o = sized(k, rows)
                    for l in range(LAYERS):
                        loaded(pe, f"ada{l}")
                        for n, part in enumerate((0, 1, 3, 4)):
                            at = part * C + m0
                            oo = o[:, (4 * l + n) * B:(4 * l + n + 1) * B]
                            mm(oo, adaw_t[l][:, at:at + rows], s_t[:], True, False)
                            i = mm(oo, adaw_u[l][:, at:at + rows], s_u[:], False, True)
                else:
                    l, b = arg
                    loaded(pe, f"ada{l}")
                    o = sized(k, 128)
                    for n, part in enumerate((2, 5)):
                        oo = o[:, n * C:(n + 1) * C]
                        mm(oo, s_t[:, b:b + 1].broadcast_to([128, T]), adaw_t[l][:, part * C:(part + 1) * C], True, False)
                        i = mm(oo, s_u[:, b:b + 1].broadcast_to([KT, T]), adaw_u[l][:, part * C:(part + 1) * C], False, True)
                i.then_inc(pre_full, 1)

            pe.wait_ge(linv_ready, 1)
            for q in range(2):
                i = pe.transpose(ps[0:D, 6, 32 * q:32 * q + 32], linv[:, q, :], ident[0:32, 0:32])
            i.then_inc(rot_full, 1)
            pe.wait_ge(rot_read, 1)
            pe.wait_ge(gram_read, 1)
            mm(ps[:, 7, 0:D], pT[:, 0:128], linvT[:])
            mm(ps[0:CT, 7, D:2 * D], pT[:, 128:C], linvT[:])
            mm(ps[0:D, 7, 2 * D:2 * D + C], linvT[:], pT[:]).then_inc(rot_full, 1)
            pe.wait_ge(rot_read, 2)
            loaded(pe, "x")
            for n in range(2):
                o = ps[0:D, 6 + n, :]
                mm(o, u_t[:], x_t[:, 512 * n:512 * n + 512], True, False)
                mm(o, u_u[:], x_u[:, 512 * n:512 * n + 512], False, True).then_inc(rot_full, 1)
            for n in range(2):
                pe.wait_ge(rot_read, 3 + n)
                pe.wait_ge(pre_read, pre_reads[-1])
                for b in range(4 * n, 4 * n + 4):
                    i = mm(ps[0:D, 6 + n, (b % 4) * T:(b % 4 + 1) * T], ex[SQUARINGS % 2][:, b, :], zT[:, b * T:(b + 1) * T])
                i.then_inc(rot_full, 1)
            for n in range(4):
                pe.wait_ge(rot_read, 5 + n)
                for b in range(2 * n, 2 * n + 2):
                    i = mm(ps[:, 6 + n % 2, (b % 2) * C:(b % 2 + 1) * C], yT[:, b * T:(b + 1) * T], uT[:])
                i.then_inc(rot_full, 1)

            reader = {bk: (rot_read, 10) for bk in (6, 7)}
            reader.update({bk: (pre_read, pre_reads[-1]) for bk in range(6)})

            def refill(bk, s_, count):
                pe.wait_ge(*reader[bk])
                reader[bk] = (s_, count)
                return ps[:, bk, :]

            def turn(o, src):
                pe.transpose(o[:, 0:T], src[:, 0:128], ident[:])
                return pe.transpose(o[0:KT, T:2 * T], src[:, 128:C + 1], ident[:])

            def h_turn(v):
                o = refill(0, hT_ready, v + 1)
                pe.wait_ge(ln_ready, v + 1)
                turn(o, ln[0][v % 2]).then_inc(hT_full, 1)

            def h2_turn(v):
                o = refill(0, h2T_ready, v + 1)
                pe.wait_ge(ln2_ready, v + 1)
                turn(o, ln[1][v % 2]).then_inc(h2T_full, 1)

            def qkv(v):
                h, l = v % 2, v // B
                o = refill(1, qkv_read, v + 1)
                pe.wait_ge(hT_ready, v + 1)
                if v % B < 2:
                    loaded(pe, f"blk{l}")
                mm(o[:, 0:3 * C], hT_t[h][:], qkvw_t[l][:], True, False)
                mm(o[:, 0:3 * C], hT_u[h][:], qkvw_u[l][:], False, True).then_inc(qkv_full, 1)

            def fc1(m, r):
                l = m // (B // 2)
                o = refill(4 + r % 2, hid_ready, 3 * m + r + 1)
                if r == 0:
                    pe.wait_ge(h2T_ready, 2 * m + 2)
                for c in range(2 * r, min(2 * r + 2, FFC)):
                    rows = 128 if c < 4 else 64
                    oo = o[0:rows, (c % 2) * 2 * T:(c % 2 + 1) * 2 * T]
                    mm(oo, fc1w_t[l][:, c * 128:c * 128 + rows], mT_t[:].rearrange("p h t -> p (h t)"), True, False)
                    i = mm(oo, fc1w_u[l][:, c * 128:c * 128 + rows], mT_u[:].rearrange("p h t -> p (h t)"), False, True)
                i.then_inc(fc1_full, 1)

            def fc2(m):
                l = m // (B // 2)
                o = refill(5, mlp_ready, m + 1)
                pe.wait_ge(hid_ready, 3 * m + 3)
                for h in range(2):
                    for c in range(FFC):
                        rows = 128 if c < 4 else 65
                        i = mm(o[:, h * C:(h + 1) * C], hid[0:rows, c, h, :], fc2w[l][0:rows, c, :], c == 0, c == FFC - 1)
                i.then_inc(fc2_full, 1)

            def parts_turn(v, k):
                o = refill(6 + k, (qT_ready, kT_ready)[k], v + 1).bitcast(BF16)
                pe.wait_ge(parts_ready, 2 * v + k + 1)
                for pair in range(H // 2):
                    i = pe.transpose(o[:, pair * T:(pair + 1) * T],
                                     parts[k][v % 2][:, 2 * pair:2 * pair + 2, :].rearrange("p h d -> p (h d)"), identb[:])
                i.then_inc((qT_full, kT_full)[k], 1)

            def operands(v, g, i):
                hd = head_of(g, i)
                r = 64 * (hd % 2)
                return hd, [qkT[k][v % 2][r:r + HROWS, hd // 2, :] for k in (0, 1)]

            def scores(v):
                pe.wait_ge(qT_ready, v + 1)
                pe.wait_ge(kT_ready, v + 1)
                for g in range(4):
                    o = refill(2 + g % 2, max_ready, 4 * v + g + 1)
                    for n in range(4):
                        _, (q, k) = operands(v, g, n)
                        i = mm(o[:, n * T:(n + 1) * T], q, k)
                    i.then_inc(s_full, 1)

            def max_turn(v):
                o = refill(0, nmT_ready, v + 1).bitcast(BF16)
                pe.wait_ge(nmp_ready, v + 1)
                pe.transpose(o[0:96, 0:T], nmp[v % 2][:], identb[:]).then_inc(mT_full, 1)

            def scores_T(v, g):
                o = refill(2 + g % 2, prob_ready, 4 * v + g + 1)
                if g == 0:
                    pe.wait_ge(nmT_ready, v + 1)
                for n in range(4):
                    hd, (q, k) = operands(v, g, n)
                    r = 64 * (hd % 2)
                    mm(o[:, n * T:(n + 1) * T], k, q, True, False)
                    i = mm(o[:, n * T:(n + 1) * T], sel[r:r + 32, hd, :], nmT[v % 2][r:r + 32, :], False, True)
                i.then_inc(sT_full, 1)

            def pv(v, g):
                if g == 0:
                    refill(4, o_raw_ready, v + 1)
                    pe.wait_ge(v_ready, v + 1)
                pe.wait_ge(prob_ready, 4 * v + g + 1)
                for n in range(4):
                    i = pe.matmul(ps[32 * n:32 * n + 32, 4, g * T:(g + 1) * T], v_aug[v % 2][:, head_of(g, n), :],
                                  prob[g][:, n, :], start=True, stop=True, skip_group_check=True)
                i.then_inc(prob_used, 1)

            def o_back(v):
                o = refill(5, o_n_ready, v + 1)
                pe.wait_ge(o_raw_ready, v + 1)
                for g in range(4):
                    i = pe.transpose(o[:, g * T:(g + 1) * T], o_raw[v % 2][:, g, :], ident[:])
                i.then_inc(back_full, 1)

            def o_turn(v):
                o = refill(0, oT_ready, v + 1)
                pe.wait_ge(o_n_ready, v + 1)
                turn(o, o_n[v % 2]).then_inc(oT_full, 1)

            def proj(v):
                h, l = v % 2, v // B
                o = refill(1, att_ready, v + 1)
                pe.wait_ge(oT_ready, v + 1)
                mm(o[:, 0:C], oT_t[h][:], projw_t[l][:], True, False)
                mm(o[:, 0:C], oT_u[h][:], projw_u[l][:], False, True).then_inc(proj_full, 1)

            pe.wait_ge(late_consts, 1)
            pe.wait_ge(sel_ready, 1)
            for s in range(STEPS + 1):
                a, b, m = 2 * s, 2 * s + 1, s - 1
                if s < STEPS:
                    h_turn(a)
                    h_turn(b)
                if m >= 0:
                    h2_turn(a - 2)
                    h2_turn(b - 2)
                if s < STEPS:
                    qkv(a)
                    qkv(b)
                if m >= 0:
                    fc1(m, 0)
                    fc1(m, 1)
                    fc1(m, 2)
                if s < STEPS:
                    for v in (a, b):
                        parts_turn(v, 0)
                        parts_turn(v, 1)
                    scores(a)
                    scores(b)
                if m >= 0:
                    fc2(m)
                if s < STEPS:
                    max_turn(a)
                    scores_T(a, 0)
                    for g in range(4):
                        if g < 3:
                            scores_T(a, g + 1)
                        pv(a, g)
                    max_turn(b)
                    scores_T(b, 0)
                    scores_T(b, 1)
                    pv(b, 0)
                    o_back(a)
                    scores_T(b, 2)
                    pv(b, 1)
                    scores_T(b, 3)
                    pv(b, 2)
                    o_turn(a)
                    pv(b, 3)
                    proj(a)
                    o_back(b)
                    o_turn(b)
                    proj(b)

        @block.vector
        def _(dve):
            d = nc.vector
            n = [0]

            def did(ins):
                n[0] += 1
                ins.then_inc(dve_step, 1)
                return n[0]

            def need(count):
                dve.wait_ge(dve_step, count)

            dve.wait_ge(silu_e, 1)
            dve.wait_ge(early_consts, 1)
            k = did(d.tensor_scalar(e_t[:], e_t[:], 1.0, None, ALU.add))
            k = did(d.tensor_scalar(e_u[0:CT, :], e_u[0:CT, :], 1.0, None, ALU.add))
            need(k)
            k = did(d.reciprocal(e_t[:], e_t[:]))
            k = did(d.reciprocal(e_u[0:CT, :], e_u[0:CT, :]))
            need(k)
            d.tensor_tensor(s_t[:], c_t[:], e_t[:], ALU.mult)
            d.tensor_tensor(s_u[0:CT, :], c_u[0:CT, :], e_u[0:CT, :], ALU.mult).then_inc(silu_ready, 1)
            d.memset(mod_u[:, :, 0:4:2, :], 0.0)
            k = did(d.memset(mod_u[:, :, 1:4:2, :], 1.0))
            for h in range(2):
                for kk in range(2):
                    d.memset(ln[kk][h][:, C:C + 1], 1.0)
                    d.memset(parts[kk][h][:, :, HROWS:64], 0.0)
                d.memset(o_n[h][:, C:C + 1], 1.0)
                d.memset(v_aug[h][:, :, HD:HD + 1], 1.0)
                d.memset(v_aug[h][:, :, HD + 1:32], 0.0)
                i = d.memset(nmp[h][:], 0.0)
            i.then_inc(late_consts, 1)

            dve.wait_ge(gram_full, 1)
            dve.wait_ge(early_consts, 2)
            d.tensor_copy(elim[:, :, 0:D], ps[0:32, 7, 0:2 * D].rearrange("p (q d) -> p q d", q=2)).then_inc(gram_read, 1)
            for base in (0, 64):
                i = d.tensor_tensor(one_h[base:base + 32, :], ident[base:base + 32, base:base + 16],
                                    ident[base:base + 32, base + 16:base + 32], ALU.add)
                i.then_inc(gram_read, 1)
            dve.wait_ge(gram_read, 1)
            loaded(dve, "p")

            g_done = {}

            def spread(rows, out_, j):
                return d.stream_shuffle(out_, rows, [j % 32] * 32)

            upd = {}
            upd["g", 0] = upd["g", 1] = upd["t", 0] = upd["t", 1] = 0

            def gram_pivot(j):
                need(upd["g", j // 32])
                if j >= 4:
                    dve.wait_ge(root_ready, j - 3)
                spread(elim[:, j // 32, j:j + D + 1], grow[:, j % 4, j:j + D + 1], j).then_inc(grow_ready, 1)

            def top_pivot(j):
                need(upd["t", j // 32])
                return did(spread(top[:, j // 32, j:D], trow[:, j % 2, j:D], j))

            for j in range(D + 1):
                gq = [q for q in range(2) if j < 32 * q + 31] if j < D else []
                tj = j - 1
                tq = [q for q in range(2) if tj < 32 * q + 31] if tj >= 0 else []
                if j < D:
                    gram_pivot(j)
                if tj >= 0:
                    k_row = top_pivot(tj)
                if j < D:
                    dve.wait_ge(grow_ready, j + 1)
                    k_rec = did(d.reciprocal(grec[:, j:j + 1], grow[:, j % 4, j:j + 1]))
                if tj >= 0:
                    need(k_row)
                    dve.wait_ge(root_ready, tj + 1)
                    k_beta = did(d.scalar_tensor_tensor(
                        out=beta[:, tj:tj + 1].bitcast(U32), in0=trow[:, tj % 2, tj:tj + 1].bitcast(U32), scalar=0x80000000,
                        in1=root[:, tj:tj + 1].bitcast(U32), op0=ALU.bitwise_and, op1=ALU.bitwise_or))
                if gq:
                    need(k_rec)
                    k_fac = did(d.scalar_tensor_tensor(
                        out=gfac[:, j % 2, :].rearrange("p (q o) -> p q o", o=1), in0=elim[:, :, j:j + 1],
                        scalar=grec[:, j:j + 1], in1=below[:, :, j:j + 1], op0=ALU.mult, op1=ALU.mult))
                if tq:
                    need(k_beta)
                    k_den = did(d.scalar_tensor_tensor(
                        out=den[:, tj:tj + 1], in0=trow[:, tj % 2, tj:tj + 1], scalar=beta[:, tj:tj + 1],
                        in1=beta[:, tj:tj + 1], op0=ALU.add, op1=ALU.mult))
                for q in gq:
                    need(k_fac)
                    w = slice(j + 1, j + D + 1)
                    upd["g", q] = did(d.scalar_tensor_tensor(
                        out=elim[:, q, w], in0=grow[:, j % 4, w], scalar=gfac[:, j % 2, q:q + 1], in1=elim[:, q, w],
                        op0=ALU.mult, op1=ALU.add))
                if tq:
                    need(k_den)
                    did(d.reciprocal(drec[:, tj:tj + 1], den[:, tj:tj + 1]))
                    k_num = did(d.scalar_tensor_tensor(
                        out=tnum[:, tj % 2, :].rearrange("p (q o) -> p q o", o=1), in0=top[:, :, tj:tj + 1],
                        scalar=beta[:, tj:tj + 1], in1=elim[:, :, tj:tj + 1], op0=ALU.mult, op1=ALU.add))
                    need(k_num)
                    k_fac2 = did(d.scalar_tensor_tensor(
                        out=tfac[:, tj % 2, :].rearrange("p (q o) -> p q o", o=1),
                        in0=tnum[:, tj % 2, :].rearrange("p (q o) -> p q o", o=1), scalar=drec[:, tj:tj + 1],
                        in1=below[:, :, tj:tj + 1], op0=ALU.mult, op1=ALU.mult))
                    need(k_fac2)
                    for q in tq:
                        w = slice(tj + 1, D)
                        upd["t", q] = did(d.scalar_tensor_tensor(
                            out=top[:, q, w], in0=trow[:, tj % 2, w], scalar=tfac[:, tj % 2, q:q + 1], in1=top[:, q, w],
                            op0=ALU.mult, op1=ALU.add))

            need(n[0])
            k = did(d.tensor_tensor(sgn[:], beta[:], grec[:], ALU.mult))
            need(k)
            for q in range(2):
                k = did(d.tensor_tensor(sgnd[:, q, :], sgn[:], diag[:, q, :], ALU.mult))
            need(k)
            k = did(d.tensor_reduce(rscale[:], sgnd[:], AX_X, ALU.add))
            need(k)
            for q in range(2):
                i = d.tensor_scalar(linv[:, q, :], elim[:, q, D:2 * D], rscale[:, q:q + 1], None, ALU.mult)
            i.then_inc(linv_ready, 1)
            dve.wait_ge(pre_full, 1)
            d.memset(hid[64:96, FFC - 1, :, :], 1.0)

            dve.wait_ge(rot_full, 1)
            d.tensor_copy(linvT[:], ps[0:D, 6, 0:D]).then_inc(rot_read, 1)
            dve.wait_ge(rot_full, 2)
            d.tensor_copy(u_t[:], ps[:, 7, 0:D])
            d.tensor_copy(u_u[:], ps[0:CT, 7, D:2 * D])
            d.tensor_copy(uT[:], ps[0:D, 7, 2 * D:2 * D + C]).then_inc(rot_read, 1)
            for n_ in range(2):
                dve.wait_ge(rot_full, 3 + n_)
                d.tensor_copy(zT[:, 512 * n_:512 * n_ + 512], ps[0:D, 6 + n_, :]).then_inc(rot_read, 1)
            for n_ in range(2):
                dve.wait_ge(rot_full, 5 + n_)
                d.tensor_copy(yT[:, 512 * n_:512 * n_ + 512], ps[0:D, 6 + n_, :]).then_inc(rot_read, 1)
            for n_ in range(4):
                dve.wait_ge(rot_full, 7 + n_)
                xs = x[:, 2 * n_:2 * n_ + 2, :].rearrange("p b c -> p (b c)")
                d.tensor_tensor(xs, xs, ps[:, 6 + n_ % 2, 0:2 * C], ALU.add).then_inc(rot_read, 1)

            def variances(kind, s, done):
                l = s // (B // 2)
                for h in range(2):
                    b = (2 * s + h) % B
                    k = did(d.bn_stats(st6[:, kind, h, :], x[:, b, :]))
                need(k)
                for h in range(2):
                    k = did(d.bn_aggr(st2[:, kind, h, :], st6[:, kind, h, :]))
                need(k)
                if l < 2:
                    d.tensor_scalar(vare[:, kind, :], st2[:, kind, :, 1], LN_EPS[l], None, ALU.add).then_inc(done, 1)
                    return
                k = did(d.tensor_tensor(msq[:, kind, :], st2[:, kind, :, 0], st2[:, kind, :, 0], ALU.mult))
                need(k)
                k = did(d.tensor_tensor(msq[:, kind, :], msq[:, kind, :], st2[:, kind, :, 1], ALU.add))
                need(k)
                d.tensor_scalar(vare[:, kind, :], msq[:, kind, :], 1e-24 / C, None, ALU.max).then_inc(done, 1)

            def normalise(kind, s, done):
                l = s // (B // 2)
                for h in range(2):
                    b = (2 * s + h) % B
                    if l < 2:
                        i = d.tensor_scalar(ln[kind][h][:, 0:C], x[:, b, :], st2[:, kind, h, 0:1], rstd[:, kind, h:h + 1],
                                            ALU.subtract, ALU.mult)
                    else:
                        i = d.tensor_scalar(ln[kind][h][:, 0:C], x[:, b, :], rstd[:, kind, h:h + 1], None, ALU.mult)
                    i.then_inc(done, 1)

            def modulated(out_t, out_u, v, kind, done):
                l, b = v // B, v % B
                d.tensor_scalar(out_t, ps[:, 0, 0:T], mod_t[:, l, 2 * kind + 1, b:b + 1], mod_t[:, l, 2 * kind, b:b + 1],
                                ALU.mult, ALU.add)
                d.tensor_scalar(out_u, ps[0:KT, 0, T:2 * T], mod_u[:, l, 2 * kind + 1, b:b + 1],
                                mod_u[:, l, 2 * kind, b:b + 1], ALU.mult, ALU.add).then_inc(done, 1)

            def slot(k, h, slots):
                return parts[k][h][:, :, 0:HROWS].rearrange("p h (s d) -> p h s d", d=HD)[:, :, slots, :]

            def unit_norms(v):
                h = v % 2
                dve.wait_ge(v_ready, v + 1)
                src = ps[:, 1, 0:2 * C].rearrange("p (k d) -> p k d", d=HD)
                raw = res[h][:].rearrange("p k h d -> p (k h) d")
                k = did(d.tensor_copy(raw, src))
                dve.wait_ge(dve_step, k)
                k = did(d.tensor_tensor(sq[:], raw, raw, ALU.mult))
                need(k)
                k = did(d.tensor_reduce(ssq[:].rearrange("p k h -> p (k h)"), sq[:], AX_X, ALU.add))
                need(k)
                k = did(d.tensor_scalar(ssq[:], ssq[:], 1e-24, None, ALU.max))
                need(k)
                k = did(d.tensor_scalar(ny[:].bitcast(I32), ssq[:].bitcast(I32), -0.5, RSQRT_SEED, ALU.mult, ALU.add))
                need(k)
                for _ in range(3):
                    k = did(d.scalar_tensor_tensor(out=my[:], in0=ny[:], scalar=-0.5, in1=ny[:], op0=ALU.mult, op1=ALU.mult))
                    need(k)
                    k = did(d.tensor_tensor(my[:], my[:], ssq[:], ALU.mult))
                    need(k)
                    k = did(d.scalar_tensor_tensor(out=ny[:], in0=my[:], scalar=1.5, in1=ny[:], op0=ALU.add, op1=ALU.mult))
                    need(k)
                for kk in range(2):
                    k = did(d.tensor_scalar(ny[:, kk, :], ny[:, kk, :], float(HD) ** 0.5, qkg[:, kk:kk + 1], ALU.mult, ALU.mult))
                need(k)
                if v - 2 * B >= 2:
                    dve.wait_ge(first_parts, 2 * (v - 2) + 2)
                fac = ny[:].rearrange("p k (h o) -> p (k h) o", o=1).broadcast_to([T, 2 * H, HD])
                d.tensor_tensor(qk[h][:].rearrange("p k h d -> p (k h) d"), raw, fac, ALU.mult).then_inc(qk_normed, 1)
                dve.wait_ge(qk_normed, v - 2 * B + 1)

            def split(v):
                h, l = v % 2, v // B
                if l == 2:
                    unit_norms(v)
                dve.wait_ge(first_parts, 2 * v + 2)
                firsts, seconds = (slice(1, 2), slice(2, 3)), (slice(0, 1), slice(0, 1))
                for k in range(2):
                    src = qk[h][:, k, :, :] if l == 2 else \
                        ps[:, 1, k * C:(k + 1) * C].rearrange("p (h d) -> p h d", d=HD)
                    i = d.tensor_tensor(res[h][:, k, :, :], src, slot(k, h, firsts[k])[:, :, 0, :], ALU.subtract)
                    if k == 0:
                        did(i)
                    else:
                        i.then_inc(qkv_read, 1)
                dve.wait_ge(qkv_read, v + 1)
                for k, slots in ((0, Q2), (1, K2)):
                    src = res[h][:, k, :, :].rearrange("p h (o d) -> p h o d", o=1).broadcast_to([T, H, 2, HD])
                    c = did(d.tensor_copy(slot(k, h, slots), src))
                need(c)
                for k, slots in ((0, Q3), (1, K3)):
                    d.tensor_tensor(slot(k, h, slots)[:, :, 0, :], res[h][:, k, :, :], slot(k, h, seconds[k])[:, :, 0, :],
                                    ALU.subtract).then_inc(parts_ready, 1)

            def q_out(v):
                dve.wait_ge(qT_full, v + 1)
                if v >= 2:
                    dve.wait_ge(sT_full, 4 * (v - 2) + 4)
                d.tensor_copy(qkT[0][v % 2].rearrange("p k t -> p (k t)"), ps[:, 6, :].bitcast(BF16)).then_inc(qT_ready, 1)

            def maxima(v):
                h = v % 2
                for g in range(4):
                    dve.wait_ge(s_full, 4 * v + g + 1)
                    first = head_of(g, 0)
                    d.tensor_reduce(nmax[:, h, first:first + 7:2], ps[:, 2 + g % 2, :].rearrange("p (i t) -> p i t", i=4),
                                    AX_X, ALU.max, negate=True).then_inc(max_ready, 1)
                dve.wait_ge(max_ready, 4 * v + 4)
                if v >= 2:
                    dve.wait_ge(mT_full, v - 1)
                k = did(d.tensor_copy(nmp[h][:, 0:16], nmax[:, h, :]))
                did(d.tensor_copy(nmp[h][:, 64:80], nmax[:, h, :]))
                need(k)
                d.tensor_tensor(nmp[h][:, 16:32], nmax[:, h, :], nmp[h][:, 0:16], ALU.subtract)
                d.tensor_tensor(nmp[h][:, 80:96], nmax[:, h, :], nmp[h][:, 0:16], ALU.subtract).then_inc(nmp_ready, 1)

            def max_out(v):
                dve.wait_ge(mT_full, v + 1)
                if v >= 2:
                    dve.wait_ge(sT_full, 4 * (v - 2) + 4)
                d.tensor_copy(nmT[v % 2][:], ps[0:96, 0, :].bitcast(BF16)[:, 0:T]).then_inc(nmT_ready, 1)

            def attended(v):
                h = v % 2
                dve.wait_ge(back_full, v + 1)
                src = ps[:, 5, :].rearrange("p (h r) -> p h r", r=32)
                k = did(d.reciprocal(orec[h][:].rearrange("p (h o) -> p h o", o=1), src[:, :, HD:HD + 1]))
                need(k)
                if v >= 2:
                    dve.wait_ge(oT_full, v - 1)
                d.tensor_tensor(o_n[h][:, 0:C].rearrange("p (h d) -> p h d", d=HD), src[:, :, 0:HD],
                                orec[h][:].rearrange("p (h o) -> p h o", o=1).broadcast_to([T, H, HD]),
                                ALU.mult).then_inc(o_n_ready, 1)

            def o_T(v):
                h = v % 2
                dve.wait_ge(oT_full, v + 1)
                if v >= 2:
                    dve.wait_ge(proj_full, v - 1)
                d.tensor_copy(oT_t[h][:], ps[:, 0, 0:T])
                d.tensor_copy(oT_u[h][:], ps[0:KT, 0, T:2 * T]).then_inc(oT_ready, 1)

            def gated(v):
                h, l, b = v % 2, v // B, v % B
                dve.wait_ge(proj_full, v + 1)
                if v >= 2:
                    dve.wait_ge(att_added, v - 1)
                d.tensor_tensor(attd[h], ps[:, 1, 0:C], gate[:, l, b, 0, :], ALU.mult).then_inc(att_ready, 1)

            def mlp_out(m):
                l, b = m // (B // 2), 2 * m % B
                dve.wait_ge(fc2_full, m + 1)
                d.tensor_tensor(mlpd, ps[:, 5, 0:2 * C].rearrange("p (h c) -> p h c", h=2), gate[:, l, b:b + 2, 1, :],
                                ALU.mult).then_inc(mlp_ready, 1)
                dve.wait_ge(mlp_ready, m + 1)
                for h in range(2):
                    d.tensor_tensor(x[:, b + h, :], x[:, b + h, :], mlpd[:, h, :], ALU.add).then_inc(mlp_added, 1)

            dve.wait_ge(rot_read, 10)
            dve.wait_ge(mods_ready, 1)
            dve.wait_ge(pre_read, pre_reads[-1])
            dve.wait_ge(late_consts, 1)
            for s in range(STEPS + 1):
                va, vb, m = 2 * s, 2 * s + 1, s - 1
                if s < STEPS:
                    if s >= B // 2:
                        dve.wait_ge(mlp_added, 2 * (s - B // 2) + 2)
                    variances(0, s, var1)
                if m >= 0:
                    dve.wait_ge(att_added, 2 * m + 2)
                    variances(1, m, var2)
                if s < STEPS:
                    dve.wait_ge(rstd1, s + 1)
                    if s >= 1:
                        dve.wait_ge(hT_full, 2 * s)
                    normalise(0, s, ln_ready)
                if m >= 0:
                    dve.wait_ge(rstd2, m + 1)
                    if m >= 1:
                        dve.wait_ge(h2T_full, 2 * m)
                    normalise(1, m, ln2_ready)
                if s == 2 * (B // 2):
                    dve.wait_ge(gates_tanh, 1)
                if s < STEPS:
                    for v in (va, vb):
                        dve.wait_ge(hT_full, v + 1)
                        if v >= 2:
                            dve.wait_ge(qkv_full, v - 1)
                        modulated(hT_t[v % 2][:], hT_u[v % 2][:], v, 0, hT_ready)
                if m >= 0:
                    if m >= 1:
                        dve.wait_ge(fc1_full, 3 * m)
                    for v in (2 * m, 2 * m + 1):
                        dve.wait_ge(h2T_full, v + 1)
                        modulated(mT_t[:, v % 2, :], mT_u[:, v % 2, :], v, 1, h2T_ready)
                if s < STEPS:
                    split(va)
                    split(vb)
                    q_out(va)
                    q_out(vb)
                    maxima(va)
                    maxima(vb)
                if m >= 0:
                    mlp_out(m)
                if s < STEPS:
                    max_out(va)
                    max_out(vb)
                    attended(va)
                    o_T(va)
                    gated(va)
                    attended(vb)
                    o_T(vb)
                    gated(vb)


def kernel(**inputs):
    import concourse.bacc as bacc
    from concourse.bass_utils import run_bass_kernel_spmd

    f = {k: np.asarray(v) for k, v in inputs.items()}

    def rows(w, b=None):
        return np.concatenate([w, np.zeros((1, w.shape[1]), np.float32) if b is None else b[None, :]], axis=0)

    iu, ju = np.triu_indices(D, k=1)
    skw = np.zeros((C + 1, D, D), np.float32)
    skw[0:C, ju, iu] = f["L0_cond_W"].T
    skw[C, ju, iu] = f["L0_cond_b"]
    order = np.concatenate([np.arange(HD) + HD * head_of(g, i) for g in range(4) for i in range(4)])
    p = f["L0_cond_P"]
    vec = lambda v: np.broadcast_to(v, (C,))
    a = {
        "x": f["x"].transpose(1, 0, 2),
        "xT": f["x"].transpose(2, 0, 1).reshape(C, B * T),
        "cond": f["cond_1152"].T,
        "p": p, "pT": p.T,
        "ptop": p.T[:, 0:D].reshape(2, 32, D).transpose(1, 0, 2),
        "skw": skw.reshape(C + 1, D * D),
        "aff": np.stack([f["L2_cond_ln1_w"], f["L2_cond_ln1_b"], f["L2_cond_ln2_w"], f["L2_cond_ln2_b"],
                         vec(f["L3_cond_g1"]), vec(f["L3_cond_g2"])], axis=1),
        "qkg": np.stack([np.broadcast_to(f["L3_cond_qg"], (T,)), np.broadcast_to(f["L3_cond_kg"], (T,))], axis=1),
        "ada0": rows(f["L1_cond_W_ada"], f["L1_cond_b_ada"]),
        "ada1": rows(f["L2_cond_ada_w"], f["L2_cond_ada_b"]),
        "ada2": rows(f["L3_cond_ada_w"].T, f["L3_cond_ada_b"]),
        "qkv0": rows(f["L1_cond_W_qkv"], f["L1_cond_b_qkv"]),
        "qkv1": rows(np.concatenate([f["L2_cond_wq"], f["L2_cond_wk"], f["L2_cond_wv"]], axis=1)),
        "qkv2": rows(f["L3_cond_qkv_w"].T, f["L3_cond_qkv_b"]),
        "proj0": rows(f["L1_cond_W_proj"][order], f["L1_cond_b_proj"]),
        "proj1": rows(f["L2_cond_wo"][order], f["L2_cond_wo_b"]),
        "proj2": rows(f["L3_cond_proj_w"].T[order], f["L3_cond_proj_b"]),
        "fc10": rows(f["L1_cond_W_fc1"], f["L1_cond_b_fc1"]),
        "fc11": rows(f["L2_cond_fc1_w"], f["L2_cond_fc1_b"]),
        "fc12": rows(f["L3_cond_fc1_w"].T, f["L3_cond_fc1_b"]),
        "fc20": rows(f["L1_cond_W_fc2"], f["L1_cond_b_fc2"]),
        "fc21": rows(f["L2_cond_fc2_w"], f["L2_cond_fc2_b"]),
        "fc22": rows(f["L3_cond_fc2_w"].T, f["L3_cond_fc2_b"]),
    }
    nc = bacc.Bacc("TRN2", target_bir_lowering=False, num_devices=1)
    arrays, t = {}, {}
    for name, v in a.items():
        v = np.ascontiguousarray(v)
        arrays["in_" + name] = v
        t[name] = nc.dram_tensor("in_" + name, v.shape, F32, kind="ExternalInput").ap()
    out = nc.dram_tensor("out_x", (T, B, C), F32, kind="ExternalOutput").ap()
    program(nc, t, out)
    r = run_bass_kernel_spmd(nc, [arrays], core_ids=[0])
    return r.results[0]["out_x"].transpose(1, 0, 2)
```

```python
from contextlib import ExitStack

import numpy as np

import concourse.bass as bass
from concourse import mybir

F32 = mybir.dt.float32
BF16 = mybir.dt.bfloat16
U32 = mybir.dt.uint32
I32 = mybir.dt.int32
ALU = mybir.AluOpType
ACT = mybir.ActivationFunctionType
AX_X = mybir.AxisListType.X

B, T, C = 8, 128, 144
D = 64
CT = C - 128
KT = CT + 1
H, HD = 16, 9
FF = 4 * C
FFC = 5
LAYERS = 3
SLOTS = 6
HROWS = SLOTS * HD
Q1, Q2, Q3 = slice(1, 6, 2), slice(0, 3, 2), slice(4, 5)
K1, K2, K3 = slice(2, 5), slice(0, 2), slice(5, 6)
KS = SLOTS * KT
GM = 2 * C + 4 * CT
WSPLIT = (3 * C + FF) // 4
SCALE = float(HD) ** -0.5
SQUARINGS = 7
STEPS = LAYERS * B // 2
LN_EPS = [1e-6, 1e-5, 0.0]
RSQRT_SEED = 1597463007.0
FACT = [1.0]
for _n in range(1, 16):
    FACT.append(FACT[-1] * _n)
COS = [(-1.0) ** k / FACT[2 * k] for k in range(4)]
SIN = [(-1.0) ** k / FACT[2 * k + 1] for k in range(4)]
VISITS = LAYERS * B
EYES = sorted(set(COS) | set(SIN) | {-1.0})


def eye_of(c):
    return EYES.index(c)


def plan_rotation():
    chain = [("upper", 0), ("skew", 0), ("n2", 0), ("n4", 0)]
    chain += [("poly", (k, f)) for k in (1, 0) for f in (0, 1)]
    chain += [("expm", 0), ("expm", 1)]
    chain += [("square", (k, f)) for k in range(1, SQUARINGS + 1) for f in (0, 1) if k < SQUARINGS or f == 0]
    other = [("gate", b) for b in range(B)] + [("mods", 0)]
    fills = chain[:2]
    for k in range(max(len(chain) - 2, len(other))):
        fills += chain[2 + k:3 + k] + other[k:k + 1]
    return fills


def head_of(g, i):
    return 8 * (g // 2) + 2 * i + g % 2


def program(nc, t, out):
    ctx = ExitStack()
    with ctx:
        def sb(name, shape, dt=F32):
            return ctx.enter_context(nc.sbuf_tensor(name, shape, dt))

        def sem(name):
            return ctx.enter_context(nc.semaphore(name))

        x = sb("x", [T, B, C])
        x_t, x_u = sb("x_t", [128, B * T]), sb("x_u", [CT, B * T])
        c_t, c_u = sb("c_t", [128, B]), sb("c_u", [KT, B])
        e_t, e_u = sb("e_t", [128, B]), sb("e_u", [KT, B])
        s_t, s_u = sb("s_t", [128, B]), sb("s_u", [KT, B])
        p_t, p_u, pT = sb("p_t", [128, D]), sb("p_u", [CT, D]), sb("pT", [D, C])
        skw_t, skw_r = sb("skw_t", [128, D * D]), sb("skw_r", [128, D * D])
        skw_u = skw_r[0:KT, :]
        qkvw_t = [sb(f"qkvw_t{l}", [128, 3 * C]) for l in range(LAYERS)]
        projw_t = [sb(f"projw_t{l}", [128, C]) for l in range(LAYERS)]
        projw_u = [sb(f"projw_u{l}", [KT, C]) for l in range(LAYERS)]
        fc1w_t = [sb(f"fc1w_t{l}", [128, FF]) for l in range(LAYERS)]
        tails = sb("tails", [KS, LAYERS, 3 * C + FF])
        tailw = sb("tailw", [KS, LAYERS, 3 * C + FF], BF16)
        tmask = sb("tmask", [KS, 2])
        fc2w = [sb(f"fc2w{l}", [128, FFC, C]) for l in range(LAYERS)]
        adaw_t = [sb(f"adaw_t{l}", [128, 6 * C]) for l in range(LAYERS)]
        adaw_u = [sb(f"adaw_u{l}", [KT, 6 * C]) for l in range(LAYERS)]
        aff_t = sb("aff_t", [128, 6])
        aff_u = sb("aff_u", [T, 2, 3, CT])
        qkg = sb("qkg", [T, 2])

        ident = sb("ident", [128, 128])
        identb = sb("identb", [128, 128], BF16)
        eyes = sb("eyes", [D, len(EYES), D])
        irep = sb("irep", [D, B, D])
        below = sb("below", [32, 2, D])
        diag = sb("diag", [32, 2, D])
        table_out = sb("table_out", [32, 1])
        half, nhalf = sb("half", [32, 1]), sb("nhalf", [T, 2])
        one_h = sb("one_h", [128, H])
        sel = sb("sel", [128, H, 128], BF16)

        elim = sb("elim", [32, 2, 2 * D])
        top = sb("top", [32, 2, D])
        grow = sb("grow", [32, 4, 2 * D])
        trow = sb("trow", [32, 2, D])
        grec, gfac = sb("grec", [32, D]), sb("gfac", [32, 2, 2])
        root = sb("root", [32, D])
        beta = sb("beta", [32, D])
        den, drec = sb("den", [32, D]), sb("drec", [32, D])
        tnum, tfac = sb("tnum", [32, 2, 2]), sb("tfac", [32, 2, 2])
        sgn = sb("sgn", [32, D])
        sgnd = sb("sgnd", [32, 2, D])
        rscale = sb("rscale", [32, 2])
        linv = sb("linv", [32, 2, D])
        linvT = sb("linvT", [D, D])
        u_t, u_u, uT = sb("u_t", [128, D]), sb("u_u", [CT, D]), sb("uT", [D, C])
        zT, yT = sb("zT", [D, B * T]), sb("yT", [D, B * T])
        upper = sb("upper", [128, B, D // 2])
        nident = sb("nident", [128, D])
        bmat = sb("bmat", [D, B, D])
        brief = sb("brief", [128, 6, B * D])
        n2, n4 = [brief[0:D, k, :].rearrange("p (b d) -> p b d", b=B) for k in range(2)]
        poly = [[brief[0:D, 2 + 2 * k + f, :].rearrange("p (b d) -> p b d", b=B) for f in range(2)] for k in range(2)]
        nodd = sb("nodd", [D, B, D])
        ex, fx = [poly[1][0], sb("ex1", [D, B, D])[:]], [poly[1][1], sb("fx1", [D, B, D])[:]]

        mod_t = sb("mod_t", [128, LAYERS, 4, B])
        mod_w = sb("mod_w", [128, B])
        gmod = sb("gmod", [T, LAYERS, B, GM])
        mod_v = sb("mod_v", [T, 2, CT])
        tprod = gmod[0:KS, 1:3, :, :].rearrange("p l b g -> p (l b g)")[:, 0:LAYERS * (3 * C + FF)].rearrange(
            "p (l n) -> p l n", l=LAYERS)

        st6 = sb("st6", [T, 2, 2, 6])
        st2 = sb("st2", [T, 2, 2, 2])
        vare, rstd = sb("vare", [T, 2, 2]), sb("rstd", [T, 2, 2])
        msq = sb("msq", [T, 2, 2])
        ln = [[sb(f"ln{k}{h}", [T, C]) for h in range(2)] for k in range(2)]
        hT_t = [sb(f"hT_t{h}", [128, T]) for h in range(2)]
        hT_u = [sb(f"hT_u{h}", [KS, T], BF16) for h in range(2)]
        mT_t, mT_u = sb("mT_t", [128, 2, T]), sb("mT_u", [KS, 2, T], BF16)
        tail = [[sb(f"tail{k}{h}", [T, CT]) for h in range(2)] for k in range(2)]
        tailp = [[sb(f"tailp{k}{h}", [T, SLOTS, KT], BF16) for h in range(2)] for k in range(2)]
        qk = [sb(f"qk{h}", [T, 2, H, HD]) for h in range(2)]
        sq = sb("sq", [T, 2 * H, HD])
        ssq, hy, ny, my = sb("ssq", [T, 2, H]), sb("hy", [T, 2, H]), sb("ny", [T, 2, H]), sb("my", [T, 2, H])
        res = [sb(f"res{h}", [T, 2, H, HD]) for h in range(2)]
        parts = [[brief[:, 2 * k + h, :].bitcast(BF16).rearrange("p (h d) -> p h d", h=H) for h in range(2)] for k in range(2)]
        n_qkT, n_hid = H // 4 * T, FFC * 2 * T
        qkT = [[skw_r[:, (2 * k + h) * n_qkT:(2 * k + h + 1) * n_qkT].bitcast(BF16)
                .rearrange("p (n t) -> p n t", t=T) for h in range(2)] for k in range(2)]
        hid = skw_r[:, 4 * n_qkT:4 * n_qkT + n_hid].rearrange("p (c h t) -> p c h t", c=FFC, h=2)
        prob = [skw_t[:, g * 4 * T:(g + 1) * 4 * T].rearrange("p (i t) -> p i t", t=T) for g in range(4)]
        o_raw = [skw_t[:, (4 + h) * 4 * T:(5 + h) * 4 * T].rearrange("p (g t) -> p g t", t=T) for h in range(2)]
        v_aug = [tile.rearrange("p (h r) -> p h r", h=H)
                 for tile in (brief[:, 4, :], brief[:, 5, :], sb("v_aug2", [T, H * 32])[:])]
        nmax = sb("nmax", [T, 2, H])
        nmp = [sb(f"nmp{h}", [T, 128], BF16) for h in range(2)]
        nmT = [sb(f"nmT{h}", [128, T], BF16) for h in range(2)]
        orec = [sb(f"orec{h}", [T, H]) for h in range(2)]
        o_n = [sb(f"o_n{h}", [T, C + 1]) for h in range(2)]
        oT_t = [sb(f"oT_t{h}", [128, T]) for h in range(2)]
        oT_u = [sb(f"oT_u{h}", [KT, T]) for h in range(2)]
        n_far = 4 * n_qkT + n_hid
        attd = [skw_r[:, n_far + h * C:n_far + (h + 1) * C] for h in range(2)]
        mlpd = skw_r[:, n_far + 2 * C:n_far + 4 * C].rearrange("p (h c) -> p h c", h=2)

        ps = ctx.enter_context(nc.psum_tensor("ps", [128, 8, 512], F32))

        ld = {n: sem("ld_" + n) for n in ("cond", "p", "skw", "x", "misc", "ada0", "ada1", "ada2",
                                          "blk0", "blk1", "blk2", "tail0", "tail1", "tail2", "tmask")}
        loads = {"cond": 2, "p": 4, "skw": 2, "x": 3, "misc": 3, "ada0": 2, "ada1": 2, "ada2": 2,
                 "blk0": 6, "blk1": 6, "blk2": 6, "tail0": 1, "tail1": 1, "tail2": 1, "tmask": 1}
        pool_step = sem("pool_step")
        dve_step = sem("dve_step")
        early_consts = sem("early_consts")
        late_consts = sem("late_consts")
        slots_zeroed = sem("slots_zeroed")
        sel_ready = sem("sel_ready")
        silu_e, silu_ready = sem("silu_e"), sem("silu_ready")
        gram_full, gram_read = sem("gram_full"), sem("gram_read")
        grow_ready = sem("grow_ready")
        root_ready = sem("root_ready")
        pre_full, pre_read = sem("pre_full"), sem("pre_read")
        rot_full, rot_read = sem("rot_full"), sem("rot_read")
        linv_ready = sem("linv_ready")
        mods_ready = sem("mods_ready")
        gate_full, gate_ready = sem("gate_full"), sem("gate_ready")
        tail_cast, tail_left, tailw_ready = sem("tail_cast"), sem("tail_left"), sem("tailw_ready")
        act_step = sem("act_step")
        tailp_ready, tail2p_ready = sem("tailp_ready"), sem("tail2p_ready")
        table_used = sem("table_used")
        var1, rstd1 = sem("var1"), sem("rstd1")
        var2, rstd2 = sem("var2"), sem("rstd2")
        ln_ready, ln2_ready = sem("ln_ready"), sem("ln2_ready")
        hT_full, hT_ready = sem("hT_full"), sem("hT_ready")
        h2T_full, h2T_ready = sem("h2T_full"), sem("h2T_ready")
        qkv_full, qkv_read = sem("qkv_full"), sem("qkv_read")
        v_ready, squared, qk_normed = sem("v_ready"), sem("squared"), sem("qk_normed")
        first_parts, parts_ready = sem("first_parts"), sem("parts_ready")
        qT_full, qT_ready = sem("qT_full"), sem("qT_ready")
        kT_full, kT_ready = sem("kT_full"), sem("kT_ready")
        s_full, max_ready = sem("s_full"), sem("max_ready")
        nmp_ready, mT_full, nmT_ready = sem("nmp_ready"), sem("mT_full"), sem("nmT_ready")
        sT_full, prob_ready, prob_used = sem("sT_full"), sem("prob_ready"), sem("prob_used")
        o_raw_ready, back_full, o_n_ready = sem("o_raw_ready"), sem("back_full"), sem("o_n_ready")
        oT_full, oT_ready = sem("oT_full"), sem("oT_ready")
        proj_full, att_ready, att_added = sem("proj_full"), sem("att_ready"), sem("att_added")
        fc1_full, hid_ready = sem("fc1_full"), sem("hid_ready")
        fc2_full, mlp_ready, mlp_added = sem("fc2_full"), sem("mlp_ready"), sem("mlp_added")
        stored = sem("stored")

        pre = plan_rotation()
        pre_at = {fill: k for k, fill in enumerate(pre)}
        reads, pre_reads = 0, []
        for fill in pre:
            reads += 2 if fill == ("poly", (0, 1)) else 1
            pre_reads.append(reads)

        def was_read(name, arg):
            return pre_reads[pre_at[name, arg]]

        block = ctx.enter_context(nc.Block())

        @block.sync
        def _(sp):
            def load(dst, src, s):
                sp.dma_start(dst, src).then_inc(ld[s], 16)

            load(p_t[:], t["p"][0:128, :], "p")
            load(p_u[:], t["p"][128:C, :], "p")
            load(c_t[:], t["cond"][0:128, :], "cond")
            load(c_u[0:CT, :], t["cond"][128:C, :], "cond")
            load(top[:], t["ptop"], "p")
            load(pT[:], t["pT"], "p")
            load(skw_t[:], t["skw"][0:128, :], "skw")
            load(skw_u, t["skw"][128:C + 1, :], "skw")
            load(tmask[:], t["tmask"], "tmask")
            for l in range(LAYERS):
                load(tails[:, l, :], t[f"tail{l}"], f"tail{l}")
            for l in range(LAYERS):
                load(adaw_t[l][:], t[f"ada{l}"][0:128, :], f"ada{l}")
                load(adaw_u[l][:], t[f"ada{l}"][128:C + 1, :], f"ada{l}")
            load(x[:], t["x"], "x")
            load(x_t[:], t["xT"][0:128, :], "x")
            load(x_u[:], t["xT"][128:C, :], "x")
            load(aff_t[:], t["aff"], "misc")
            load(aff_u[:], t["aff_u"], "misc")
            load(qkg[:], t["qkg"], "misc")
            for l in range(LAYERS):
                load(qkvw_t[l][:], t[f"qkv{l}"][0:128, :], f"blk{l}")
                load(projw_t[l][:], t[f"proj{l}"][0:128, :], f"blk{l}")
                load(projw_u[l][:], t[f"proj{l}"][128:C + 1, :], f"blk{l}")
                load(fc1w_t[l][:], t[f"fc1{l}"][0:128, :], f"blk{l}")
                load(fc2w[l][:, 0:4, :], t[f"fc2{l}"][0:512, :].rearrange("(c p) n -> p c n", p=128), f"blk{l}")
                load(fc2w[l][0:65, 4, :], t[f"fc2{l}"][512:FF + 1, :], f"blk{l}")
            for pair in range(B // 2):
                sp.wait_ge(mlp_added, 2 * (STEPS - B // 2 + pair) + 2)
                sp.dma_start(out[:, 2 * pair:2 * pair + 2, :], x[:, 2 * pair:2 * pair + 2, :]).then_inc(stored, 16)
            sp.wait_ge(stored, 16 * (B // 2))

        FC1_BANKS, GATE_BANKS = (5, 0, 5), (None, 0, 0)

        def mlp_step(slot, lag):
            m = (slot - lag) // 2
            return m if slot >= lag and (slot - lag) % 2 == 0 and m < STEPS else None

        def loaded(eng, s):
            eng.wait_ge(ld[s], 16 * loads[s])

        @block.gpsimd
        def _(pool):
            g = nc.gpsimd
            n = [0]

            def step(ins):
                n[0] += 1
                ins.then_inc(pool_step, 1)
                pool.wait_ge(pool_step, n[0])

            def filled(tile, fill, base=0, compare=ALU.not_equal):
                step(g.memset(tile, 0.0))
                return g.affine_select(out=tile, in_=tile, compare_op=compare, fill=fill, base=-base,
                                       pattern=[[1, tile.shape[1]]], channel_multiplier=-1)

            g.memset(s_u[:], 1.0).then_inc(early_consts, 1)
            g.memset(half[:], 0.5)
            g.memset(nhalf[:], -0.5)
            for q in range(2):
                step(filled(elim[:, q, D:2 * D], 1.0, 32 * q))
                step(filled(diag[:, q, :], -1.0, 32 * q))
                step(filled(below[:, q, :], -1.0, 32 * q, ALU.is_ge))
                step(filled(nident[64 * q:64 * q + 64, :], -1.0))
            filled(ident[:], 1.0).then_inc(early_consts, 1)
            pool.wait_ge(early_consts, 2)
            for k, c in enumerate(EYES):
                g.tensor_scalar(eyes[:, k, :], ident[0:D, 0:D], c, None, ALU.mult)
            for b in range(B):
                step(g.tensor_copy(irep[:, b, :], ident[0:D, 0:D]))
            g.tensor_copy(identb[:], ident[:]).then_inc(early_consts, 1)

            def weight_left(k, l, c):
                pool.wait_ge(tail_cast, LAYERS * k + l + 1)
                w = tails[:, l, c * WSPLIT:(c + 1) * WSPLIT]
                i = g.tensor_tensor(w, w, tprod[:, l, c * WSPLIT:(c + 1) * WSPLIT], ALU.add)
                if c == 3:
                    i.then_inc(tail_left, 1)

            for j in range(D):
                pool.wait_ge(grow_ready, j + 1)
                g.tensor_tensor(root[:, j:j + 1], grow[:, j % 4, j:j + 1], half[:], ALU.pow).then_inc(root_ready, 1)
                if 10 <= j < 10 + 4 * LAYERS:
                    weight_left(0, (j - 10) // 4, (j - 10) % 4)
                elif 38 <= j < 38 + 8 * LAYERS and j % 2 == 0:
                    weight_left(1, (j - 38) // 8, (j - 38) // 2 % 4)

            pool.wait_ge(pre_read, pre_reads[-1])
            for h in range(2):
                for k in range(2):
                    g.memset(parts[k][h][:, :, HROWS:64], 0.0)
            for h in range(3):
                g.memset(v_aug[h][:, :, HD:HD + 1], 1.0)
                i = g.memset(v_aug[h][:, :, HD + 1:32], 0.0)
            i.then_inc(slots_zeroed, 1)
            loaded(pool, "misc")
            for l in range(LAYERS):
                for k in range(2):
                    mul, add = mod_t[:, l, 2 * k + 1, :], mod_t[:, l, 2 * k, :]
                    step(g.tensor_scalar(mul, mul, 1.0, None, ALU.add))
                    if l == 1:
                        w, b = aff_t[:, 2 * k:2 * k + 1], aff_t[:, 2 * k + 1:2 * k + 2]
                        step(g.tensor_scalar(mod_w[:], mul, b, None, ALU.mult))
                        step(g.tensor_tensor(add, add, mod_w[:], ALU.add))
                        step(g.tensor_scalar(mul, mul, w, None, ALU.mult))
                    if l == 2:
                        step(g.tensor_scalar(mul, mul, aff_t[:, 4 + k:5 + k], None, ALU.mult))

            def tail_mods(l, b):
                m = gmod[:, l, b, 2 * C:GM].rearrange("p (k s c) -> p k s c", k=2, s=2)
                mul, add = m[:, :, 1, :], m[:, :, 0, :]
                step(g.tensor_scalar(mul, mul, 1.0, None, ALU.add))
                if l == 1:
                    step(g.tensor_tensor(mod_v[:], mul, aff_u[:, :, 1, :], ALU.mult))
                    step(g.tensor_tensor(add, add, mod_v[:], ALU.add))
                    step(g.tensor_tensor(mul, mul, aff_u[:, :, 0, :], ALU.mult))
                if l == 2:
                    step(g.tensor_tensor(mul, mul, aff_u[:, :, 2, :], ALU.mult))

            for b in range(B):
                tail_mods(0, b)
            for k in range(2):
                for h in range(2):
                    step(g.memset(tailp[k][h][:], 0.0))
                    step(g.memset(tailp[k][h][:, Q1, CT:KT], 1.0))
            g.memset(mod_w[:], 0.0).then_inc(mods_ready, 1)

            def tail_parts(kind, v, input_ready, used, done):
                h, l, b = v % 2, v // B, v % B
                y, p = tail[kind][h], tailp[kind][h]
                m = gmod[:, l, b, 2 * C + kind * 2 * CT:2 * C + (kind + 1) * 2 * CT]

                def again(slots):
                    n_ = len(range(SLOTS)[slots])
                    return y[:].rearrange("p (o c) -> p o c", o=1).broadcast_to([T, n_, CT])

                pool.wait_ge(*input_ready)
                if used is not None:
                    pool.wait_ge(*used)
                step(g.tensor_tensor(y[:], ln[kind][h][:, 128:C], m[:, CT:2 * CT], ALU.mult))
                step(g.tensor_tensor(y[:], y[:], m[:, 0:CT], ALU.add))
                step(g.tensor_copy(p[:, Q1, 0:CT], again(Q1)))
                step(g.tensor_tensor(y[:], y[:], p[:, 1, 0:CT], ALU.subtract))
                step(g.tensor_copy(p[:, Q2, 0:CT], again(Q2)))
                g.tensor_tensor(p[:, 4, 0:CT], y[:], p[:, 0, 0:CT], ALU.subtract).then_inc(done, 1)

            for slot in range(-2, VISITS + 3):
                m = mlp_step(slot, 3)
                v, u = slot + 2, slot - 2
                if v < VISITS:
                    pool.wait_ge(var1, v + 1)
                    h = v % 2
                    g.tensor_tensor(rstd[:, 0, h:h + 1], vare[:, 0, h:h + 1], nhalf[:, 0:1], ALU.pow).then_inc(rstd1, 1)
                if 0 <= u < VISITS:
                    pool.wait_ge(att_ready, u + 1)
                    g.tensor_tensor(x[:, u % B, :], x[:, u % B, :], attd[u % 2], ALU.add).then_inc(att_added, 1)
                if m is not None:
                    pool.wait_ge(var2, m + 1)
                    g.tensor_tensor(rstd[:, 1, :], vare[:, 1, :], nhalf[:], ALU.pow).then_inc(rstd2, 1)
                if v < VISITS:
                    tail_parts(0, v, (ln_ready, v + 1), (hT_full, v - 1) if v >= 2 else None, tailp_ready)
                if m is not None:
                    for n_ in (2 * m, 2 * m + 1):
                        tail_parts(1, n_, (ln2_ready, n_ + 1), (h2T_full, m) if m >= 1 else None, tail2p_ready)
                if 1 <= slot <= B:
                    pool.wait_ge(gate_ready, 2 * slot)
                    tail_mods(1, slot - 1)
                    tail_mods(2, slot - 1)

        @block.scalar
        def _(act):
            a = nc.scalar

            loaded(act, "cond")
            a.activation(e_t[:], c_t[:], ACT.Exp, scale=-1.0)
            a.activation(e_u[0:CT, :], c_u[0:CT, :], ACT.Exp, scale=-1.0).then_inc(silu_e, 1)

            def flat(tile):
                return tile.rearrange("p b d -> p (b d)")

            def weight_part(k, l):
                if k == 1:
                    act.wait_ge(tail_left, l + 1)
                a.activation(tailw[:, l, :], tails[:, l, :], ACT.Copy).then_inc(act_step, 1)
                act.wait_ge(act_step, LAYERS * k + l + 1)
                a.activation(tprod[:, l, :], tailw[:, l, :], ACT.Copy, scale=tmask[:, k:k + 1]).then_inc(tail_cast, 1)

            loaded(act, "tmask")
            for l in range(LAYERS):
                loaded(act, f"tail{l}")
                weight_part(0, l)

            for k, (name, arg) in enumerate(pre):
                act.wait_ge(pre_full, k + 1)
                src = ps[:, k % 6, :]
                if name == "upper":
                    i = a.activation(upper[:], src[:, 0:D // 2 * B].rearrange("p (j b) -> p b j", b=B), ACT.Copy,
                                     scale=2.0 ** -SQUARINGS)
                elif name == "skew":
                    i = a.activation(flat(bmat[:]), src[0:D, :], ACT.Copy)
                elif name == "n2":
                    i = a.activation(flat(n2), src[0:D, :], ACT.Copy)
                elif name == "n4":
                    i = a.activation(flat(n4), src[0:D, :], ACT.Copy)
                elif name == "poly":
                    i = a.activation(flat(poly[arg[0]][arg[1]]), src[0:D, :], ACT.Copy)
                    if arg == (0, 1):
                        i.then_inc(pre_read, 1)
                        i = a.activation(flat(nodd[:]), src[0:D, :], ACT.Copy, scale=-1.0)
                elif name == "expm":
                    i = a.activation(flat((ex, fx)[arg][0]), src[0:D, :], ACT.Copy)
                elif name == "square":
                    i = a.activation(flat((ex, fx)[arg[1]][arg[0] % 2]), src[0:D, :], ACT.Copy)
                elif name == "mods":
                    i = a.activation(mod_t[:].rearrange("p l k b -> p (l k b)"), src[:, 0:LAYERS * 4 * B], ACT.Copy)
                else:
                    i = a.activation(gmod[:, 0, arg, :], src[:, 0:GM], ACT.Copy)
                i.then_inc(pre_read, 1)
                if 6 <= k < 6 + LAYERS:
                    weight_part(1, k - 6)

            for l in range(LAYERS):
                act.wait_ge(tail_left, LAYERS + l + 1)
                a.activation(tailw[:, l, :], tails[:, l, :], ACT.Copy).then_inc(tailw_ready, 1)
            act.wait_ge(gram_read, 2)
            a.activation(sel[:], one_h[:].rearrange("p (h o) -> p h o", o=1).broadcast_to([128, H, 128]),
                         ACT.Copy).then_inc(sel_ready, 1)

            def v_out(v):
                act.wait_ge(qkv_full, v + 1)
                if v >= 3:
                    act.wait_ge(prob_used, 4 * (v - 3) + 4)
                a.activation(v_aug[v % 3][:, :, 0:HD], ps[:, 1, 2 * C:3 * C].rearrange("p (h d) -> p h d", d=HD),
                             ACT.Copy).then_inc(v_ready, 1)

            def squares(v):
                if v % B >= 1:
                    act.wait_ge(qk_normed, v - 2 * B)
                a.activation(sq[:], ps[:, 1, 0:2 * C].rearrange("p (k d) -> p k d", d=HD), ACT.Square).then_inc(squared, 1)

            def first(v, k):
                h, l = v % 2, v // B
                if v >= 2:
                    act.wait_ge((qT_full, kT_full)[k], v - 1)
                if l == 2:
                    act.wait_ge(qk_normed, v - 2 * B + 1)
                src = qk[h][:, k, :, :] if l == 2 else \
                    ps[:, 1, k * C:(k + 1) * C].rearrange("p (h d) -> p h d", d=HD)
                src = src.rearrange("p h (o d) -> p h o d", o=1).broadcast_to([T, H, 3, HD])
                dst = parts[k][h][:, :, 0:HROWS].rearrange("p h (s d) -> p h s d", d=HD)[:, :, (Q1, K1)[k], :]
                a.activation(dst, src, ACT.Copy).then_inc(first_parts, 1)

            def k_out(v):
                act.wait_ge(kT_full, v + 1)
                if v >= 2:
                    act.wait_ge(sT_full, 4 * (v - 2) + 4)
                for n in (0, 4):
                    a.activation(qkT[1][v % 2][:, n:n + 4, :].rearrange("p k t -> p (k t)"),
                                 ps[:, 7, :].bitcast(BF16)[:, n * T:(n + 4) * T], ACT.Copy).then_inc(kT_ready, 1)

            def exps(v, g):
                act.wait_ge(sT_full, 4 * v + g + 1)
                if v >= 1:
                    act.wait_ge(prob_used, 4 * (v - 1) + g + 1)
                a.activation(prob[g].rearrange("p i t -> p (i t)"), ps[:, 2 + g % 2, :], ACT.Exp,
                             scale=SCALE).then_inc(prob_ready, 1)

            def gate_out(l, b):
                act.wait_ge(gate_full, 2 * b + l)
                if l == 2:
                    a.activation(gmod[:, l, b, 0:2 * C], ps[:, GATE_BANKS[l], 0:2 * C], ACT.Tanh)
                    i = a.activation(gmod[:, l, b, 2 * C:GM], ps[:, GATE_BANKS[l], 2 * C:GM], ACT.Copy)
                else:
                    i = a.activation(gmod[:, l, b, :], ps[:, GATE_BANKS[l], 0:GM], ACT.Copy)
                i.then_inc(gate_ready, 1)

            def o_out(v):
                act.wait_ge(prob_used, 4 * v + 4)
                if v >= 2:
                    act.wait_ge(back_full, v - 1)
                a.activation(o_raw[v % 2].rearrange("p g t -> p (g t)"), ps[:, 4, :],
                             ACT.Copy).then_inc(o_raw_ready, 1)

            tables = [0]

            def bring_table(f):
                if tables[0]:
                    act.wait_ge(table_used, tables[0])
                tables[0] += 1
                a.activation(table_out[:], half[:], f).then_inc(table_used, 1)

            def gelu(m, r):
                f = ACT.Gelu if m // (B // 2) == 1 else ACT.Gelu_apprx_tanh
                if m >= 1:
                    act.wait_ge(fc2_full, m)
                act.wait_ge(fc1_full, 3 * m + r + 1)
                rows, n = (128, 2) if r < 2 else (64, 1)
                a.activation(hid[0:rows, 2 * r:2 * r + n, :, :].rearrange("p c h t -> p (c h t)"),
                             ps[0:rows, FC1_BANKS[r], 0:n * 2 * T], f).then_inc(hid_ready, 1)

            def o_T(v):
                h = v % 2
                act.wait_ge(oT_full, v + 1)
                if v >= 2:
                    act.wait_ge(proj_full, v - 1)
                a.activation(oT_t[h][:], ps[:, 4, 0:T], ACT.Copy)
                a.activation(oT_u[h][:], ps[0:KT, 4, T:2 * T], ACT.Copy).then_inc(oT_ready, 1)

            act.wait_ge(late_consts, 1)
            act.wait_ge(slots_zeroed, 1)
            v_out(0)
            first(0, 0)
            first(0, 1)
            for slot in range(VISITS + 4):
                v, w = slot, slot - 1
                new, old = v < VISITS, 0 <= w < VISITS
                m = mlp_step(slot, 4)
                coming, third = v + 1 < VISITS, (v + 1) // B == 2
                if new:
                    k_out(v)
                if 0 <= slot - 2 < VISITS:
                    o_T(slot - 2)
                if coming:
                    v_out(v + 1)
                if coming and third:
                    squares(v + 1)
                if old:
                    exps(w, 0)
                if coming and not third:
                    first(v + 1, 0)
                    first(v + 1, 1)
                if old:
                    exps(w, 1)
                    exps(w, 2)
                    exps(w, 3)
                if coming and third:
                    first(v + 1, 0)
                    first(v + 1, 1)
                if m is not None:
                    bring_table(ACT.Gelu if m // (B // 2) == 1 else ACT.Gelu_apprx_tanh)
                if old:
                    o_out(w)
                if slot < B:
                    gate_out(1, slot)
                if m is not None:
                    gelu(m, 0)
                    gelu(m, 1)
                    gelu(m, 2)
                    bring_table(ACT.Exp)
                if slot < B:
                    gate_out(2, slot)

        @block.tensor
        def _(pe):
            def mm(o, lhsT, rhs, start=True, stop=True):
                return pe.matmul(o, lhsT, rhs, start=start, stop=stop, skip_group_check=True)

            loaded(pe, "p")
            for q in range(2):
                o = ps[0:32, 7, q * D:(q + 1) * D]
                mm(o, p_t[:, 32 * q:32 * q + 32], p_t[:], True, False)
                i = mm(o, p_u[:, 32 * q:32 * q + 32], p_u[:], False, True)
            i.then_inc(gram_full, 1)

            def sized(k, n):
                if k >= 6:
                    pe.wait_ge(pre_read, pre_reads[k - 6])
                return ps[0:D, k % 6, :].rearrange("p (b d) -> p b d", b=B) if n is None else ps[0:n, k % 6, :]

            def gates(o, l, b):
                loaded(pe, f"ada{l}")
                mm(o[:, 0:GM], s_t[:, b:b + 1].broadcast_to([128, T]), adaw_t[l][:, 0:GM], True, False)
                i = mm(o[:, 0:GM], s_u[:, b:b + 1].broadcast_to([KT, T]), adaw_u[l][:, 0:GM], False, True)
                return i

            pe.wait_ge(early_consts, 3)
            for k, (name, arg) in enumerate(pre):
                if name == "upper":
                    pe.wait_ge(silu_ready, 1)
                    loaded(pe, "skw")
                    o = sized(k, 128)
                    for j in range(D // 2):
                        mm(o[:, j * B:(j + 1) * B], skw_t[:, 2 * j * D:2 * (j + 1) * D], s_t[:], True, False)
                        i = mm(o[:, j * B:(j + 1) * B], skw_u[:, 2 * j * D:2 * (j + 1) * D], s_u[:], False, True)
                elif name == "skew":
                    pe.wait_ge(pre_read, was_read("upper", 0))
                    o = sized(k, None)
                    for q in range(2):
                        mm(o[:, :, 32 * q:32 * q + 32], ident[:, D * q:D * q + D], upper[:], q == 0, False)
                    for b in range(B):
                        for q in range(2):
                            r = slice(D * q, D * q + D)
                            i = mm(o[32 * q:32 * q + 32, b, :], upper[r, b, :], nident[r, :], False, b == B - 1)
                elif name == "n2":
                    pe.wait_ge(pre_read, was_read("skew", 0))
                    o = sized(k, None)
                    for b in range(B):
                        i = mm(o[:, b, :], bmat[:, b, :], bmat[:, b, :])
                elif name == "n4":
                    pe.wait_ge(pre_read, was_read("n2", 0))
                    o = sized(k, None)
                    for b in range(B):
                        i = mm(o[:, b, :], n2[:, b, :], n2[:, b, :])
                elif name == "poly":
                    d, f = arg
                    c = (COS, SIN)[f]
                    pe.wait_ge(pre_read, was_read("n2", 0) if d == 1 else was_read("poly", (d + 1, f)))
                    o = sized(k, None)
                    mm(o, eyes[:, eye_of(c[2 * d]), :], irep[:], True, False)
                    i = mm(o, eyes[:, eye_of(c[2 * d + 1]), :], n2, False, d == 1)
                    if d == 0:
                        for b in range(B):
                            i = mm(o[:, b, :], n4[:, b, :], poly[d + 1][f][:, b, :], False, b == B - 1)
                elif name == "expm":
                    pe.wait_ge(pre_read, was_read("poly", (0, 1)))
                    o = sized(k, None)
                    mm(o, ident[0:D, 0:D], poly[0][0], True, False)
                    odd = (nodd, poly[0][1])[arg]
                    for b in range(B):
                        i = mm(o[:, b, :], bmat[:, b, :], odd[:, b, :], False, b == B - 1)
                elif name == "square":
                    d, f = arg
                    last = d == SQUARINGS
                    pe.wait_ge(pre_read, was_read("expm", 1) if d == 1 else was_read("square", (d - 1, 1)))
                    o = sized(k, None)
                    if last:
                        mm(o, eyes[:, eye_of(-1.0), :], irep[:], True, False)
                    e, t_ = ((ex, fx), (fx, ex))[f]
                    for b in range(B):
                        i = mm(o[:, b, :], t_[(d - 1) % 2][:, b, :], e[(d - 1) % 2][:, b, :], not last, b == B - 1 or not last)
                elif name == "mods":
                    o = sized(k, 128)
                    for l in range(LAYERS):
                        loaded(pe, f"ada{l}")
                        for n in range(4):
                            at = GM + n * 128
                            oo = o[:, (4 * l + n) * B:(4 * l + n + 1) * B]
                            mm(oo, adaw_t[l][:, at:at + 128], s_t[:], True, False)
                            i = mm(oo, adaw_u[l][:, at:at + 128], s_u[:], False, True)
                else:
                    i = gates(sized(k, 128), 0, arg)
                i.then_inc(pre_full, 1)

            pe.wait_ge(linv_ready, 1)
            for q in range(2):
                i = pe.transpose(ps[0:D, 6, 32 * q:32 * q + 32], linv[:, q, :], ident[0:32, 0:32])
            i.then_inc(rot_full, 1)
            pe.wait_ge(rot_read, 1)
            pe.wait_ge(gram_read, 1)
            mm(ps[:, 7, 0:D], pT[:, 0:128], linvT[:])
            mm(ps[0:CT, 7, D:2 * D], pT[:, 128:C], linvT[:])
            mm(ps[0:D, 7, 2 * D:2 * D + C], linvT[:], pT[:]).then_inc(rot_full, 1)
            pe.wait_ge(rot_read, 2)
            loaded(pe, "x")
            for n in range(2):
                o = ps[0:D, 6 + n, :]
                mm(o, u_t[:], x_t[:, 512 * n:512 * n + 512], True, False)
                mm(o, u_u[:], x_u[:, 512 * n:512 * n + 512], False, True).then_inc(rot_full, 1)
            for n in range(2):
                pe.wait_ge(rot_read, 3 + n)
                pe.wait_ge(pre_read, pre_reads[-1])
                for b in range(4 * n, 4 * n + 4):
                    i = mm(ps[0:D, 6 + n, (b % 4) * T:(b % 4 + 1) * T], ex[SQUARINGS % 2][:, b, :], zT[:, b * T:(b + 1) * T])
                i.then_inc(rot_full, 1)
            for n in range(4):
                pe.wait_ge(rot_read, 5 + n)
                for b in range(2 * n, 2 * n + 2):
                    i = mm(ps[:, 6 + n % 2, (b % 2) * C:(b % 2 + 1) * C], yT[:, b * T:(b + 1) * T], uT[:])
                i.then_inc(rot_full, 1)

            reader = {bk: (rot_read, 10) for bk in (6, 7)}
            reader.update({bk: (pre_read, pre_reads[-1]) for bk in range(6)})

            def refill(bk, s_, count):
                pe.wait_ge(*reader[bk])
                reader[bk] = (s_, count)
                return ps[:, bk, :]

            def turn(o, src):
                pe.transpose(o[:, 0:T], src[:, 0:128], ident[:])
                return pe.transpose(o[0:KT, T:2 * T], src[:, 128:C + 1], ident[:])

            def turn_parts(o, src):
                return pe.transpose(o, src[:].rearrange("p s c -> p (s c)"), identb[:])

            def h_turn(v):
                o = refill(0, hT_ready, v + 1)
                pe.wait_ge(ln_ready, v + 1)
                pe.transpose(o[:, 0:T], ln[0][v % 2][:, 0:128], ident[:])
                pe.wait_ge(tailp_ready, v + 1)
                turn_parts(o.bitcast(BF16)[0:KS, 2 * T:3 * T], tailp[0][v % 2]).then_inc(hT_full, 1)

            def h2_turn(m):
                o = refill(0, h2T_ready, 2 * m + 2)
                for h in range(2):
                    pe.wait_ge(ln2_ready, 2 * m + h + 1)
                    pe.transpose(o[:, h * T:(h + 1) * T], ln[1][h][:, 0:128], ident[:])
                for h in range(2):
                    pe.wait_ge(tail2p_ready, 2 * m + h + 1)
                    i = turn_parts(o.bitcast(BF16)[0:KS, (4 + h) * T:(5 + h) * T], tailp[1][h])
                i.then_inc(h2T_full, 1)

            def qkv(v):
                h, l = v % 2, v // B
                o = refill(1, qkv_read, v + 1)
                pe.wait_ge(hT_ready, v + 1)
                if v % B < 2:
                    loaded(pe, f"blk{l}")
                    pe.wait_ge(tailw_ready, l + 1)
                mm(o[:, 0:3 * C], hT_t[h][:], qkvw_t[l][:], True, False)
                mm(o[:, 0:3 * C], hT_u[h][:], tailw[:, l, 0:3 * C], False, True).then_inc(qkv_full, 1)

            def fc1(m, r):
                l = m // (B // 2)
                o = refill(FC1_BANKS[r], hid_ready, 3 * m + r + 1)
                if r == 0:
                    pe.wait_ge(h2T_ready, 2 * m + 2)
                for c in range(2 * r, min(2 * r + 2, FFC)):
                    rows = 128 if c < 4 else 64
                    oo = o[0:rows, (c % 2) * 2 * T:(c % 2 + 1) * 2 * T]
                    mm(oo, fc1w_t[l][:, c * 128:c * 128 + rows], mT_t[:].rearrange("p h t -> p (h t)"), True, False)
                    i = mm(oo, tailw[:, l, 3 * C + c * 128:3 * C + c * 128 + rows], mT_u[:].rearrange("p h t -> p (h t)"), False, True)
                i.then_inc(fc1_full, 1)

            def fc2(m, h):
                l = m // (B // 2)
                if h == 0:
                    refill(5, mlp_ready, m + 1)
                    pe.wait_ge(hid_ready, 3 * m + 3)
                for c in range(FFC):
                    rows = 128 if c < 4 else 65
                    i = mm(ps[:, 5, h * C:(h + 1) * C], hid[0:rows, c, h, :], fc2w[l][0:rows, c, :], c == 0, c == FFC - 1)
                if h == 1:
                    i.then_inc(fc2_full, 1)

            def parts_turn(v, k):
                o = refill(6 + k, (qT_ready, kT_ready)[k], 2 * v + 2).bitcast(BF16)
                pe.wait_ge(parts_ready, 2 * v + k + 1)
                for pair in range(H // 2):
                    i = pe.transpose(o[:, pair * T:(pair + 1) * T],
                                     parts[k][v % 2][:, 2 * pair:2 * pair + 2, :].rearrange("p h d -> p (h d)"), identb[:])
                i.then_inc((qT_full, kT_full)[k], 1)

            def operands(v, g, i):
                hd = head_of(g, i)
                r = 64 * (hd % 2)
                return hd, [qkT[k][v % 2][r:r + HROWS, hd // 2, :] for k in (0, 1)]

            def scores(v, g):
                pe.wait_ge(qT_ready, 2 * v + g // 2 + 1)
                pe.wait_ge(kT_ready, 2 * v + g // 2 + 1)
                o = refill(6 + g % 2, max_ready, 4 * v + g + 1)
                for n in range(4):
                    _, (q, k) = operands(v, g, n)
                    i = mm(o[:, n * T:(n + 1) * T], q, k)
                i.then_inc(s_full, 1)

            def late_gates(l, b):
                gates(refill(GATE_BANKS[l], gate_ready, 2 * b + l), l, b).then_inc(gate_full, 1)

            def max_turn(v):
                o = refill(7, nmT_ready, v + 1).bitcast(BF16)
                pe.wait_ge(nmp_ready, v + 1)
                pe.transpose(o[:, 0:T], nmp[v % 2][:], identb[:]).then_inc(mT_full, 1)

            def scores_T(v, g):
                o = refill(2 + g % 2, prob_ready, 4 * v + g + 1)
                if g == 0:
                    pe.wait_ge(nmT_ready, v + 1)
                for n in range(4):
                    hd, (q, k) = operands(v, g, n)
                    mm(o[:, n * T:(n + 1) * T], k, q, True, False)
                    i = mm(o[:, n * T:(n + 1) * T], sel[:, hd, :], nmT[v % 2][:], False, True)
                i.then_inc(sT_full, 1)

            def pv(v, g):
                if g == 0:
                    refill(4, o_raw_ready, v + 1)
                    pe.wait_ge(v_ready, v + 1)
                pe.wait_ge(prob_ready, 4 * v + g + 1)
                for n in range(4):
                    i = mm(ps[32 * n:32 * n + 32, 4, g * T:(g + 1) * T], v_aug[v % 3][:, head_of(g, n), :], prob[g][:, n, :])
                i.then_inc(prob_used, 1)

            def o_back(v):
                o = refill(4, o_n_ready, v + 1)
                pe.wait_ge(o_raw_ready, v + 1)
                for g in range(4):
                    i = pe.transpose(o[:, g * T:(g + 1) * T], o_raw[v % 2][:, g, :], ident[:])
                i.then_inc(back_full, 1)

            def o_turn(v):
                o = refill(4, oT_ready, v + 1)
                pe.wait_ge(o_n_ready, v + 1)
                turn(o, o_n[v % 2]).then_inc(oT_full, 1)

            def proj(v):
                h, l = v % 2, v // B
                o = refill(4, att_ready, v + 1)
                pe.wait_ge(oT_ready, v + 1)
                mm(o[:, 0:C], oT_t[h][:], projw_t[l][:], True, False)
                mm(o[:, 0:C], oT_u[h][:], projw_u[l][:], False, True).then_inc(proj_full, 1)

            pe.wait_ge(late_consts, 1)
            pe.wait_ge(sel_ready, 1)
            h_turn(0)
            qkv(0)
            h_turn(1)
            for slot in range(VISITS + 4):
                v, w, u = slot, slot - 1, slot - 2
                new, old = v < VISITS, 0 <= w < VISITS
                m_fc1, m_fc2 = mlp_step(slot, 4), mlp_step(slot, 5)
                if new:
                    parts_turn(v, 0)
                    parts_turn(v, 1)
                if 0 <= u < VISITS:
                    o_turn(u)
                if v + 1 < VISITS:
                    qkv(v + 1)
                if m_fc1 is not None:
                    h2_turn(m_fc1)
                if old:
                    scores_T(w, 0)
                    scores_T(w, 1)
                if new:
                    scores(v, 0)
                    scores(v, 1)
                if 0 <= u < VISITS:
                    proj(u)
                if m_fc1 is not None:
                    fc1(m_fc1, 0)
                if m_fc2 is not None:
                    fc2(m_fc2, 0)
                if old:
                    scores_T(w, 2)
                    pv(w, 0)
                    scores_T(w, 3)
                    pv(w, 1)
                if new:
                    scores(v, 2)
                if old:
                    pv(w, 2)
                if new:
                    scores(v, 3)
                if old:
                    pv(w, 3)
                if slot < B:
                    late_gates(1, slot)
                if m_fc1 is not None:
                    fc1(m_fc1, 1)
                if m_fc2 is not None:
                    fc2(m_fc2, 1)
                if old:
                    o_back(w)
                if v + 2 < VISITS:
                    h_turn(v + 2)
                if new:
                    max_turn(v)
                if m_fc1 is not None:
                    fc1(m_fc1, 2)
                if slot < B:
                    late_gates(2, slot)

        @block.vector
        def _(dve):
            d = nc.vector
            n = [0]

            def did(ins):
                n[0] += 1
                ins.then_inc(dve_step, 1)
                return n[0]

            def need(count):
                dve.wait_ge(dve_step, count)

            dve.wait_ge(silu_e, 1)
            dve.wait_ge(early_consts, 1)
            k = did(d.tensor_scalar(e_t[:], e_t[:], 1.0, None, ALU.add))
            k = did(d.tensor_scalar(e_u[0:CT, :], e_u[0:CT, :], 1.0, None, ALU.add))
            need(k)
            k = did(d.reciprocal(e_t[:], e_t[:]))
            k = did(d.reciprocal(e_u[0:CT, :], e_u[0:CT, :]))
            need(k)
            d.tensor_tensor(s_t[:], c_t[:], e_t[:], ALU.mult)
            d.tensor_tensor(s_u[0:CT, :], c_u[0:CT, :], e_u[0:CT, :], ALU.mult).then_inc(silu_ready, 1)
            for h in range(2):
                d.memset(o_n[h][:, C:C + 1], 1.0)
                i = d.memset(nmp[h][:], 0.0)
            i.then_inc(late_consts, 1)

            dve.wait_ge(gram_full, 1)
            dve.wait_ge(early_consts, 2)
            d.tensor_copy(elim[:, :, 0:D], ps[0:32, 7, 0:2 * D].rearrange("p (q d) -> p q d", q=2)).then_inc(gram_read, 1)
            d.tensor_tensor(one_h[:], ident[:, 0:16], ident[:, 16:32], ALU.add).then_inc(gram_read, 1)
            dve.wait_ge(gram_read, 1)
            loaded(dve, "p")

            g_done = {}

            def spread(rows, out_, j):
                return d.stream_shuffle(out_, rows, [j % 32] * 32)

            upd = {}
            upd["g", 0] = upd["g", 1] = upd["t", 0] = upd["t", 1] = 0

            def gram_pivot(j):
                need(upd["g", j // 32])
                if j >= 4:
                    dve.wait_ge(root_ready, j - 3)
                spread(elim[:, j // 32, j:j + D + 1], grow[:, j % 4, j:j + D + 1], j).then_inc(grow_ready, 1)

            def top_pivot(j):
                need(upd["t", j // 32])
                return did(spread(top[:, j // 32, j:D], trow[:, j % 2, j:D], j))

            for j in range(D + 1):
                gq = [q for q in range(2) if j < 32 * q + 31] if j < D else []
                tj = j - 1
                tq = [q for q in range(2) if tj < 32 * q + 31] if tj >= 0 else []
                if j < D:
                    gram_pivot(j)
                if tj >= 0:
                    k_row = top_pivot(tj)
                if j < D:
                    dve.wait_ge(grow_ready, j + 1)
                    k_rec = did(d.reciprocal(grec[:, j:j + 1], grow[:, j % 4, j:j + 1]))
                if tj >= 0:
                    need(k_row)
                    dve.wait_ge(root_ready, tj + 1)
                    k_beta = did(d.scalar_tensor_tensor(
                        out=beta[:, tj:tj + 1].bitcast(U32), in0=trow[:, tj % 2, tj:tj + 1].bitcast(U32), scalar=0x80000000,
                        in1=root[:, tj:tj + 1].bitcast(U32), op0=ALU.bitwise_and, op1=ALU.bitwise_or))
                if gq:
                    need(k_rec)
                    k_fac = did(d.scalar_tensor_tensor(
                        out=gfac[:, j % 2, :].rearrange("p (q o) -> p q o", o=1), in0=elim[:, :, j:j + 1],
                        scalar=grec[:, j:j + 1], in1=below[:, :, j:j + 1], op0=ALU.mult, op1=ALU.mult))
                if tq:
                    need(k_beta)
                    k_den = did(d.scalar_tensor_tensor(
                        out=den[:, tj:tj + 1], in0=trow[:, tj % 2, tj:tj + 1], scalar=beta[:, tj:tj + 1],
                        in1=beta[:, tj:tj + 1], op0=ALU.add, op1=ALU.mult))
                for q in gq:
                    need(k_fac)
                    w = slice(j + 1, j + D + 1)
                    upd["g", q] = did(d.scalar_tensor_tensor(
                        out=elim[:, q, w], in0=grow[:, j % 4, w], scalar=gfac[:, j % 2, q:q + 1], in1=elim[:, q, w],
                        op0=ALU.mult, op1=ALU.add))
                if tq:
                    need(k_den)
                    did(d.reciprocal(drec[:, tj:tj + 1], den[:, tj:tj + 1]))
                    k_num = did(d.scalar_tensor_tensor(
                        out=tnum[:, tj % 2, :].rearrange("p (q o) -> p q o", o=1), in0=top[:, :, tj:tj + 1],
                        scalar=beta[:, tj:tj + 1], in1=elim[:, :, tj:tj + 1], op0=ALU.mult, op1=ALU.add))
                    need(k_num)
                    k_fac2 = did(d.scalar_tensor_tensor(
                        out=tfac[:, tj % 2, :].rearrange("p (q o) -> p q o", o=1),
                        in0=tnum[:, tj % 2, :].rearrange("p (q o) -> p q o", o=1), scalar=drec[:, tj:tj + 1],
                        in1=below[:, :, tj:tj + 1], op0=ALU.mult, op1=ALU.mult))
                    need(k_fac2)
                    for q in tq:
                        w = slice(tj + 1, D)
                        upd["t", q] = did(d.scalar_tensor_tensor(
                            out=top[:, q, w], in0=trow[:, tj % 2, w], scalar=tfac[:, tj % 2, q:q + 1], in1=top[:, q, w],
                            op0=ALU.mult, op1=ALU.add))

            need(n[0])
            k = did(d.tensor_tensor(sgn[:], beta[:], grec[:], ALU.mult))
            need(k)
            for q in range(2):
                k = did(d.tensor_tensor(sgnd[:, q, :], sgn[:], diag[:, q, :], ALU.mult))
            need(k)
            k = did(d.tensor_reduce(rscale[:], sgnd[:], AX_X, ALU.add))
            need(k)
            for q in range(2):
                i = d.tensor_scalar(linv[:, q, :], elim[:, q, D:2 * D], rscale[:, q:q + 1], None, ALU.mult)
            i.then_inc(linv_ready, 1)
            dve.wait_ge(pre_full, 1)
            d.memset(hid[64:96, FFC - 1, :, :], 1.0)

            dve.wait_ge(rot_full, 1)
            d.tensor_copy(linvT[:], ps[0:D, 6, 0:D]).then_inc(rot_read, 1)
            dve.wait_ge(rot_full, 2)
            d.tensor_copy(u_t[:], ps[:, 7, 0:D])
            d.tensor_copy(u_u[:], ps[0:CT, 7, D:2 * D])
            d.tensor_copy(uT[:], ps[0:D, 7, 2 * D:2 * D + C]).then_inc(rot_read, 1)
            for n_ in range(2):
                dve.wait_ge(rot_full, 3 + n_)
                d.tensor_copy(zT[:, 512 * n_:512 * n_ + 512], ps[0:D, 6 + n_, :]).then_inc(rot_read, 1)
            for n_ in range(2):
                dve.wait_ge(rot_full, 5 + n_)
                d.tensor_copy(yT[:, 512 * n_:512 * n_ + 512], ps[0:D, 6 + n_, :]).then_inc(rot_read, 1)
            for n_ in range(4):
                dve.wait_ge(rot_full, 7 + n_)
                xs = x[:, 2 * n_:2 * n_ + 2, :].rearrange("p b c -> p (b c)")
                d.tensor_tensor(xs, xs, ps[:, 6 + n_ % 2, 0:2 * C], ALU.add).then_inc(rot_read, 1)

            def variances(kind, visits, done):
                l = visits[0] // B
                hs = slice(visits[0] % 2, visits[-1] % 2 + 1)
                for v in visits:
                    k = did(d.bn_stats(st6[:, kind, v % 2, :], x[:, v % B, :]))
                need(k)
                for v in visits:
                    k = did(d.bn_aggr(st2[:, kind, v % 2, :], st6[:, kind, v % 2, :]))
                need(k)
                if l < 2:
                    d.tensor_scalar(vare[:, kind, hs], st2[:, kind, hs, 1], LN_EPS[l], None, ALU.add).then_inc(done, 1)
                    return
                k = did(d.tensor_tensor(msq[:, kind, hs], st2[:, kind, hs, 0], st2[:, kind, hs, 0], ALU.mult))
                need(k)
                k = did(d.tensor_tensor(msq[:, kind, hs], msq[:, kind, hs], st2[:, kind, hs, 1], ALU.add))
                need(k)
                d.tensor_scalar(vare[:, kind, hs], msq[:, kind, hs], 1e-24 / C, None, ALU.max).then_inc(done, 1)

            def normalise(kind, v, done):
                h = v % 2
                if v // B < 2:
                    i = d.tensor_scalar(ln[kind][h][:, 0:C], x[:, v % B, :], st2[:, kind, h, 0:1], rstd[:, kind, h:h + 1],
                                        ALU.subtract, ALU.mult)
                else:
                    i = d.tensor_scalar(ln[kind][h][:, 0:C], x[:, v % B, :], rstd[:, kind, h:h + 1], None, ALU.mult)
                i.then_inc(done, 1)

            def modulated(v, kind):
                h, l, b = v % 2, v // B, v % B
                out_, at = (hT_t[h][:], 0) if kind == 0 else (mT_t[:, h, :], h * T)
                return d.tensor_scalar(out_, ps[:, 0, at:at + T], mod_t[:, l, 2 * kind + 1, b:b + 1],
                                       mod_t[:, l, 2 * kind, b:b + 1], ALU.mult, ALU.add)

            def h_out(v):
                dve.wait_ge(hT_full, v + 1)
                if v >= 2:
                    dve.wait_ge(qkv_full, v - 1)
                modulated(v, 0)
                d.tensor_copy(hT_u[v % 2][:], ps[:, 0, :].bitcast(BF16)[0:KS, 2 * T:3 * T]).then_inc(hT_ready, 1)

            def h2_out(m):
                dve.wait_ge(h2T_full, m + 1)
                if m >= 1:
                    dve.wait_ge(fc1_full, 3 * m)
                d.tensor_copy(mT_u[:].rearrange("p h t -> p (h t)"),
                              ps[:, 0, :].bitcast(BF16)[0:KS, 4 * T:6 * T]).then_inc(h2T_ready, 1)
                modulated(2 * m, 1)
                modulated(2 * m + 1, 1).then_inc(h2T_ready, 1)

            def of_slots(k, h, slots):
                return parts[k][h][:, :, 0:HROWS].rearrange("p h (s d) -> p h s d", d=HD)[:, :, slots, :]

            def unit_norms(v):
                h = v % 2
                dve.wait_ge(squared, v - 2 * B + 1)
                need(did(d.tensor_reduce(ssq[:].rearrange("p k h -> p (k h)"), sq[:], AX_X, ALU.add)))
                need(did(d.tensor_scalar(ssq[:], ssq[:], 1e-24, None, ALU.max)))
                need(did(d.tensor_scalar(ny[:].bitcast(I32), ssq[:].bitcast(I32), -0.5, RSQRT_SEED, ALU.mult, ALU.add)))
                need(did(d.tensor_tensor(my[:], ny[:], ny[:], ALU.mult)))
                need(did(d.tensor_tensor(my[:], my[:], ssq[:], ALU.mult)))
                need(did(d.scalar_tensor_tensor(out=my[:], in0=my[:], scalar=-10.0 / 3.0, in1=my[:], op0=ALU.add, op1=ALU.mult)))
                need(did(d.scalar_tensor_tensor(out=ny[:], in0=my[:], scalar=5.0, in1=ny[:], op0=ALU.add, op1=ALU.mult)))
                k = did(d.scalar_tensor_tensor(out=my[:], in0=ny[:], scalar=-0.5 * (3.0 / 8.0) ** 2, in1=ny[:],
                                               op0=ALU.mult, op1=ALU.mult))
                for kk in range(2):
                    k2 = did(d.tensor_scalar(hy[:, kk, :], ny[:, kk, :], 3.0 / 8.0 * float(HD) ** 0.5, qkg[:, kk:kk + 1],
                                             ALU.mult, ALU.mult))
                need(k)
                need(did(d.tensor_tensor(my[:], my[:], ssq[:], ALU.mult)))
                need(k2)
                need(did(d.scalar_tensor_tensor(out=ny[:], in0=my[:], scalar=1.5, in1=hy[:], op0=ALU.add, op1=ALU.mult)))
                if v - 2 * B >= 2:
                    dve.wait_ge(first_parts, 2 * (v - 2) + 2)
                fac = ny[:].rearrange("p k (h o) -> p (k h) o", o=1).broadcast_to([T, 2 * H, HD])
                src = ps[:, 1, 0:2 * C].rearrange("p (k d) -> p k d", d=HD)
                d.tensor_tensor(qk[h][:].rearrange("p k h d -> p (k h) d"), src, fac, ALU.mult).then_inc(qk_normed, 1)
                dve.wait_ge(qk_normed, v - 2 * B + 1)

            def split(v):
                h, l = v % 2, v // B
                dve.wait_ge(first_parts, 2 * v + 2)
                firsts, seconds = (slice(1, 2), slice(2, 3)), (slice(0, 1), slice(0, 1))
                for k in range(2):
                    src = qk[h][:, k, :, :] if l == 2 else \
                        ps[:, 1, k * C:(k + 1) * C].rearrange("p (h d) -> p h d", d=HD)
                    i = d.tensor_tensor(res[h][:, k, :, :], src, of_slots(k, h, firsts[k])[:, :, 0, :], ALU.subtract)
                    if k == 0:
                        did(i)
                    else:
                        i.then_inc(qkv_read, 1)
                dve.wait_ge(qkv_read, v + 1)
                for k, slots in ((0, Q2), (1, K2)):
                    src = res[h][:, k, :, :].rearrange("p h (o d) -> p h o d", o=1).broadcast_to([T, H, 2, HD])
                    c = did(d.tensor_copy(of_slots(k, h, slots), src))
                need(c)
                for k, slots in ((0, Q3), (1, K3)):
                    d.tensor_tensor(of_slots(k, h, slots)[:, :, 0, :], res[h][:, k, :, :], of_slots(k, h, seconds[k])[:, :, 0, :],
                                    ALU.subtract).then_inc(parts_ready, 1)

            def q_out(v):
                dve.wait_ge(qT_full, v + 1)
                if v >= 2:
                    dve.wait_ge(sT_full, 4 * (v - 2) + 4)
                for n in (0, 4):
                    d.tensor_copy(qkT[0][v % 2][:, n:n + 4, :].rearrange("p k t -> p (k t)"),
                                  ps[:, 6, :].bitcast(BF16)[:, n * T:(n + 4) * T]).then_inc(qT_ready, 1)

            def maxima(v, g):
                dve.wait_ge(s_full, 4 * v + g + 1)
                first = head_of(g, 0)
                d.tensor_reduce(nmax[:, v % 2, first:first + 7:2], ps[:, 6 + g % 2, :].rearrange("p (i t) -> p i t", i=4),
                                AX_X, ALU.max, negate=True).then_inc(max_ready, 1)

            def max_parts(v):
                h = v % 2
                dve.wait_ge(max_ready, 4 * v + 4)
                if v >= 2:
                    dve.wait_ge(mT_full, v - 1)
                need(did(d.tensor_copy(nmp[h][:, 0:16], nmax[:, h, :])))
                d.tensor_tensor(nmp[h][:, 16:32], nmax[:, h, :], nmp[h][:, 0:16], ALU.subtract).then_inc(nmp_ready, 1)

            def max_out(v):
                dve.wait_ge(mT_full, v + 1)
                if v >= 2:
                    dve.wait_ge(sT_full, 4 * (v - 2) + 4)
                d.tensor_copy(nmT[v % 2][:], ps[:, 7, :].bitcast(BF16)[:, 0:T]).then_inc(nmT_ready, 1)

            def attended(v):
                h = v % 2
                dve.wait_ge(back_full, v + 1)
                src = ps[:, 4, :].rearrange("p (h r) -> p h r", r=32)
                k = did(d.reciprocal(orec[h][:].rearrange("p (h o) -> p h o", o=1), src[:, :, HD:HD + 1]))
                need(k)
                if v >= 2:
                    dve.wait_ge(oT_full, v - 1)
                d.tensor_tensor(o_n[h][:, 0:C].rearrange("p (h d) -> p h d", d=HD), src[:, :, 0:HD],
                                orec[h][:].rearrange("p (h o) -> p h o", o=1).broadcast_to([T, H, HD]),
                                ALU.mult).then_inc(o_n_ready, 1)

            def gated(v):
                h, l, b = v % 2, v // B, v % B
                dve.wait_ge(proj_full, v + 1)
                if l > 0:
                    dve.wait_ge(gate_ready, 2 * B)
                if v >= 2:
                    dve.wait_ge(att_added, v - 1)
                d.tensor_tensor(attd[h], ps[:, 4, 0:C], gmod[:, l, b, 0:C], ALU.mult).then_inc(att_ready, 1)

            def mlp_out(m):
                l, b = m // (B // 2), 2 * m % B
                dve.wait_ge(fc2_full, m + 1)
                if m >= 1:
                    dve.wait_ge(mlp_added, 2 * m)
                d.tensor_tensor(mlpd, ps[:, 5, 0:2 * C].rearrange("p (h c) -> p h c", h=2), gmod[:, l, b:b + 2, C:2 * C],
                                ALU.mult).then_inc(mlp_ready, 1)
                dve.wait_ge(mlp_ready, m + 1)
                for h in range(2):
                    d.tensor_tensor(x[:, b + h, :], x[:, b + h, :], mlpd[:, h, :], ALU.add).then_inc(mlp_added, 1)

            def next_input(v):
                if v >= B:
                    dve.wait_ge(mlp_added, 2 * ((v - B) // 2) + 2)
                variances(0, [v], var1)

            def next_normal(v):
                dve.wait_ge(rstd1, v + 1)
                if v >= 2:
                    dve.wait_ge(hT_full, v - 1)
                normalise(0, v, ln_ready)

            dve.wait_ge(rot_read, 10)
            dve.wait_ge(mods_ready, 1)
            dve.wait_ge(slots_zeroed, 1)
            dve.wait_ge(pre_read, pre_reads[-1])
            for v in (0, 1):
                next_input(v)
                next_normal(v)
                h_out(v)
            split(0)
            for slot in range(VISITS + 4):
                v, w = slot, slot - 1
                new, old = v < VISITS, 0 <= w < VISITS
                m_norm, m_fc1, m_out = mlp_step(slot, 3), mlp_step(slot, 4), mlp_step(slot, 5)
                if new:
                    q_out(v)
                if m_fc1 is not None:
                    h2_out(m_fc1)
                if v + 1 < VISITS and (v + 1) // B == 2:
                    unit_norms(v + 1)
                if v + 2 < VISITS:
                    next_input(v + 2)
                if 0 <= slot - 2 < VISITS:
                    gated(slot - 2)
                if new:
                    maxima(v, 0)
                if m_norm is not None:
                    dve.wait_ge(att_added, 2 * m_norm + 2)
                    variances(1, [2 * m_norm, 2 * m_norm + 1], var2)
                if new:
                    maxima(v, 1)
                if v + 2 < VISITS:
                    next_normal(v + 2)
                if v + 1 < VISITS:
                    split(v + 1)
                if m_norm is not None:
                    dve.wait_ge(rstd2, m_norm + 1)
                    if m_norm >= 1:
                        dve.wait_ge(h2T_full, m_norm)
                    for u in (2 * m_norm, 2 * m_norm + 1):
                        normalise(1, u, ln2_ready)
                if new:
                    maxima(v, 2)
                    maxima(v, 3)
                    max_parts(v)
                if v + 2 < VISITS:
                    h_out(v + 2)
                if new:
                    max_out(v)
                if old:
                    attended(w)
                if m_out is not None:
                    mlp_out(m_out)


def kernel(**inputs):
    import concourse.bacc as bacc
    from concourse.bass_utils import run_bass_kernel_spmd

    f = {k: np.asarray(v) for k, v in inputs.items()}

    def rows(w, b=None):
        return np.concatenate([w, np.zeros((1, w.shape[1]), np.float32) if b is None else b[None, :]], axis=0)

    iu, ju = np.triu_indices(D, k=1)
    skw = np.zeros((C + 1, D, D), np.float32)
    skw[0:C, ju, iu] = f["L0_cond_W"].T
    skw[C, ju, iu] = f["L0_cond_b"]
    skw = skw.reshape(C + 1, 2, D // 2, D).transpose(0, 2, 1, 3)
    order = np.concatenate([np.arange(HD) + HD * head_of(g, i) for g in range(4) for i in range(4)])
    p = f["L0_cond_P"]
    vec = lambda v: np.broadcast_to(v, (C,))
    aff = np.stack([f["L2_cond_ln1_w"], f["L2_cond_ln1_b"], f["L2_cond_ln2_w"], f["L2_cond_ln2_b"],
                    vec(f["L3_cond_g1"]), vec(f["L3_cond_g2"])], axis=1)

    def modulation(w, b):
        w = rows(w, b).reshape(C + 1, 6, C)
        parts = [w[:, [2, 5], :], w[:, [0, 1, 3, 4], 128:C], w[:, [0, 1, 3, 4], 0:128]]
        return np.concatenate([p_.reshape(C + 1, -1) for p_ in parts], axis=1)

    qkv = [rows(f["L1_cond_W_qkv"], f["L1_cond_b_qkv"]),
           rows(np.concatenate([f["L2_cond_wq"], f["L2_cond_wk"], f["L2_cond_wv"]], axis=1)),
           rows(f["L3_cond_qkv_w"].T, f["L3_cond_qkv_b"])]
    fc1 = [rows(f["L1_cond_W_fc1"], f["L1_cond_b_fc1"]), rows(f["L2_cond_fc1_w"], f["L2_cond_fc1_b"]),
           rows(f["L3_cond_fc1_w"].T, f["L3_cond_fc1_b"])]
    a = {
        "x": f["x"].transpose(1, 0, 2),
        "xT": f["x"].transpose(2, 0, 1).reshape(C, B * T),
        "cond": f["cond_1152"].T,
        "p": p, "pT": p.T,
        "ptop": p.T[:, 0:D].reshape(2, 32, D).transpose(1, 0, 2),
        "skw": skw.reshape(C + 1, D * D),
        "aff": aff[0:128, :],
        "aff_u": np.broadcast_to(aff[128:C, [0, 1, 4, 2, 3, 5]].T.reshape(1, 2, 3, CT), (T, 2, 3, CT)),
        "tmask": np.repeat(np.array([[-1, 0], [-1, 0], [0, 0], [0, 0], [0, 0], [-1, -1]], np.float32), KT, axis=0),
        "qkg": np.stack([np.broadcast_to(f["L3_cond_qg"], (T,)), np.broadcast_to(f["L3_cond_kg"], (T,))], axis=1),
        "ada0": modulation(f["L1_cond_W_ada"], f["L1_cond_b_ada"]),
        "ada1": modulation(f["L2_cond_ada_w"], f["L2_cond_ada_b"]),
        "ada2": modulation(f["L3_cond_ada_w"].T, f["L3_cond_ada_b"]),
        "proj0": rows(f["L1_cond_W_proj"][order], f["L1_cond_b_proj"]),
        "proj1": rows(f["L2_cond_wo"][order], f["L2_cond_wo_b"]),
        "proj2": rows(f["L3_cond_proj_w"].T[order], f["L3_cond_proj_b"]),
        "fc20": rows(f["L1_cond_W_fc2"], f["L1_cond_b_fc2"]),
        "fc21": rows(f["L2_cond_fc2_w"], f["L2_cond_fc2_b"]),
        "fc22": rows(f["L3_cond_fc2_w"].T, f["L3_cond_fc2_b"]),
    }
    for l in range(LAYERS):
        a[f"qkv{l}"], a[f"fc1{l}"] = qkv[l][0:128], fc1[l][0:128]
        a[f"tail{l}"] = np.tile(np.concatenate([qkv[l][128:], fc1[l][128:]], axis=1), (SLOTS, 1))
    nc = bacc.Bacc("TRN2", target_bir_lowering=False, num_devices=1)
    arrays, t = {}, {}
    for name, v in a.items():
        v = np.ascontiguousarray(v)
        arrays["in_" + name] = v
        t[name] = nc.dram_tensor("in_" + name, v.shape, F32, kind="ExternalInput").ap()
    out = nc.dram_tensor("out_x", (T, B, C), F32, kind="ExternalOutput").ap()
    program(nc, t, out)
    r = run_bass_kernel_spmd(nc, [arrays], core_ids=[0])
    return r.results[0]["out_x"].transpose(1, 0, 2)
```

```python
from contextlib import ExitStack

import numpy as np

import concourse.bass as bass
from concourse import mybir

F32 = mybir.dt.float32
BF16 = mybir.dt.bfloat16
U32 = mybir.dt.uint32
I32 = mybir.dt.int32
ALU = mybir.AluOpType
ACT = mybir.ActivationFunctionType
AX_X = mybir.AxisListType.X

B, T, C = 8, 128, 144
D = 64
CT = C - 128
KT = CT + 1
H, HD = 16, 9
FF = 4 * C
FFC = 5
LAYERS = 3
SLOTS = 6
HROWS = SLOTS * HD
Q1, Q2, Q3 = slice(1, 6, 2), slice(0, 3, 2), slice(4, 5)
K1, K2, K3 = slice(2, 5), slice(0, 2), slice(5, 6)
KS = SLOTS * KT
GM = 2 * C + 4 * CT
WSPLIT = (3 * C + FF) // 4
SCALE = float(HD) ** -0.5
SQUARINGS = 7
STEPS = LAYERS * B // 2
LN_EPS = [1e-6, 1e-5, 0.0]
RSQRT_SEED = 1597463007.0
FACT = [1.0]
for _n in range(1, 16):
    FACT.append(FACT[-1] * _n)
COS = [(-1.0) ** k / FACT[2 * k] for k in range(4)]
SIN = [(-1.0) ** k / FACT[2 * k + 1] for k in range(4)]
VISITS = LAYERS * B
EYES = sorted(set(COS) | set(SIN) | {-1.0})


def eye_of(c):
    return EYES.index(c)


def plan_rotation():
    chain = [("upper", 0), ("skew", 0), ("n2", 0), ("n4", 0)]
    chain += [("poly", (k, f)) for k in (1, 0) for f in (0, 1)]
    chain += [("expm", 0), ("expm", 1)]
    chain += [("square", (k, g)) for k in range(1, SQUARINGS) for g in (0, 1)] + [("square", (SQUARINGS, 0))]
    other = [("mods", 0)] + [("gate", l) for l in range(LAYERS)] + [("xp", 0), ("xp", 1)]
    fills = chain[:2]
    for k in range(max(len(chain) - 2, len(other))):
        fills += chain[2 + k:3 + k] + other[k:k + 1]
    return fills


def head_of(g, i):
    return 8 * (g // 2) + 2 * i + g % 2


def program(nc, t, out, spread_mods):
    ctx = ExitStack()
    with ctx:
        def sb(name, shape, dt=F32):
            return ctx.enter_context(nc.sbuf_tensor(name, shape, dt))

        def sem(name):
            return ctx.enter_context(nc.semaphore(name))

        x = sb("x", [T, B, C])
        x_t, x_u = sb("x_t", [128, B * T]), sb("x_u", [CT, B * T])
        c_t, c_u = sb("c_t", [128, B]), sb("c_u", [KT, B])
        e_t, e_u = sb("e_t", [128, B]), sb("e_u", [KT, B])
        s_t, s_u = sb("s_t", [128, B]), sb("s_u", [KT, B])
        p_t, p_u, pT = sb("p_t", [128, D]), sb("p_u", [CT, D]), sb("pT", [D, C])
        skw_t, skw_r = sb("skw_t", [128, D * D]), sb("skw_r", [128, D * D])
        skw_u = skw_r[0:KT, :]
        qkvw_t = [sb(f"qkvw_t{l}", [128, 3 * C]) for l in range(LAYERS)]
        projw_t = [sb(f"projw_t{l}", [128, C]) for l in range(LAYERS)]
        projw_u = [sb(f"projw_u{l}", [KT, C]) for l in range(LAYERS)]
        fc1w_t = [sb(f"fc1w_t{l}", [128, FF]) for l in range(LAYERS)]
        tails = sb("tails", [KS, LAYERS, 3 * C + FF])
        tailw = sb("tailw", [KS, LAYERS, 3 * C + FF], BF16)
        tmask = sb("tmask", [KS, 2])
        fc2w = [sb(f"fc2w{l}", [128, FFC, C]) for l in range(LAYERS)]
        adaw_t = [sb(f"adaw_t{l}", [128, 6 * C]) for l in range(LAYERS)]
        adaw_u = [sb(f"adaw_u{l}", [KT, 6 * C]) for l in range(LAYERS)]
        aff_t = sb("aff_t", [128, 6])
        aff_u = sb("aff_u", [B, 2, 3, CT])
        qkg = sb("qkg", [T, 2])

        ident = sb("ident", [128, 128])
        identb = sb("identb", [128, 128], BF16)
        eyes = sb("eyes", [D, len(EYES), D])
        irep = sb("irep", [D, B, D])
        below = sb("below", [32, 2, D])
        diag = sb("diag", [32, 2, D])
        table_out = sb("table_out", [32, 1])
        half, nhalf = sb("half", [32, 1]), sb("nhalf", [T, 2])
        one_h = sb("one_h", [128, H])
        sel = sb("sel", [128, H, 128], BF16)

        elim = sb("elim", [32, 2, 2 * D])
        top = sb("top", [32, 2, D])
        grow = sb("grow", [32, 4, 2 * D])
        trow = sb("trow", [32, 2, D])
        grec, gfac = sb("grec", [32, D]), sb("gfac", [32, 2, 2])
        root = sb("root", [32, D])
        beta = sb("beta", [32, D])
        den, drec = sb("den", [32, D]), sb("drec", [32, D])
        tnum, tfac = sb("tnum", [32, 2, 2]), sb("tfac", [32, 2, 2])
        sgn = sb("sgn", [32, D])
        sgnd = sb("sgnd", [32, 2, D])
        rscale = sb("rscale", [32, 2])
        linv = sb("linv", [32, 2, D])
        linvT = sb("linvT", [D, D])
        uT = sb("uT", [D, C])
        xpT = sb("xpT", [D, B * T])
        rmi = skw_r[0:32, 0:2 * B * D].rearrange("p (q n) -> p q n", q=2)
        lrmi = skw_r[0:D, 2 * B * D:3 * B * D]
        yT = skw_t[0:D, D * D - B * T:D * D]
        upper = sb("upper", [128, B, D // 2])
        nident = sb("nident", [128, D])
        bmat = sb("bmat", [D, B, D])
        brief = sb("brief", [128, 6, B * D])
        n2, n4 = [brief[0:D, k, :].rearrange("p (b d) -> p b d", b=B) for k in range(2)]
        poly = [[brief[0:D, 2 + 2 * k + f, :].rearrange("p (b d) -> p b d", b=B) for f in range(2)] for k in range(2)]
        nodd = sb("nodd", [D, B, D])
        ef = [brief[0:D, 4:6, :].rearrange("p f (b d) -> p f b d", b=B), sb("ef1", [D, 2, B, D])[:]]

        mod_t = sb("mod_t", [128, LAYERS, 4, B])
        mod_w = sb("mod_w", [128, B])
        gmod_b = sb("gmod_b", [B, LAYERS, GM])
        gmod = sb("gmod", [T, LAYERS, B, GM])
        mod_v = sb("mod_v", [B, 2, CT])
        tprod = gmod[0:KS, 1:3, :, :].rearrange("p l b g -> p (l b g)")[:, 0:LAYERS * (3 * C + FF)].rearrange(
            "p (l n) -> p l n", l=LAYERS)

        st6 = sb("st6", [T, 2, 2, 6])
        st2 = sb("st2", [T, 2, 2, 2])
        vare, rstd = sb("vare", [T, 2, 2]), sb("rstd", [T, 2, 2])
        msq = sb("msq", [T, 2, 2])
        ln = [[sb(f"ln{k}{h}", [T, C]) for h in range(2)] for k in range(2)]
        hT_t = [sb(f"hT_t{h}", [128, T]) for h in range(2)]
        hT_u = [sb(f"hT_u{h}", [KS, T], BF16) for h in range(2)]
        mT_t, mT_u = sb("mT_t", [128, 2, T]), sb("mT_u", [KS, 2, T], BF16)
        tail = [[sb(f"tail{k}{h}", [T, CT]) for h in range(2)] for k in range(2)]
        tailp = [[sb(f"tailp{k}{h}", [T, SLOTS, KT], BF16) for h in range(2)] for k in range(2)]
        qk = [sb(f"qk{h}", [T, 2, H, HD]) for h in range(2)]
        sq = sb("sq", [T, 2 * H, HD])
        ssq, hy, ny, my = sb("ssq", [T, 2, H]), sb("hy", [T, 2, H]), sb("ny", [T, 2, H]), sb("my", [T, 2, H])
        res = [sb(f"res{h}", [T, 2, H, HD]) for h in range(2)]
        parts = [[brief[:, 2 * k + h, :].bitcast(BF16).rearrange("p (h d) -> p h d", h=H) for h in range(2)] for k in range(2)]
        n_qkT, n_hid = H // 4 * T, FFC * 2 * T
        qkT = [[skw_r[:, (2 * k + h) * n_qkT:(2 * k + h + 1) * n_qkT].bitcast(BF16)
                .rearrange("p (n t) -> p n t", t=T) for h in range(2)] for k in range(2)]
        hid = skw_r[:, 4 * n_qkT:4 * n_qkT + n_hid].rearrange("p (c h t) -> p c h t", c=FFC, h=2)
        prob = [skw_t[:, g * 4 * T:(g + 1) * 4 * T].rearrange("p (i t) -> p i t", t=T) for g in range(4)]
        o_raw = [skw_t[:, (4 + h) * 4 * T:(5 + h) * 4 * T].rearrange("p (g t) -> p g t", t=T) for h in range(2)]
        v_aug = [tile.rearrange("p (h r) -> p h r", h=H)
                 for tile in (brief[:, 4, :], brief[:, 5, :], sb("v_aug2", [T, H * 32])[:])]
        nmax = sb("nmax", [T, 2, H])
        nmp = [sb(f"nmp{h}", [T, 128], BF16) for h in range(2)]
        nmT = [sb(f"nmT{h}", [128, T], BF16) for h in range(2)]
        orec = [sb(f"orec{h}", [T, H]) for h in range(2)]
        o_n = [sb(f"o_n{h}", [T, C + 1]) for h in range(2)]
        oT_t = [sb(f"oT_t{h}", [128, T]) for h in range(2)]
        oT_u = [sb(f"oT_u{h}", [KT, T]) for h in range(2)]
        n_far = 4 * n_qkT + n_hid
        attd = [skw_r[:, n_far + h * C:n_far + (h + 1) * C] for h in range(2)]
        mlpd = skw_r[:, n_far + 2 * C:n_far + 4 * C].rearrange("p (h c) -> p h c", h=2)

        ps = ctx.enter_context(nc.psum_tensor("ps", [128, 8, 512], F32))

        ld = {n: sem("ld_" + n) for n in ("cond", "p", "skw", "x", "misc", "ada0", "ada1", "ada2",
                                          "blk0", "blk1", "blk2", "tail0", "tail1", "tail2", "tmask", "gmod0", "gmod1", "gmod2")}
        loads = {"cond": 2, "p": 4, "skw": 2, "x": 3, "misc": 3, "ada0": 2, "ada1": 2, "ada2": 2,
                 "blk0": 6, "blk1": 6, "blk2": 6, "tail0": 1, "tail1": 1, "tail2": 1, "tmask": 1, "gmod0": 1, "gmod1": 1, "gmod2": 1}
        pool_step = sem("pool_step")
        dve_step = sem("dve_step")
        early_consts = sem("early_consts")
        late_consts = sem("late_consts")
        slots_zeroed = sem("slots_zeroed")
        sel_ready = sem("sel_ready")
        silu_e, silu_ready = sem("silu_e"), sem("silu_ready")
        gram_full, gram_read = sem("gram_full"), sem("gram_read")
        grow_ready = sem("grow_ready")
        root_ready = sem("root_ready")
        pre_full, pre_read = sem("pre_full"), sem("pre_read")
        rot_full, rot_read = sem("rot_full"), sem("rot_read")
        linv_ready = sem("linv_ready")
        mods_ready = sem("mods_ready")
        gmod_ready, gmod_stored = sem("gmod_ready"), sem("gmod_stored")
        tail_cast, tail_left, tailw_ready = sem("tail_cast"), sem("tail_left"), sem("tailw_ready")
        act_step = sem("act_step")
        tailp_ready, tail2p_ready = sem("tailp_ready"), sem("tail2p_ready")
        table_used = sem("table_used")
        var1, rstd1 = sem("var1"), sem("rstd1")
        var2, rstd2 = sem("var2"), sem("rstd2")
        ln_ready, ln2_ready = sem("ln_ready"), sem("ln2_ready")
        hT_full, hT_ready = sem("hT_full"), sem("hT_ready")
        h2T_full, h2T_ready = sem("h2T_full"), sem("h2T_ready")
        qkv_full, qkv_read = sem("qkv_full"), sem("qkv_read")
        v_ready, squared, qk_normed = sem("v_ready"), sem("squared"), sem("qk_normed")
        first_parts, parts_ready = sem("first_parts"), sem("parts_ready")
        qT_full, qT_ready = sem("qT_full"), sem("qT_ready")
        kT_full, kT_ready = sem("kT_full"), sem("kT_ready")
        s_full, max_ready = sem("s_full"), sem("max_ready")
        nmp_ready, mT_full, nmT_ready = sem("nmp_ready"), sem("mT_full"), sem("nmT_ready")
        sT_full, prob_ready, prob_used = sem("sT_full"), sem("prob_ready"), sem("prob_used")
        o_raw_ready, back_full, o_n_ready = sem("o_raw_ready"), sem("back_full"), sem("o_n_ready")
        oT_full, oT_ready = sem("oT_full"), sem("oT_ready")
        proj_full, att_ready, att_added = sem("proj_full"), sem("att_ready"), sem("att_added")
        fc1_full, hid_ready = sem("fc1_full"), sem("hid_ready")
        fc2_full, mlp_ready, mlp_added = sem("fc2_full"), sem("mlp_ready"), sem("mlp_added")
        stored = sem("stored")

        pre = plan_rotation()
        pre_at = {fill: k for k, fill in enumerate(pre)}
        reads, pre_reads = 0, []
        for fill in pre:
            reads += 2 if fill == ("poly", (0, 1)) else 1
            pre_reads.append(reads)

        def was_read(name, arg):
            return pre_reads[pre_at[name, arg]]

        block = ctx.enter_context(nc.Block())

        @block.sync
        def _(sp):
            def load(dst, src, s):
                sp.dma_start(dst, src).then_inc(ld[s], 16)

            load(p_t[:], t["p"][0:128, :], "p")
            load(p_u[:], t["p"][128:C, :], "p")
            load(c_t[:], t["cond"][0:128, :], "cond")
            load(c_u[0:CT, :], t["cond"][128:C, :], "cond")
            load(top[:], t["ptop"], "p")
            load(pT[:], t["pT"], "p")
            load(skw_t[:], t["skw"][0:128, :], "skw")
            load(skw_u, t["skw"][128:C + 1, :], "skw")
            load(tmask[:], t["tmask"], "tmask")
            for l in range(LAYERS):
                load(tails[:, l, :], t[f"tail{l}"], f"tail{l}")
            for l in range(LAYERS):
                load(adaw_t[l][:], t[f"ada{l}"][0:128, :], f"ada{l}")
                load(adaw_u[l][:], t[f"ada{l}"][128:C + 1, :], f"ada{l}")
            load(x[:], t["x"], "x")
            load(x_t[:], t["xT"][0:128, :], "x")
            load(x_u[:], t["xT"][128:C, :], "x")
            load(aff_t[:], t["aff"], "misc")
            load(aff_u[:], t["aff_u"], "misc")
            load(qkg[:], t["qkg"], "misc")
            for l in range(LAYERS):
                load(qkvw_t[l][:], t[f"qkv{l}"][0:128, :], f"blk{l}")
                load(projw_t[l][:], t[f"proj{l}"][0:128, :], f"blk{l}")
                load(projw_u[l][:], t[f"proj{l}"][128:C + 1, :], f"blk{l}")
                load(fc1w_t[l][:], t[f"fc1{l}"][0:128, :], f"blk{l}")
                load(fc2w[l][:, 0:4, :], t[f"fc2{l}"][0:512, :].rearrange("(c p) n -> p c n", p=128), f"blk{l}")
                load(fc2w[l][0:65, 4, :], t[f"fc2{l}"][512:FF + 1, :], f"blk{l}")
            sp.wait_ge(gmod_ready, LAYERS)
            sp.dma_start(spread_mods, gmod_b[:]).then_inc(gmod_stored, 16)
            sp.wait_ge(gmod_stored, 16)
            for l in range(LAYERS):
                if l == 1:
                    sp.wait_ge(tail_left, 2 * LAYERS)
                load(gmod[:, l, :, :], spread_mods[:, l, :].partition_broadcast(T), f"gmod{l}")
            for pair in range(B // 2):
                sp.wait_ge(mlp_added, 2 * (STEPS - B // 2 + pair) + 2)
                sp.dma_start(out[:, 2 * pair:2 * pair + 2, :], x[:, 2 * pair:2 * pair + 2, :]).then_inc(stored, 16)
            sp.wait_ge(stored, 16 * (B // 2))

        FC1_BANKS = (5, 0, 5)

        def mlp_step(slot, lag):
            m = (slot - lag) // 2
            return m if slot >= lag and (slot - lag) % 2 == 0 and m < STEPS else None

        def loaded(eng, s):
            eng.wait_ge(ld[s], 16 * loads[s])

        @block.gpsimd
        def _(pool):
            g = nc.gpsimd
            n = [0]

            def step(ins):
                n[0] += 1
                ins.then_inc(pool_step, 1)
                pool.wait_ge(pool_step, n[0])

            def filled(tile, fill, base=0, compare=ALU.not_equal):
                step(g.memset(tile, 0.0))
                return g.affine_select(out=tile, in_=tile, compare_op=compare, fill=fill, base=-base,
                                       pattern=[[1, tile.shape[1]]], channel_multiplier=-1)

            g.memset(s_u[:], 1.0).then_inc(early_consts, 1)
            g.memset(half[:], 0.5)
            g.memset(nhalf[:], -0.5)
            for q in range(2):
                step(filled(elim[:, q, D:2 * D], 1.0, 32 * q))
                step(filled(diag[:, q, :], -1.0, 32 * q))
                step(filled(below[:, q, :], -1.0, 32 * q, ALU.is_ge))
                step(filled(nident[64 * q:64 * q + 64, :], -1.0))
            filled(ident[:], 1.0).then_inc(early_consts, 1)
            pool.wait_ge(early_consts, 2)
            for k, c in enumerate(EYES):
                g.tensor_scalar(eyes[:, k, :], ident[0:D, 0:D], c, None, ALU.mult)
            for b in range(B):
                step(g.tensor_copy(irep[:, b, :], ident[0:D, 0:D]))
            g.tensor_copy(identb[:], ident[:]).then_inc(early_consts, 1)

            def weight_left(k, l, c):
                pool.wait_ge(tail_cast, LAYERS * k + l + 1)
                w = tails[:, l, c * WSPLIT:(c + 1) * WSPLIT]
                i = g.tensor_tensor(w, w, tprod[:, l, c * WSPLIT:(c + 1) * WSPLIT], ALU.add)
                if c == 3:
                    i.then_inc(tail_left, 1)

            def tail_mods(l):
                pool.wait_ge(pre_read, was_read("gate", l))
                loaded(pool, "misc")
                m = gmod_b[:, l, 2 * C:GM].rearrange("p (k s c) -> p k s c", k=2, s=2)
                mul, add = m[:, :, 1, :], m[:, :, 0, :]
                i = g.tensor_scalar(mul, mul, 1.0, None, ALU.add)
                if l == 1:
                    step(i)
                    step(g.tensor_tensor(mod_v[:], mul, aff_u[:, :, 1, :], ALU.mult))
                    step(g.tensor_tensor(add, add, mod_v[:], ALU.add))
                    i = g.tensor_tensor(mul, mul, aff_u[:, :, 0, :], ALU.mult)
                if l == 2:
                    step(i)
                    i = g.tensor_tensor(mul, mul, aff_u[:, :, 2, :], ALU.mult)
                i.then_inc(gmod_ready, 1)

            for j in range(D):
                pool.wait_ge(grow_ready, j + 1)
                g.tensor_tensor(root[:, j:j + 1], grow[:, j % 4, j:j + 1], half[:], ALU.pow).then_inc(root_ready, 1)
                if 10 <= j < 10 + 4 * LAYERS:
                    weight_left(0, (j - 10) // 4, (j - 10) % 4)
                elif 38 <= j < 38 + 8 * LAYERS and j % 2 == 0:
                    weight_left(1, (j - 38) // 8, (j - 38) // 2 % 4)
                elif j in (51, 53, 55):
                    tail_mods((j - 51) // 2)

            pool.wait_ge(pre_read, pre_reads[-1])
            for h in range(2):
                for k in range(2):
                    g.memset(parts[k][h][:, :, HROWS:64], 0.0)
            for h in range(3):
                g.memset(v_aug[h][:, :, HD:HD + 1], 1.0)
                i = g.memset(v_aug[h][:, :, HD + 1:32], 0.0)
            i.then_inc(slots_zeroed, 1)
            loaded(pool, "misc")
            for l in range(LAYERS):
                for k in range(2):
                    mul, add = mod_t[:, l, 2 * k + 1, :], mod_t[:, l, 2 * k, :]
                    step(g.tensor_scalar(mul, mul, 1.0, None, ALU.add))
                    if l == 1:
                        w, b = aff_t[:, 2 * k:2 * k + 1], aff_t[:, 2 * k + 1:2 * k + 2]
                        step(g.tensor_scalar(mod_w[:], mul, b, None, ALU.mult))
                        step(g.tensor_tensor(add, add, mod_w[:], ALU.add))
                        step(g.tensor_scalar(mul, mul, w, None, ALU.mult))
                    if l == 2:
                        step(g.tensor_scalar(mul, mul, aff_t[:, 4 + k:5 + k], None, ALU.mult))

            for k in range(2):
                for h in range(2):
                    step(g.memset(tailp[k][h][:], 0.0))
                    step(g.memset(tailp[k][h][:, Q1, CT:KT], 1.0))
            g.memset(mod_w[:], 0.0).then_inc(mods_ready, 1)

            def tail_parts(kind, v, input_ready, used, done):
                h, l, b = v % 2, v // B, v % B
                y, p = tail[kind][h], tailp[kind][h]
                m = gmod[:, l, b, 2 * C + kind * 2 * CT:2 * C + (kind + 1) * 2 * CT]

                def again(slots):
                    n_ = len(range(SLOTS)[slots])
                    return y[:].rearrange("p (o c) -> p o c", o=1).broadcast_to([T, n_, CT])

                pool.wait_ge(*input_ready)
                if b == 0:
                    loaded(pool, f"gmod{l}")
                if used is not None:
                    pool.wait_ge(*used)
                step(g.tensor_tensor(y[:], ln[kind][h][:, 128:C], m[:, CT:2 * CT], ALU.mult))
                step(g.tensor_tensor(y[:], y[:], m[:, 0:CT], ALU.add))
                step(g.tensor_copy(p[:, Q1, 0:CT], again(Q1)))
                step(g.tensor_tensor(y[:], y[:], p[:, 1, 0:CT], ALU.subtract))
                step(g.tensor_copy(p[:, Q2, 0:CT], again(Q2)))
                g.tensor_tensor(p[:, 4, 0:CT], y[:], p[:, 0, 0:CT], ALU.subtract).then_inc(done, 1)

            for slot in range(-2, VISITS + 3):
                m = mlp_step(slot, 3)
                v, u = slot + 2, slot - 2
                if 0 <= u < VISITS:
                    pool.wait_ge(att_ready, u + 1)
                    g.tensor_tensor(x[:, u % B, :], x[:, u % B, :], attd[u % 2], ALU.add).then_inc(att_added, 1)
                if v < VISITS:
                    pool.wait_ge(var1, v + 1)
                    h = v % 2
                    g.tensor_tensor(rstd[:, 0, h:h + 1], vare[:, 0, h:h + 1], nhalf[:, 0:1], ALU.pow).then_inc(rstd1, 1)
                if m is not None:
                    pool.wait_ge(var2, m + 1)
                    g.tensor_tensor(rstd[:, 1, :], vare[:, 1, :], nhalf[:], ALU.pow).then_inc(rstd2, 1)
                if v < VISITS:
                    tail_parts(0, v, (ln_ready, v + 1), (hT_full, v - 1) if v >= 2 else None, tailp_ready)
                if m is not None:
                    for n_ in (2 * m, 2 * m + 1):
                        tail_parts(1, n_, (ln2_ready, n_ + 1), (h2T_full, m) if m >= 1 else None, tail2p_ready)

        @block.scalar
        def _(act):
            a = nc.scalar

            loaded(act, "cond")
            a.activation(e_t[:], c_t[:], ACT.Exp, scale=-1.0)
            a.activation(e_u[0:CT, :], c_u[0:CT, :], ACT.Exp, scale=-1.0).then_inc(silu_e, 1)

            def flat(tile):
                return tile.rearrange("p b d -> p (b d)")

            def weight_part(k, l):
                if k == 1:
                    act.wait_ge(tail_left, l + 1)
                a.activation(tailw[:, l, :], tails[:, l, :], ACT.Copy).then_inc(act_step, 1)
                act.wait_ge(act_step, LAYERS * k + l + 1)
                a.activation(tprod[:, l, :], tailw[:, l, :], ACT.Copy, scale=tmask[:, k:k + 1]).then_inc(tail_cast, 1)

            loaded(act, "tmask")
            for l in range(LAYERS):
                loaded(act, f"tail{l}")
                weight_part(0, l)

            for k, (name, arg) in enumerate(pre):
                act.wait_ge(pre_full, k + 1)
                src = ps[:, k % 6, :]
                if name == "upper":
                    i = a.activation(upper[:], src[:, 0:D // 2 * B].rearrange("p (j b) -> p b j", b=B), ACT.Copy,
                                     scale=2.0 ** -SQUARINGS)
                elif name == "skew":
                    i = a.activation(flat(bmat[:]), src[0:D, :], ACT.Copy)
                elif name == "n2":
                    i = a.activation(flat(n2), src[0:D, :], ACT.Copy)
                elif name == "n4":
                    i = a.activation(flat(n4), src[0:D, :], ACT.Copy)
                elif name == "poly":
                    i = a.activation(flat(poly[arg[0]][arg[1]]), src[0:D, :], ACT.Copy)
                    if arg == (0, 1):
                        i.then_inc(pre_read, 1)
                        i = a.activation(flat(nodd[:]), src[0:D, :], ACT.Copy, scale=-1.0)
                elif name == "expm":
                    i = a.activation(flat(ef[0][:, arg]), src[0:D, :], ACT.Copy)
                elif name == "square" and arg[0] == SQUARINGS:
                    a.activation(rmi[:, 0, :], src[0:32, :], ACT.Copy)
                    i = a.activation(rmi[:, 1, :], src[32:D, :], ACT.Copy)
                elif name == "square":
                    group = slice(B // 2 * arg[1], B // 2 * (arg[1] + 1))
                    i = a.activation(ef[arg[0] % 2][:, :, group, :],
                                     src[0:D, :].rearrange("p (f b d) -> p f b d", f=2, b=B // 2), ACT.Copy)
                elif name == "xp":
                    i = a.activation(xpT[:, 512 * arg:512 * arg + 512], src[0:D, :], ACT.Copy)
                elif name == "mods":
                    i = a.activation(mod_t[:].rearrange("p l k b -> p (l k b)"), src[:, 0:LAYERS * 4 * B], ACT.Copy)
                else:
                    a.activation(gmod_b[:, arg, 0:2 * C], src[0:B, 0:2 * C], ACT.Tanh if arg == 2 else ACT.Copy)
                    i = a.activation(gmod_b[:, arg, 2 * C:GM], src[0:B, 2 * C:GM], ACT.Copy)
                i.then_inc(pre_read, 1)
                if 6 <= k < 6 + LAYERS:
                    weight_part(1, k - 6)

            for l in range(LAYERS):
                act.wait_ge(tail_left, LAYERS + l + 1)
                a.activation(tailw[:, l, :], tails[:, l, :], ACT.Copy).then_inc(tailw_ready, 1)
            act.wait_ge(gram_read, 2)
            a.activation(sel[:], one_h[:].rearrange("p (h o) -> p h o", o=1).broadcast_to([128, H, 128]),
                         ACT.Copy).then_inc(sel_ready, 1)

            def v_out(v):
                act.wait_ge(qkv_full, v + 1)
                if v >= 3:
                    act.wait_ge(prob_used, 4 * (v - 3) + 4)
                a.activation(v_aug[v % 3][:, :, 0:HD], ps[:, 1, 2 * C:3 * C].rearrange("p (h d) -> p h d", d=HD),
                             ACT.Copy).then_inc(v_ready, 1)

            def squares(v):
                if v % B >= 1:
                    act.wait_ge(qk_normed, 2 * (v - 2 * B))
                a.activation(sq[:], ps[:, 1, 0:2 * C].rearrange("p (k d) -> p k d", d=HD), ACT.Square).then_inc(squared, 1)

            def first(v, k):
                h, l = v % 2, v // B
                if v >= 2:
                    act.wait_ge((qT_full, kT_full)[k], v - 1)
                if l == 2:
                    act.wait_ge(qk_normed, 2 * (v - 2 * B) + k + 1)
                src = qk[h][:, k, :, :] if l == 2 else \
                    ps[:, 1, k * C:(k + 1) * C].rearrange("p (h d) -> p h d", d=HD)
                src = src.rearrange("p h (o d) -> p h o d", o=1).broadcast_to([T, H, 3, HD])
                dst = parts[k][h][:, :, 0:HROWS].rearrange("p h (s d) -> p h s d", d=HD)[:, :, (Q1, K1)[k], :]
                a.activation(dst, src, ACT.Copy).then_inc(first_parts, 1)

            def k_out(v):
                act.wait_ge(kT_full, v + 1)
                if v >= 2:
                    act.wait_ge(sT_full, 4 * (v - 2) + 4)
                for n in (0, 4):
                    a.activation(qkT[1][v % 2][:, n:n + 4, :].rearrange("p k t -> p (k t)"),
                                 ps[:, 7, :].bitcast(BF16)[:, n * T:(n + 4) * T], ACT.Copy).then_inc(kT_ready, 1)

            def exps(v, g):
                act.wait_ge(sT_full, 4 * v + g + 1)
                if v >= 1:
                    act.wait_ge(prob_used, 4 * (v - 1) + g + 1)
                a.activation(prob[g].rearrange("p i t -> p (i t)"), ps[:, 2 + g % 2, :], ACT.Exp,
                             scale=SCALE).then_inc(prob_ready, 1)

            def o_out(v):
                act.wait_ge(prob_used, 4 * v + 4)
                if v >= 2:
                    act.wait_ge(back_full, v - 1)
                a.activation(o_raw[v % 2].rearrange("p g t -> p (g t)"), ps[:, 4, :],
                             ACT.Copy).then_inc(o_raw_ready, 1)

            tables = [0]

            def bring_table(f):
                if tables[0]:
                    act.wait_ge(table_used, tables[0])
                tables[0] += 1
                a.activation(table_out[:], half[:], f).then_inc(table_used, 1)

            def gelu(m, r):
                f = ACT.Gelu if m // (B // 2) == 1 else ACT.Gelu_apprx_tanh
                if m >= 1:
                    act.wait_ge(fc2_full, m)
                act.wait_ge(fc1_full, 3 * m + r + 1)
                rows, n = (128, 2) if r < 2 else (64, 1)
                a.activation(hid[0:rows, 2 * r:2 * r + n, :, :].rearrange("p c h t -> p (c h t)"),
                             ps[0:rows, FC1_BANKS[r], 0:n * 2 * T], f).then_inc(hid_ready, 1)

            def o_T(v):
                h = v % 2
                act.wait_ge(oT_full, v + 1)
                if v >= 2:
                    act.wait_ge(proj_full, v - 1)
                a.activation(oT_t[h][:], ps[:, 4, 0:T], ACT.Copy)
                a.activation(oT_u[h][:], ps[0:KT, 4, T:2 * T], ACT.Copy).then_inc(oT_ready, 1)

            act.wait_ge(late_consts, 1)
            act.wait_ge(slots_zeroed, 1)
            v_out(0)
            first(0, 0)
            first(0, 1)
            for slot in range(VISITS + 4):
                v, w = slot, slot - 1
                new, old = v < VISITS, 0 <= w < VISITS
                m = mlp_step(slot, 4)
                coming, third = v + 1 < VISITS, (v + 1) // B == 2
                if new:
                    k_out(v)
                if 0 <= slot - 2 < VISITS:
                    o_T(slot - 2)
                if coming:
                    v_out(v + 1)
                if coming and third:
                    squares(v + 1)
                if old:
                    exps(w, 0)
                if coming and not third:
                    first(v + 1, 0)
                    first(v + 1, 1)
                if old:
                    exps(w, 1)
                    exps(w, 2)
                if coming and third:
                    first(v + 1, 0)
                    first(v + 1, 1)
                if old:
                    exps(w, 3)
                if m is not None:
                    bring_table(ACT.Gelu if m // (B // 2) == 1 else ACT.Gelu_apprx_tanh)
                if old:
                    o_out(w)
                if m is not None:
                    gelu(m, 0)
                    gelu(m, 1)
                    gelu(m, 2)
                    bring_table(ACT.Exp)

        @block.tensor
        def _(pe):
            def mm(o, lhsT, rhs, start=True, stop=True):
                return pe.matmul(o, lhsT, rhs, start=start, stop=stop, skip_group_check=True)

            loaded(pe, "p")
            for q in range(2):
                o = ps[0:32, 7, q * D:(q + 1) * D]
                mm(o, p_t[:, 32 * q:32 * q + 32], p_t[:], True, False)
                i = mm(o, p_u[:, 32 * q:32 * q + 32], p_u[:], False, True)
            i.then_inc(gram_full, 1)

            def sized(k, n):
                if k >= 6:
                    pe.wait_ge(pre_read, pre_reads[k - 6])
                return ps[0:D, k % 6, :].rearrange("p (b d) -> p b d", b=B) if n is None else ps[0:n, k % 6, :]

            pe.wait_ge(early_consts, 3)
            for k, (name, arg) in enumerate(pre):
                if name == "upper":
                    pe.wait_ge(silu_ready, 1)
                    loaded(pe, "skw")
                    o = sized(k, 128)
                    for j in range(D // 2):
                        mm(o[:, j * B:(j + 1) * B], skw_t[:, 2 * j * D:2 * (j + 1) * D], s_t[:], True, False)
                        i = mm(o[:, j * B:(j + 1) * B], skw_u[:, 2 * j * D:2 * (j + 1) * D], s_u[:], False, True)
                elif name == "skew":
                    pe.wait_ge(pre_read, was_read("upper", 0))
                    o = sized(k, None)
                    for q in range(2):
                        mm(o[:, :, 32 * q:32 * q + 32], ident[:, D * q:D * q + D], upper[:], q == 0, False)
                    for b in range(B):
                        for q in range(2):
                            r = slice(D * q, D * q + D)
                            i = mm(o[32 * q:32 * q + 32, b, :], upper[r, b, :], nident[r, :], False, b == B - 1)
                elif name == "n2":
                    pe.wait_ge(pre_read, was_read("skew", 0))
                    o = sized(k, None)
                    for b in range(B):
                        i = mm(o[:, b, :], bmat[:, b, :], bmat[:, b, :])
                elif name == "n4":
                    pe.wait_ge(pre_read, was_read("n2", 0))
                    o = sized(k, None)
                    for b in range(B):
                        i = mm(o[:, b, :], n2[:, b, :], n2[:, b, :])
                elif name == "poly":
                    d, f = arg
                    c = (COS, SIN)[f]
                    pe.wait_ge(pre_read, was_read("n2", 0) if d == 1 else was_read("poly", (d + 1, f)))
                    o = sized(k, None)
                    mm(o, eyes[:, eye_of(c[2 * d]), :], irep[:], True, False)
                    i = mm(o, eyes[:, eye_of(c[2 * d + 1]), :], n2, False, d == 1)
                    if d == 0:
                        for b in range(B):
                            i = mm(o[:, b, :], n4[:, b, :], poly[d + 1][f][:, b, :], False, b == B - 1)
                elif name == "expm":
                    pe.wait_ge(pre_read, was_read("poly", (0, 1)))
                    o = sized(k, None)
                    mm(o, ident[0:D, 0:D], poly[0][0], True, False)
                    odd = (nodd, poly[0][1])[arg]
                    for b in range(B):
                        i = mm(o[:, b, :], bmat[:, b, :], odd[:, b, :], False, b == B - 1)
                elif name == "square":
                    d, g = arg
                    o = sized(k, None)
                    e = ef[(d - 1) % 2]
                    if d < SQUARINGS:
                        pe.wait_ge(pre_read, was_read("expm", 1) if d == 1 else was_read("square", (d - 1, g)))
                        for f in range(2):
                            for b in range(B // 2):
                                i = mm(o[:, f * (B // 2) + b, :], e[:, 1 - f, g * (B // 2) + b, :], e[:, f, g * (B // 2) + b, :])
                    else:
                        mm(o, eyes[:, eye_of(-1.0), :], irep[:], True, False)
                        for b in range(B):
                            if b % (B // 2) == 0:
                                pe.wait_ge(pre_read, was_read("square", (d - 1, b // (B // 2))))
                            i = mm(o[:, b, :], e[:, 1, b, :], e[:, 0, b, :], False, b == B - 1)
                elif name == "xp":
                    loaded(pe, "x")
                    o = sized(k, D)
                    mm(o, p_t[:], x_t[:, 512 * arg:512 * arg + 512], True, False)
                    i = mm(o, p_u[:], x_u[:, 512 * arg:512 * arg + 512], False, True)
                elif name == "mods":
                    o = sized(k, 128)
                    for l in range(LAYERS):
                        loaded(pe, f"ada{l}")
                        for n in range(4):
                            at = GM + n * 128
                            oo = o[:, (4 * l + n) * B:(4 * l + n + 1) * B]
                            mm(oo, adaw_t[l][:, at:at + 128], s_t[:], True, False)
                            i = mm(oo, adaw_u[l][:, at:at + 128], s_u[:], False, True)
                else:
                    loaded(pe, f"ada{arg}")
                    o = sized(k, B)
                    mm(o[:, 0:GM], s_t[:], adaw_t[arg][:, 0:GM], True, False)
                    i = mm(o[:, 0:GM], s_u[:], adaw_u[arg][:, 0:GM], False, True)
                i.then_inc(pre_full, 1)

            pe.wait_ge(linv_ready, 1)
            for q in range(2):
                i = pe.transpose(ps[0:D, 6, 32 * q:32 * q + 32], linv[:, q, :], ident[0:32, 0:32])
            i.then_inc(rot_full, 1)
            pe.wait_ge(gram_read, 1)
            pe.wait_ge(pre_read, pre_reads[-1])
            for q in range(2):
                i = mm(ps[0:D, 7, :], linv[:, q, :], rmi[:, q, :], q == 0, q == 1)
            i.then_inc(rot_full, 1)
            pe.wait_ge(rot_read, 1)
            mm(ps[0:D, 6, 0:C], linvT[:], pT[:]).then_inc(rot_full, 1)
            for n in range(2):
                pe.wait_ge(rot_read, 2 + n)
                for b in range(4 * n, 4 * n + 4):
                    i = mm(ps[0:D, 7 - n, (b % 4) * T:(b % 4 + 1) * T], lrmi[:, b * D:(b + 1) * D], xpT[:, b * T:(b + 1) * T])
                i.then_inc(rot_full, 1)
            for n in range(4):
                pe.wait_ge(rot_read, 4 + n)
                for b in range(2 * n, 2 * n + 2):
                    i = mm(ps[:, 7 - n % 2, (b % 2) * C:(b % 2 + 1) * C], yT[:, b * T:(b + 1) * T], uT[:])
                i.then_inc(rot_full, 1)

            reader = {bk: (rot_read, 9) for bk in (6, 7)}
            reader.update({bk: (pre_read, pre_reads[-1]) for bk in range(6)})

            def refill(bk, s_, count):
                pe.wait_ge(*reader[bk])
                reader[bk] = (s_, count)
                return ps[:, bk, :]

            def turn(o, src):
                pe.transpose(o[:, 0:T], src[:, 0:128], ident[:])
                return pe.transpose(o[0:KT, T:2 * T], src[:, 128:C + 1], ident[:])

            def turn_parts(o, src):
                return pe.transpose(o, src[:].rearrange("p s c -> p (s c)"), identb[:])

            def h_turn(v):
                o = refill(0, hT_ready, v + 1)
                pe.wait_ge(ln_ready, v + 1)
                pe.transpose(o[:, 0:T], ln[0][v % 2][:, 0:128], ident[:])
                pe.wait_ge(tailp_ready, v + 1)
                turn_parts(o.bitcast(BF16)[0:KS, 2 * T:3 * T], tailp[0][v % 2]).then_inc(hT_full, 1)

            def h2_turn(m):
                o = refill(0, h2T_ready, 2 * m + 2)
                for h in range(2):
                    pe.wait_ge(ln2_ready, 2 * m + h + 1)
                    pe.transpose(o[:, h * T:(h + 1) * T], ln[1][h][:, 0:128], ident[:])
                for h in range(2):
                    pe.wait_ge(tail2p_ready, 2 * m + h + 1)
                    i = turn_parts(o.bitcast(BF16)[0:KS, (4 + h) * T:(5 + h) * T], tailp[1][h])
                i.then_inc(h2T_full, 1)

            def qkv(v):
                h, l = v % 2, v // B
                o = refill(1, qkv_read, v + 1)
                pe.wait_ge(hT_ready, v + 1)
                if v % B < 2:
                    loaded(pe, f"blk{l}")
                    pe.wait_ge(tailw_ready, l + 1)
                mm(o[:, 0:3 * C], hT_t[h][:], qkvw_t[l][:], True, False)
                mm(o[:, 0:3 * C], hT_u[h][:], tailw[:, l, 0:3 * C], False, True).then_inc(qkv_full, 1)

            def fc1(m, r):
                l = m // (B // 2)
                o = refill(FC1_BANKS[r], hid_ready, 3 * m + r + 1)
                if r == 0:
                    pe.wait_ge(h2T_ready, 2 * m + 2)
                for c in range(2 * r, min(2 * r + 2, FFC)):
                    rows = 128 if c < 4 else 64
                    oo = o[0:rows, (c % 2) * 2 * T:(c % 2 + 1) * 2 * T]
                    mm(oo, fc1w_t[l][:, c * 128:c * 128 + rows], mT_t[:].rearrange("p h t -> p (h t)"), True, False)
                    i = mm(oo, tailw[:, l, 3 * C + c * 128:3 * C + c * 128 + rows], mT_u[:].rearrange("p h t -> p (h t)"), False, True)
                i.then_inc(fc1_full, 1)

            def fc2(m, h):
                l = m // (B // 2)
                if h == 0:
                    refill(5, mlp_ready, m + 1)
                    pe.wait_ge(hid_ready, 3 * m + 3)
                for c in range(FFC):
                    rows = 128 if c < 4 else 65
                    i = mm(ps[:, 5, h * C:(h + 1) * C], hid[0:rows, c, h, :], fc2w[l][0:rows, c, :], c == 0, c == FFC - 1)
                if h == 1:
                    i.then_inc(fc2_full, 1)

            def parts_turn(v, k):
                o = refill(6 + k, (qT_ready, kT_ready)[k], 2 * v + 2).bitcast(BF16)
                pe.wait_ge(parts_ready, 2 * v + k + 1)
                for pair in range(H // 2):
                    i = pe.transpose(o[:, pair * T:(pair + 1) * T],
                                     parts[k][v % 2][:, 2 * pair:2 * pair + 2, :].rearrange("p h d -> p (h d)"), identb[:])
                i.then_inc((qT_full, kT_full)[k], 1)

            def operands(v, g, i):
                hd = head_of(g, i)
                r = 64 * (hd % 2)
                return hd, [qkT[k][v % 2][r:r + HROWS, hd // 2, :] for k in (0, 1)]

            def scores(v, g):
                pe.wait_ge(qT_ready, 2 * v + g // 2 + 1)
                pe.wait_ge(kT_ready, 2 * v + g // 2 + 1)
                o = refill(6 + g % 2, max_ready, 4 * v + g + 1)
                for n in range(4):
                    _, (q, k) = operands(v, g, n)
                    i = mm(o[:, n * T:(n + 1) * T], q, k)
                i.then_inc(s_full, 1)

            def max_turn(v):
                o = refill(7, nmT_ready, v + 1).bitcast(BF16)
                pe.wait_ge(nmp_ready, v + 1)
                pe.transpose(o[:, 0:T], nmp[v % 2][:], identb[:]).then_inc(mT_full, 1)

            def scores_T(v, g):
                o = refill(2 + g % 2, prob_ready, 4 * v + g + 1)
                if g == 0:
                    pe.wait_ge(nmT_ready, v + 1)
                for n in range(4):
                    hd, (q, k) = operands(v, g, n)
                    mm(o[:, n * T:(n + 1) * T], k, q, True, False)
                    i = mm(o[:, n * T:(n + 1) * T], sel[:, hd, :], nmT[v % 2][:], False, True)
                i.then_inc(sT_full, 1)

            def pv(v, g):
                if g == 0:
                    refill(4, o_raw_ready, v + 1)
                    pe.wait_ge(v_ready, v + 1)
                pe.wait_ge(prob_ready, 4 * v + g + 1)
                for n in range(4):
                    i = mm(ps[32 * n:32 * n + 32, 4, g * T:(g + 1) * T], v_aug[v % 3][:, head_of(g, n), :], prob[g][:, n, :])
                i.then_inc(prob_used, 1)

            def o_back(v):
                o = refill(4, o_n_ready, v + 1)
                pe.wait_ge(o_raw_ready, v + 1)
                for g in range(4):
                    i = pe.transpose(o[:, g * T:(g + 1) * T], o_raw[v % 2][:, g, :], ident[:])
                i.then_inc(back_full, 1)

            def o_turn(v):
                o = refill(4, oT_ready, v + 1)
                pe.wait_ge(o_n_ready, v + 1)
                turn(o, o_n[v % 2]).then_inc(oT_full, 1)

            def proj(v):
                h, l = v % 2, v // B
                o = refill(4, att_ready, v + 1)
                pe.wait_ge(oT_ready, v + 1)
                mm(o[:, 0:C], oT_t[h][:], projw_t[l][:], True, False)
                mm(o[:, 0:C], oT_u[h][:], projw_u[l][:], False, True).then_inc(proj_full, 1)

            pe.wait_ge(late_consts, 1)
            pe.wait_ge(sel_ready, 1)
            h_turn(0)
            qkv(0)
            h_turn(1)
            for slot in range(VISITS + 4):
                v, w, u = slot, slot - 1, slot - 2
                new, old = v < VISITS, 0 <= w < VISITS
                m_fc1, m_fc2 = mlp_step(slot, 4), mlp_step(slot, 5)
                if new:
                    parts_turn(v, 0)
                    parts_turn(v, 1)
                if 0 <= u < VISITS:
                    o_turn(u)
                if v + 1 < VISITS:
                    qkv(v + 1)
                if m_fc1 is not None:
                    h2_turn(m_fc1)
                if old:
                    scores_T(w, 0)
                    scores_T(w, 1)
                if new:
                    scores(v, 0)
                    scores(v, 1)
                if 0 <= u < VISITS:
                    proj(u)
                if m_fc1 is not None:
                    fc1(m_fc1, 0)
                if m_fc2 is not None:
                    fc2(m_fc2, 0)
                if old:
                    scores_T(w, 2)
                    pv(w, 0)
                    scores_T(w, 3)
                    pv(w, 1)
                if new:
                    scores(v, 2)
                if old:
                    pv(w, 2)
                if new:
                    scores(v, 3)
                if old:
                    pv(w, 3)
                if m_fc1 is not None:
                    fc1(m_fc1, 1)
                if m_fc2 is not None:
                    fc2(m_fc2, 1)
                if old:
                    o_back(w)
                if v + 2 < VISITS:
                    h_turn(v + 2)
                if new:
                    max_turn(v)
                if m_fc1 is not None:
                    fc1(m_fc1, 2)

        @block.vector
        def _(dve):
            d = nc.vector
            n = [0]

            def did(ins):
                n[0] += 1
                ins.then_inc(dve_step, 1)
                return n[0]

            def need(count):
                dve.wait_ge(dve_step, count)

            dve.wait_ge(silu_e, 1)
            dve.wait_ge(early_consts, 1)
            k = did(d.tensor_scalar(e_t[:], e_t[:], 1.0, None, ALU.add))
            k = did(d.tensor_scalar(e_u[0:CT, :], e_u[0:CT, :], 1.0, None, ALU.add))
            need(k)
            k = did(d.reciprocal(e_t[:], e_t[:]))
            k = did(d.reciprocal(e_u[0:CT, :], e_u[0:CT, :]))
            need(k)
            d.tensor_tensor(s_t[:], c_t[:], e_t[:], ALU.mult)
            d.tensor_tensor(s_u[0:CT, :], c_u[0:CT, :], e_u[0:CT, :], ALU.mult).then_inc(silu_ready, 1)
            for h in range(2):
                d.memset(o_n[h][:, C:C + 1], 1.0)
                i = d.memset(nmp[h][:], 0.0)
            i.then_inc(late_consts, 1)

            dve.wait_ge(gram_full, 1)
            dve.wait_ge(early_consts, 2)
            d.tensor_copy(elim[:, :, 0:D], ps[0:32, 7, 0:2 * D].rearrange("p (q d) -> p q d", q=2)).then_inc(gram_read, 1)
            d.tensor_tensor(one_h[:], ident[:, 0:16], ident[:, 16:32], ALU.add).then_inc(gram_read, 1)
            dve.wait_ge(gram_read, 1)
            loaded(dve, "p")

            def spread(rows, out_, j):
                return d.stream_shuffle(out_, rows, [j % 32] * 32)

            upd = {}
            upd["g", 0] = upd["g", 1] = upd["t", 0] = upd["t", 1] = 0

            def gram_pivot(j):
                need(upd["g", j // 32])
                if j >= 4:
                    dve.wait_ge(root_ready, j - 3)
                spread(elim[:, j // 32, j:j + D + 1], grow[:, j % 4, j:j + D + 1], j).then_inc(grow_ready, 1)

            def top_pivot(j):
                need(upd["t", j // 32])
                return did(spread(top[:, j // 32, j:D], trow[:, j % 2, j:D], j))

            def gram_reciprocal(j):
                dve.wait_ge(grow_ready, j + 1)
                return did(d.reciprocal(grec[:, j:j + 1], grow[:, j % 4, j:j + 1]))

            def gram_factor(j, k_rec):
                need(k_rec)
                return did(d.scalar_tensor_tensor(
                    out=gfac[:, j % 2, :].rearrange("p (q o) -> p q o", o=1), in0=elim[:, :, j:j + 1],
                    scalar=grec[:, j:j + 1], in1=below[:, :, j:j + 1], op0=ALU.mult, op1=ALU.mult))

            def gram_update(j, q, k_fac):
                need(k_fac)
                w = slice(j + 1, j + D + 1)
                upd["g", q] = did(d.scalar_tensor_tensor(
                    out=elim[:, q, w], in0=grow[:, j % 4, w], scalar=gfac[:, j % 2, q:q + 1], in1=elim[:, q, w],
                    op0=ALU.mult, op1=ALU.add))

            EARLY = 32
            gram_pivot(0)
            for j in range(D + 1):
                gq = [q for q in range(2) if j < 32 * q + 31] if j < D else []
                tj = j - 1
                tq = [q for q in range(2) if tj < 32 * q + 31] if tj >= 0 else []
                if tj >= 0:
                    k_row = top_pivot(tj)
                if j < EARLY:
                    k_rec = gram_reciprocal(j)
                if tj >= 0:
                    need(k_row)
                    dve.wait_ge(root_ready, tj + 1)
                    k_beta = did(d.scalar_tensor_tensor(
                        out=beta[:, tj:tj + 1].bitcast(U32), in0=trow[:, tj % 2, tj:tj + 1].bitcast(U32), scalar=0x80000000,
                        in1=root[:, tj:tj + 1].bitcast(U32), op0=ALU.bitwise_and, op1=ALU.bitwise_or))
                if gq and j < EARLY:
                    k_fac = gram_factor(j, k_rec)
                elif gq:
                    gram_update(j, 1, k_fac)
                if tq:
                    need(k_beta)
                    k_den = did(d.scalar_tensor_tensor(
                        out=den[:, tj:tj + 1], in0=trow[:, tj % 2, tj:tj + 1], scalar=beta[:, tj:tj + 1],
                        in1=beta[:, tj:tj + 1], op0=ALU.add, op1=ALU.mult))
                    k_num = did(d.scalar_tensor_tensor(
                        out=tnum[:, tj % 2, :].rearrange("p (q o) -> p q o", o=1), in0=top[:, :, tj:tj + 1],
                        scalar=beta[:, tj:tj + 1], in1=elim[:, :, tj:tj + 1], op0=ALU.mult, op1=ALU.add))
                    need(k_den)
                    k_drec = did(d.reciprocal(drec[:, tj:tj + 1], den[:, tj:tj + 1]))
                if j < EARLY:
                    for q in gq:
                        gram_update(j, q, k_fac)
                elif j + 1 < D:
                    gram_pivot(j + 1)
                if tq:
                    need(k_drec)
                    need(k_num)
                    k_fac2 = did(d.scalar_tensor_tensor(
                        out=tfac[:, tj % 2, :].rearrange("p (q o) -> p q o", o=1),
                        in0=tnum[:, tj % 2, :].rearrange("p (q o) -> p q o", o=1), scalar=drec[:, tj:tj + 1],
                        in1=below[:, :, tj:tj + 1], op0=ALU.mult, op1=ALU.mult))
                if j < EARLY:
                    gram_pivot(j + 1)
                if EARLY <= j + 1 < D:
                    k_rec = gram_reciprocal(j + 1)
                if tq:
                    need(k_fac2)
                    for q in tq:
                        w = slice(tj + 1, D)
                        upd["t", q] = did(d.scalar_tensor_tensor(
                            out=top[:, q, w], in0=trow[:, tj % 2, w], scalar=tfac[:, tj % 2, q:q + 1], in1=top[:, q, w],
                            op0=ALU.mult, op1=ALU.add))
                if EARLY <= j + 1 < D - 1:
                    k_fac = gram_factor(j + 1, k_rec)

            need(n[0])
            k = did(d.tensor_tensor(sgn[:], beta[:], grec[:], ALU.mult))
            need(k)
            for q in range(2):
                k = did(d.tensor_tensor(sgnd[:, q, :], sgn[:], diag[:, q, :], ALU.mult))
            need(k)
            k = did(d.tensor_reduce(rscale[:], sgnd[:], AX_X, ALU.add))
            need(k)
            for q in range(2):
                i = d.tensor_scalar(linv[:, q, :], elim[:, q, D:2 * D], rscale[:, q:q + 1], None, ALU.mult)
            i.then_inc(linv_ready, 1)
            dve.wait_ge(pre_full, 1)
            d.memset(hid[64:96, FFC - 1, :, :], 1.0)

            dve.wait_ge(rot_full, 1)
            d.tensor_copy(linvT[:], ps[0:D, 6, 0:D]).then_inc(rot_read, 1)
            dve.wait_ge(rot_full, 2)
            d.tensor_copy(lrmi, ps[0:D, 7, :]).then_inc(rot_read, 1)
            dve.wait_ge(rot_full, 3)
            d.tensor_copy(uT[:], ps[0:D, 6, 0:C]).then_inc(rot_read, 1)
            for n_ in range(2):
                dve.wait_ge(rot_full, 4 + n_)
                d.tensor_copy(yT[:, 512 * n_:512 * n_ + 512], ps[0:D, 7 - n_, :]).then_inc(rot_read, 1)

            def rotated(n_):
                dve.wait_ge(rot_full, 6 + n_)
                xs = x[:, 2 * n_:2 * n_ + 2, :].rearrange("p b c -> p (b c)")
                d.tensor_tensor(xs, xs, ps[:, 7 - n_ % 2, 0:2 * C], ALU.add).then_inc(rot_read, 1)

            def variances(kind, visits, done):
                l = visits[0] // B
                hs = slice(visits[0] % 2, visits[-1] % 2 + 1)
                for v in visits:
                    k = did(d.bn_stats(st6[:, kind, v % 2, :], x[:, v % B, :]))
                need(k)
                for v in visits:
                    k = did(d.bn_aggr(st2[:, kind, v % 2, :], st6[:, kind, v % 2, :]))
                need(k)
                if l < 2:
                    d.tensor_scalar(vare[:, kind, hs], st2[:, kind, hs, 1], LN_EPS[l], None, ALU.add).then_inc(done, 1)
                    return
                for v in visits:
                    h = slice(v % 2, v % 2 + 1)
                    k = did(d.scalar_tensor_tensor(out=msq[:, kind, h], in0=st2[:, kind, h, 0], scalar=st2[:, kind, h, 0],
                                                   in1=st2[:, kind, h, 1], op0=ALU.mult, op1=ALU.add))
                need(k)
                d.tensor_scalar(vare[:, kind, hs], msq[:, kind, hs], 1e-24 / C, None, ALU.max).then_inc(done, 1)

            def normalise(kind, v, done):
                h = v % 2
                if v // B < 2:
                    i = d.tensor_scalar(ln[kind][h][:, 0:C], x[:, v % B, :], st2[:, kind, h, 0:1], rstd[:, kind, h:h + 1],
                                        ALU.subtract, ALU.mult)
                else:
                    i = d.tensor_scalar(ln[kind][h][:, 0:C], x[:, v % B, :], rstd[:, kind, h:h + 1], None, ALU.mult)
                i.then_inc(done, 1)

            def modulated(v, kind):
                h, l, b = v % 2, v // B, v % B
                out_, at = (hT_t[h][:], 0) if kind == 0 else (mT_t[:, h, :], h * T)
                return d.tensor_scalar(out_, ps[:, 0, at:at + T], mod_t[:, l, 2 * kind + 1, b:b + 1],
                                       mod_t[:, l, 2 * kind, b:b + 1], ALU.mult, ALU.add)

            def h_out(v):
                dve.wait_ge(hT_full, v + 1)
                if v >= 2:
                    dve.wait_ge(qkv_full, v - 1)
                modulated(v, 0)
                d.tensor_copy(hT_u[v % 2][:], ps[:, 0, :].bitcast(BF16)[0:KS, 2 * T:3 * T]).then_inc(hT_ready, 1)

            def h2_out(m):
                dve.wait_ge(h2T_full, m + 1)
                if m >= 1:
                    dve.wait_ge(fc1_full, 3 * m)
                d.tensor_copy(mT_u[:].rearrange("p h t -> p (h t)"),
                              ps[:, 0, :].bitcast(BF16)[0:KS, 4 * T:6 * T]).then_inc(h2T_ready, 1)
                modulated(2 * m, 1)
                modulated(2 * m + 1, 1).then_inc(h2T_ready, 1)

            def of_slots(k, h, slots):
                return parts[k][h][:, :, 0:HROWS].rearrange("p h (s d) -> p h s d", d=HD)[:, :, slots, :]

            def norms(v):
                more = v + 1 < VISITS
                h = slice((v + 1) % 2, (v + 1) % 2 + 1)
                dve.wait_ge(squared, v - 2 * B + 1)
                k = did(d.tensor_reduce(ssq[:].rearrange("p k h -> p (k h)"), sq[:], AX_X, ALU.add))
                if more:
                    dve.wait_ge(mlp_added, 2 * ((v + 1 - B) // 2) + 2)
                    k_stats = did(d.bn_stats(st6[:, 0, (v + 1) % 2, :], x[:, (v + 1) % B, :]))
                need(k)
                k = did(d.tensor_scalar(ssq[:], ssq[:], 1e-24, None, ALU.max))
                if more:
                    need(k_stats)
                    k_aggr = did(d.bn_aggr(st2[:, 0, (v + 1) % 2, :], st6[:, 0, (v + 1) % 2, :]))
                need(k)
                k = did(d.tensor_scalar(ny[:].bitcast(I32), ssq[:].bitcast(I32), -0.5, RSQRT_SEED, ALU.mult, ALU.add))
                if more:
                    need(k_aggr)
                    k_msq = did(d.scalar_tensor_tensor(out=msq[:, 0, h], in0=st2[:, 0, h, 0], scalar=st2[:, 0, h, 0],
                                                       in1=st2[:, 0, h, 1], op0=ALU.mult, op1=ALU.add))
                need(k)
                k = did(d.tensor_tensor(my[:], ny[:], ny[:], ALU.mult))
                if more:
                    need(k_msq)
                    d.tensor_scalar(vare[:, 0, h], msq[:, 0, h], 1e-24 / C, None, ALU.max).then_inc(var1, 1)
                need(k)
                need(did(d.tensor_tensor(my[:], my[:], ssq[:], ALU.mult)))
                need(did(d.scalar_tensor_tensor(out=my[:], in0=my[:], scalar=-10.0 / 3.0, in1=my[:], op0=ALU.add, op1=ALU.mult)))
                need(did(d.scalar_tensor_tensor(out=ny[:], in0=my[:], scalar=5.0, in1=ny[:], op0=ALU.add, op1=ALU.mult)))

            def unit_parts(v):
                h = v % 2
                k = did(d.scalar_tensor_tensor(out=my[:], in0=ny[:], scalar=-0.5 * (3.0 / 8.0) ** 2, in1=ny[:],
                                               op0=ALU.mult, op1=ALU.mult))
                for kk in range(2):
                    k2 = did(d.tensor_scalar(hy[:, kk, :], ny[:, kk, :], 3.0 / 8.0 * float(HD) ** 0.5, qkg[:, kk:kk + 1],
                                             ALU.mult, ALU.mult))
                need(k)
                need(did(d.tensor_tensor(my[:], my[:], ssq[:], ALU.mult)))
                need(k2)
                need(did(d.scalar_tensor_tensor(out=ny[:], in0=my[:], scalar=1.5, in1=hy[:], op0=ALU.add, op1=ALU.mult)))
                if v - 2 * B >= 2:
                    dve.wait_ge(first_parts, 2 * (v - 2) + 2)
                for kk in range(2):
                    fac = ny[:, kk, :].rearrange("p (h o) -> p h o", o=1).broadcast_to([T, H, HD])
                    src = ps[:, 1, kk * C:(kk + 1) * C].rearrange("p (h d) -> p h d", d=HD)
                    d.tensor_tensor(qk[h][:, kk, :, :], src, fac, ALU.mult).then_inc(qk_normed, 1)

            def split(v):
                h, l = v % 2, v // B
                firsts, seconds = (slice(1, 2), slice(2, 3)), (slice(0, 1), slice(0, 1))
                for k in range(2):
                    dve.wait_ge(first_parts, 2 * v + (k + 1 if l == 2 else 2))
                    if l == 2:
                        dve.wait_ge(qk_normed, 2 * (v - 2 * B) + k + 1)
                    src = qk[h][:, k, :, :] if l == 2 else \
                        ps[:, 1, k * C:(k + 1) * C].rearrange("p (h d) -> p h d", d=HD)
                    i = d.tensor_tensor(res[h][:, k, :, :], src, of_slots(k, h, firsts[k])[:, :, 0, :], ALU.subtract)
                    if k == 0:
                        did(i)
                    else:
                        i.then_inc(qkv_read, 1)
                dve.wait_ge(qkv_read, v + 1)
                for k, slots in ((0, Q2), (1, K2)):
                    src = res[h][:, k, :, :].rearrange("p h (o d) -> p h o d", o=1).broadcast_to([T, H, 2, HD])
                    c = did(d.tensor_copy(of_slots(k, h, slots), src))
                need(c)
                for k, slots in ((0, Q3), (1, K3)):
                    d.tensor_tensor(of_slots(k, h, slots)[:, :, 0, :], res[h][:, k, :, :], of_slots(k, h, seconds[k])[:, :, 0, :],
                                    ALU.subtract).then_inc(parts_ready, 1)

            def q_out(v):
                dve.wait_ge(qT_full, v + 1)
                if v >= 2:
                    dve.wait_ge(sT_full, 4 * (v - 2) + 4)
                for n in (0, 4):
                    d.tensor_copy(qkT[0][v % 2][:, n:n + 4, :].rearrange("p k t -> p (k t)"),
                                  ps[:, 6, :].bitcast(BF16)[:, n * T:(n + 4) * T]).then_inc(qT_ready, 1)

            def maxima(v, g):
                dve.wait_ge(s_full, 4 * v + g + 1)
                first = head_of(g, 0)
                d.tensor_reduce(nmax[:, v % 2, first:first + 7:2], ps[:, 6 + g % 2, :].rearrange("p (i t) -> p i t", i=4),
                                AX_X, ALU.max, negate=True).then_inc(max_ready, 1)

            def max_parts(v):
                h = v % 2
                dve.wait_ge(max_ready, 4 * v + 4)
                if v >= 2:
                    dve.wait_ge(mT_full, v - 1)
                need(did(d.tensor_copy(nmp[h][:, 0:16], nmax[:, h, :])))
                d.tensor_tensor(nmp[h][:, 16:32], nmax[:, h, :], nmp[h][:, 0:16], ALU.subtract).then_inc(nmp_ready, 1)

            def max_out(v):
                dve.wait_ge(mT_full, v + 1)
                if v >= 2:
                    dve.wait_ge(sT_full, 4 * (v - 2) + 4)
                d.tensor_copy(nmT[v % 2][:], ps[:, 7, :].bitcast(BF16)[:, 0:T]).then_inc(nmT_ready, 1)

            def attended(v):
                h = v % 2
                dve.wait_ge(back_full, v + 1)
                src = ps[:, 4, :].rearrange("p (h r) -> p h r", r=32)
                k = did(d.reciprocal(orec[h][:].rearrange("p (h o) -> p h o", o=1), src[:, :, HD:HD + 1]))
                need(k)
                if v >= 2:
                    dve.wait_ge(oT_full, v - 1)
                d.tensor_tensor(o_n[h][:, 0:C].rearrange("p (h d) -> p h d", d=HD), src[:, :, 0:HD],
                                orec[h][:].rearrange("p (h o) -> p h o", o=1).broadcast_to([T, H, HD]),
                                ALU.mult).then_inc(o_n_ready, 1)

            def gated(v):
                h, l, b = v % 2, v // B, v % B
                dve.wait_ge(proj_full, v + 1)
                if b == 0:
                    loaded(dve, f"gmod{l}")
                if v >= 2:
                    dve.wait_ge(att_added, v - 1)
                d.tensor_tensor(attd[h], ps[:, 4, 0:C], gmod[:, l, b, 0:C], ALU.mult).then_inc(att_ready, 1)

            def mlp_out(m):
                l, b = m // (B // 2), 2 * m % B
                dve.wait_ge(fc2_full, m + 1)
                if m >= 1:
                    dve.wait_ge(mlp_added, 2 * m)
                d.tensor_tensor(mlpd, ps[:, 5, 0:2 * C].rearrange("p (h c) -> p h c", h=2), gmod[:, l, b:b + 2, C:2 * C],
                                ALU.mult).then_inc(mlp_ready, 1)
                dve.wait_ge(mlp_ready, m + 1)
                for h in range(2):
                    d.tensor_tensor(x[:, b + h, :], x[:, b + h, :], mlpd[:, h, :], ALU.add).then_inc(mlp_added, 1)

            def next_input(v):
                if v >= B:
                    dve.wait_ge(mlp_added, 2 * ((v - B) // 2) + 2)
                variances(0, [v], var1)

            def next_normal(v):
                dve.wait_ge(rstd1, v + 1)
                if v >= 2:
                    dve.wait_ge(hT_full, v - 1)
                normalise(0, v, ln_ready)

            dve.wait_ge(slots_zeroed, 1)
            rotated(0)
            dve.wait_ge(rot_read, 6)
            next_input(0)
            rotated(1)
            next_normal(0)
            rotated(2)
            next_input(1)
            rotated(3)
            next_normal(1)
            dve.wait_ge(rot_read, 9)
            dve.wait_ge(mods_ready, 1)
            dve.wait_ge(pre_read, pre_reads[-1])
            h_out(0)
            h_out(1)
            split(0)
            for slot in range(VISITS + 4):
                v, w = slot, slot - 1
                new, old = v < VISITS, 0 <= w < VISITS
                m_norm, m_fc1, m_out = mlp_step(slot, 3), mlp_step(slot, 4), mlp_step(slot, 5)
                if new:
                    q_out(v)
                if m_fc1 is not None:
                    h2_out(m_fc1)
                third = v + 1 < VISITS and (v + 1) // B == 2
                if third:
                    maxima(v, 0)
                    norms(v + 1)
                elif v + 2 < VISITS:
                    next_input(v + 2)
                if 0 <= slot - 2 < VISITS:
                    gated(slot - 2)
                if third:
                    maxima(v, 1)
                    unit_parts(v + 1)
                elif new:
                    maxima(v, 0)
                if m_norm is not None:
                    dve.wait_ge(att_added, 2 * m_norm + 2)
                    variances(1, [2 * m_norm, 2 * m_norm + 1], var2)
                if new and not third:
                    maxima(v, 1)
                if v + 2 < VISITS:
                    next_normal(v + 2)
                if v + 1 < VISITS:
                    split(v + 1)
                if m_norm is not None:
                    dve.wait_ge(rstd2, m_norm + 1)
                    if m_norm >= 1:
                        dve.wait_ge(h2T_full, m_norm)
                    for u in (2 * m_norm, 2 * m_norm + 1):
                        normalise(1, u, ln2_ready)
                if new:
                    maxima(v, 2)
                    maxima(v, 3)
                    max_parts(v)
                if v + 2 < VISITS:
                    h_out(v + 2)
                if new:
                    max_out(v)
                if old:
                    attended(w)
                if m_out is not None:
                    mlp_out(m_out)


def kernel(**inputs):
    import concourse.bacc as bacc
    from concourse.bass_utils import run_bass_kernel_spmd

    f = {k: np.asarray(v) for k, v in inputs.items()}

    def rows(w, b=None):
        return np.concatenate([w, np.zeros((1, w.shape[1]), np.float32) if b is None else b[None, :]], axis=0)

    iu, ju = np.triu_indices(D, k=1)
    skw = np.zeros((C + 1, D, D), np.float32)
    skw[0:C, ju, iu] = f["L0_cond_W"].T
    skw[C, ju, iu] = f["L0_cond_b"]
    skw = skw.reshape(C + 1, 2, D // 2, D).transpose(0, 2, 1, 3)
    order = np.concatenate([np.arange(HD) + HD * head_of(g, i) for g in range(4) for i in range(4)])
    p = f["L0_cond_P"]
    vec = lambda v: np.broadcast_to(v, (C,))
    aff = np.stack([f["L2_cond_ln1_w"], f["L2_cond_ln1_b"], f["L2_cond_ln2_w"], f["L2_cond_ln2_b"],
                    vec(f["L3_cond_g1"]), vec(f["L3_cond_g2"])], axis=1)

    def modulation(w, b):
        w = rows(w, b).reshape(C + 1, 6, C)
        parts = [w[:, [2, 5], :], w[:, [0, 1, 3, 4], 128:C], w[:, [0, 1, 3, 4], 0:128]]
        return np.concatenate([p_.reshape(C + 1, -1) for p_ in parts], axis=1)

    qkv = [rows(f["L1_cond_W_qkv"], f["L1_cond_b_qkv"]),
           rows(np.concatenate([f["L2_cond_wq"], f["L2_cond_wk"], f["L2_cond_wv"]], axis=1)),
           rows(f["L3_cond_qkv_w"].T, f["L3_cond_qkv_b"])]
    fc1 = [rows(f["L1_cond_W_fc1"], f["L1_cond_b_fc1"]), rows(f["L2_cond_fc1_w"], f["L2_cond_fc1_b"]),
           rows(f["L3_cond_fc1_w"].T, f["L3_cond_fc1_b"])]
    a = {
        "x": f["x"].transpose(1, 0, 2),
        "xT": f["x"].transpose(2, 0, 1).reshape(C, B * T),
        "cond": f["cond_1152"].T,
        "p": p, "pT": p.T,
        "ptop": p.T[:, 0:D].reshape(2, 32, D).transpose(1, 0, 2),
        "skw": skw.reshape(C + 1, D * D),
        "aff": aff[0:128, :],
        "aff_u": np.broadcast_to(aff[128:C, [0, 1, 4, 2, 3, 5]].T.reshape(1, 2, 3, CT), (B, 2, 3, CT)),
        "tmask": np.repeat(np.array([[-1, 0], [-1, 0], [0, 0], [0, 0], [0, 0], [-1, -1]], np.float32), KT, axis=0),
        "qkg": np.stack([np.broadcast_to(f["L3_cond_qg"], (T,)), np.broadcast_to(f["L3_cond_kg"], (T,))], axis=1),
        "ada0": modulation(f["L1_cond_W_ada"], f["L1_cond_b_ada"]),
        "ada1": modulation(f["L2_cond_ada_w"], f["L2_cond_ada_b"]),
        "ada2": modulation(f["L3_cond_ada_w"].T, f["L3_cond_ada_b"]),
        "proj0": rows(f["L1_cond_W_proj"][order], f["L1_cond_b_proj"]),
        "proj1": rows(f["L2_cond_wo"][order], f["L2_cond_wo_b"]),
        "proj2": rows(f["L3_cond_proj_w"].T[order], f["L3_cond_proj_b"]),
        "fc20": rows(f["L1_cond_W_fc2"], f["L1_cond_b_fc2"]),
        "fc21": rows(f["L2_cond_fc2_w"], f["L2_cond_fc2_b"]),
        "fc22": rows(f["L3_cond_fc2_w"].T, f["L3_cond_fc2_b"]),
    }
    for l in range(LAYERS):
        a[f"qkv{l}"], a[f"fc1{l}"] = qkv[l][0:128], fc1[l][0:128]
        a[f"tail{l}"] = np.tile(np.concatenate([qkv[l][128:], fc1[l][128:]], axis=1), (SLOTS, 1))
    nc = bacc.Bacc("TRN2", target_bir_lowering=False, num_devices=1)
    arrays, t = {}, {}
    for name, v in a.items():
        v = np.ascontiguousarray(v)
        arrays["in_" + name] = v
        t[name] = nc.dram_tensor("in_" + name, v.shape, F32, kind="ExternalInput").ap()
    out = nc.dram_tensor("out_x", (T, B, C), F32, kind="ExternalOutput").ap()
    spread_mods = nc.dram_tensor("spread_mods", (B, LAYERS, GM), F32, kind="Internal").ap()
    program(nc, t, out, spread_mods)
    r = run_bass_kernel_spmd(nc, [arrays], core_ids=[0])
    return r.results[0]["out_x"].transpose(1, 0, 2)
```
